# Optimizing a Trainium2 kernel written in Bass

```python
import numpy as np
import jax
import jax.numpy as jnp

def _softmax(x, axis=-1):
    return jax.nn.softmax(x, axis=axis)

def _gelu(x):
    return jax.nn.gelu(x, approximate=True)

def _silu(x):
    return jax.nn.silu(x)

def _sigmoid(x):
    return jax.nn.sigmoid(x)

def _layernorm(x, axis=-1, eps=1e-05):
    m = jnp.mean(x, axis=axis, keepdims=True)
    v = jnp.var(x, axis=axis, keepdims=True)
    return (x - m) / jnp.sqrt(v + eps)

def _scatter_add(tgt, idx, src, axis=0):
    return tgt.at[idx].add(src)

def _segment_sum(src, seg, n):
    return jax.ops.segment_sum(src, seg, n)
kernel_name = 'mk_gnn_preln_d4_gnn_r16_6effca'

def setup_inputs(seed: int=0):
    np.random.seed(seed)
    _w = jnp.asarray

    def _rec_inputs():
        import jax
        import jax.numpy as jnp
        _gk = jax.random.key(seed)
        x = -0.000202 + 1 * jax.random.normal(jax.random.fold_in(_gk, 1), (3125, 128), jnp.float32)
        src = jax.random.randint(jax.random.fold_in(_gk, 2), (100000,), 0, 3125, jnp.int32)
        dst = jax.random.randint(jax.random.fold_in(_gk, 3), (100000,), 0, 3125, jnp.int32)
        _o = jnp.argsort(dst, stable=True)
        src = src[_o]
        dst = dst[_o]
        edge_type_8 = jax.random.randint(jax.random.fold_in(_gk, 12), (100000,), 0, 8, jnp.int32)
        return (x, src, dst, edge_type_8)
    x, src, dst, edge_type_8 = _rec_inputs()

    def _L0_gnn_setup():
        import jax, jax.numpy as jnp
        import numpy as np
        NUM_LAYERS = 4
        HIDDEN = 128
        N_NODES = 3125
        N_EDGES = 50000

        def _gru_cell(inp, h, w_ih, w_hh, b_ih, b_hh):
            gi = inp @ w_ih.T + b_ih
            gh = h @ w_hh.T + b_hh
            i_r, i_z, i_n = jnp.split(gi, 3, axis=-1)
            h_r, h_z, h_n = jnp.split(gh, 3, axis=-1)
            r = jax.nn.sigmoid(i_r + h_r)
            z = jax.nn.sigmoid(i_z + h_z)
            n = jnp.tanh(i_n + r * h_n)
            return (1.0 - z) * n + z * h
        key = jax.random.key(seed)
        ks = jax.random.split(key, 8)
        s = 1.0 / np.sqrt(HIDDEN)
        node_embed = jax.random.normal(ks[0], (N_NODES, HIDDEN), dtype=jnp.float32)
        edge_index = jax.random.randint(ks[1], (2, N_EDGES), 0, N_NODES, dtype=jnp.int64)
        weight = jax.random.normal(ks[2], (NUM_LAYERS, HIDDEN, HIDDEN), dtype=jnp.float32) * s
        w_ih = jax.random.normal(ks[3], (3 * HIDDEN, HIDDEN), dtype=jnp.float32) * s
        w_hh = jax.random.normal(ks[4], (3 * HIDDEN, HIDDEN), dtype=jnp.float32) * s
        b_ih = jax.random.normal(ks[5], (3 * HIDDEN,), dtype=jnp.float32) * s
        b_hh = jax.random.normal(ks[6], (3 * HIDDEN,), dtype=jnp.float32) * s
        return {'node_embed': node_embed, 'edge_index': edge_index, 'weight': weight, 'w_ih': w_ih, 'w_hh': w_hh, 'b_ih': b_ih, 'b_hh': b_hh}
    _L0_gnn_all = _L0_gnn_setup()
    _L0_gnn_in = {k: v for k, v in _L0_gnn_all.items() if k in ('weight', 'w_ih', 'w_hh', 'b_ih', 'b_hh')}
    del _L0_gnn_all

    def _L1_gnn_setup():
        import jax, jax.numpy as jnp
        import numpy as np
        N_NODES = 2500
        N_EDGES = 40000
        D = 128
        key = jax.random.key(seed)
        k1, k2, k3, k4 = jax.random.split(key, 4)
        scale = 1.0 / np.sqrt(D)
        return {'edge_index': jax.random.randint(k1, (2, N_EDGES), 0, N_NODES, dtype=jnp.int64), 'x_init': jax.random.normal(k2, (N_NODES, D), dtype=jnp.float32), 'W0': jax.random.normal(k3, (D, D), dtype=jnp.float32) * scale, 'b0': jnp.zeros((D,), dtype=jnp.float32), 'W1': jax.random.normal(k4, (D, D), dtype=jnp.float32) * scale, 'b1': jnp.zeros((D,), dtype=jnp.float32)}
    _L1_gnn_all = _L1_gnn_setup()
    _L1_gnn_in = {k: v for k, v in _L1_gnn_all.items() if k in ('W0', 'b0', 'W1', 'b1')}
    del _L1_gnn_all

    def _L2_gnn_setup():
        import jax, jax.numpy as jnp
        import numpy as np
        N, E, IN_DIM, OUT_DIM, R = (3125, 50000, 128, 128, 8)
        key = jax.random.key(seed)
        k1, k2, k3, k4, k5 = jax.random.split(key, 5)
        x = jax.random.normal(k1, (N, IN_DIM), dtype=jnp.float32)
        edge_index = jax.random.randint(k2, (2, E), 0, N, dtype=jnp.int32)
        edge_type = jax.random.randint(k3, (E,), 0, R, dtype=jnp.int32)
        lim_w = float(np.sqrt(6.0 / (IN_DIM + OUT_DIM)))
        weight = jax.random.uniform(k4, (R, IN_DIM, OUT_DIM), dtype=jnp.float32, minval=-lim_w, maxval=lim_w)
        self_weight = jax.random.uniform(k5, (IN_DIM, OUT_DIM), dtype=jnp.float32, minval=-lim_w, maxval=lim_w)
        return {'x': x, 'weight': weight, 'self_weight': self_weight, 'edge_index': edge_index, 'edge_type': edge_type}
    _L2_gnn_all = _L2_gnn_setup()
    _L2_gnn_in = {k: v for k, v in _L2_gnn_all.items() if k in ('weight', 'self_weight')}
    del _L2_gnn_all

    def _L3_gnn_setup():
        import jax, jax.numpy as jnp
        import numpy as np
        TOPK = 2
        key = jax.random.key(seed)
        ks = jax.random.split(key, 18)
        N, E = (1250, 20000)
        IN, H, OUT, L = (128, 256, 128, 3)
        NW, NS = (4, 4)
        NE = NW + NS

        def w(k, shape, fan):
            return jax.random.normal(k, shape, dtype=jnp.float32) / np.float32(np.sqrt(fan))
        inp = {'x': jax.random.normal(ks[0], (N, IN), dtype=jnp.float32), 'edge_index': jax.random.randint(ks[1], (2, E), 0, N, dtype=jnp.int64), 'W_in': w(ks[2], (IN, H), IN), 'b_in': jnp.zeros((H,), jnp.float32), 'router_W': w(ks[3], (L, 2 * H, NE), 2 * H), 'router_b': jnp.zeros((L, NE), jnp.float32), 'weak_W': w(ks[4], (L, NW, H, H), H), 'weak_b': jnp.zeros((L, NW, H), jnp.float32), 'strong_W1': w(ks[5], (L, NS, H, 2 * H), H), 'strong_b1': jnp.zeros((L, NS, 2 * H), jnp.float32), 'strong_W2': w(ks[6], (L, NS, 2 * H, H), 2 * H), 'strong_b2': jnp.zeros((L, NS, H), jnp.float32), 'conf_W': w(ks[7], (L, H, 1), H), 'conf_b': jnp.zeros((L, 1), jnp.float32), 'W_out': w(ks[8], (H, OUT), H), 'b_out': jnp.zeros((OUT,), jnp.float32)}
        return inp
    _L3_gnn_all = _L3_gnn_setup()
    _L3_gnn_in = {k: v for k, v in _L3_gnn_all.items() if k in ('W_in', 'b_in', 'router_W', 'router_b', 'weak_W', 'weak_b', 'strong_W1', 'strong_b1', 'strong_W2', 'strong_b2', 'conf_W', 'conf_b', 'W_out', 'b_out')}
    del _L3_gnn_all
    return {'x': x, 'src': src, 'dst': dst, 'edge_type_8': edge_type_8, 'L0_gnn_weight': _L0_gnn_in['weight'], 'L0_gnn_w_ih': _L0_gnn_in['w_ih'], 'L0_gnn_w_hh': _L0_gnn_in['w_hh'], 'L0_gnn_b_ih': _L0_gnn_in['b_ih'], 'L0_gnn_b_hh': _L0_gnn_in['b_hh'], 'L1_gnn_W0': _L1_gnn_in['W0'], 'L1_gnn_b0': _L1_gnn_in['b0'], 'L1_gnn_W1': _L1_gnn_in['W1'], 'L1_gnn_b1': _L1_gnn_in['b1'], 'L2_gnn_weight': _L2_gnn_in['weight'], 'L2_gnn_self_weight': _L2_gnn_in['self_weight'], 'L3_gnn_W_in': _L3_gnn_in['W_in'], 'L3_gnn_b_in': _L3_gnn_in['b_in'], 'L3_gnn_router_W': _L3_gnn_in['router_W'], 'L3_gnn_router_b': _L3_gnn_in['router_b'], 'L3_gnn_weak_W': _L3_gnn_in['weak_W'], 'L3_gnn_weak_b': _L3_gnn_in['weak_b'], 'L3_gnn_strong_W1': _L3_gnn_in['strong_W1'], 'L3_gnn_strong_b1': _L3_gnn_in['strong_b1'], 'L3_gnn_strong_W2': _L3_gnn_in['strong_W2'], 'L3_gnn_strong_b2': _L3_gnn_in['strong_b2'], 'L3_gnn_conf_W': _L3_gnn_in['conf_W'], 'L3_gnn_conf_b': _L3_gnn_in['conf_b'], 'L3_gnn_W_out': _L3_gnn_in['W_out'], 'L3_gnn_b_out': _L3_gnn_in['b_out']}

def reference(x, src, dst, edge_type_8, L0_gnn_weight, L0_gnn_w_ih, L0_gnn_w_hh, L0_gnn_b_ih, L0_gnn_b_hh, L1_gnn_W0, L1_gnn_b0, L1_gnn_W1, L1_gnn_b1, L2_gnn_weight, L2_gnn_self_weight, L3_gnn_W_in, L3_gnn_b_in, L3_gnn_router_W, L3_gnn_router_b, L3_gnn_weak_W, L3_gnn_weak_b, L3_gnn_strong_W1, L3_gnn_strong_b1, L3_gnn_strong_W2, L3_gnn_strong_b2, L3_gnn_conf_W, L3_gnn_conf_b, L3_gnn_W_out, L3_gnn_b_out):
    import jax
    import jax.numpy as jnp

    def _L0_gnn_ref(node_embed, edge_index, weight, w_ih, w_hh, b_ih, b_hh):
        import jax, jax.numpy as jnp
        import numpy as np
        NUM_LAYERS = 4
        HIDDEN = 128
        N_NODES = 3125
        N_EDGES = 50000

        def _gru_cell(inp, h, w_ih, w_hh, b_ih, b_hh):
            gi = inp @ w_ih.T + b_ih
            gh = h @ w_hh.T + b_hh
            i_r, i_z, i_n = jnp.split(gi, 3, axis=-1)
            h_r, h_z, h_n = jnp.split(gh, 3, axis=-1)
            r = jax.nn.sigmoid(i_r + h_r)
            z = jax.nn.sigmoid(i_z + h_z)
            n = jnp.tanh(i_n + r * h_n)
            return (1.0 - z) * n + z * h
        src = edge_index[0]
        dst = edge_index[1]
        n_nodes = node_embed.shape[0]
        x = node_embed
        for l in range(NUM_LAYERS):
            m = x @ weight[l]
            agg = jax.ops.segment_sum(m[src], dst, num_segments=n_nodes)
            x = _gru_cell(agg, x, w_ih, w_hh, b_ih, b_hh)
        return x + node_embed

    def _L1_gnn_ref(edge_index, x_init, W0, b0, W1, b1):
        import jax, jax.numpy as jnp
        import numpy as np
        N_NODES = 2500
        N_EDGES = 40000
        D = 128
        N = x_init.shape[0]
        src, dst = (edge_index[0], edge_index[1])
        h = x_init @ W0
        x = jax.ops.segment_sum(h[src], dst, num_segments=N) + b0
        h = x @ W1
        loops = jnp.arange(N, dtype=src.dtype)
        src2 = jnp.concatenate([src, loops])
        dst2 = jnp.concatenate([dst, loops])
        deg = jax.ops.segment_sum(jnp.ones(src2.shape, h.dtype), dst2, num_segments=N)
        dinv = jnp.where(deg > 0, jax.lax.rsqrt(deg), 0.0)
        w = dinv[src2] * dinv[dst2]
        x = jax.ops.segment_sum(w[:, None] * h[src2], dst2, num_segments=N) + b1
        return x

    def _L2_gnn_ref(x, weight, self_weight, edge_index, edge_type):
        import jax, jax.numpy as jnp
        import numpy as np
        N, E, IN_DIM, OUT_DIM, R = (3125, 50000, 128, 128, 8)
        n = x.shape[0]
        r = weight.shape[0]
        d_out = weight.shape[2]
        src, dst = (edge_index[0], edge_index[1])
        src_all = jnp.concatenate([src, dst])
        dst_all = jnp.concatenate([dst, src])
        et_all = jnp.concatenate([edge_type, edge_type])
        xw = jnp.einsum('ni,rio->rno', x, weight)
        msg = xw[et_all, src_all]
        seg = et_all.astype(jnp.int32) * n + dst_all
        agg = jax.ops.segment_sum(msg, seg, num_segments=r * n).reshape(r, n, d_out)
        deg = jax.ops.segment_sum(jnp.ones_like(seg, dtype=x.dtype), seg, num_segments=r * n).reshape(r, n)
        deg_inv = jnp.where(deg > 0, 1.0 / jnp.maximum(deg, 1.0), jnp.zeros_like(deg))
        out = jnp.sum(agg * deg_inv[..., None], axis=0)
        out = out + x @ self_weight
        return out

    def _L3_gnn_ref(x, edge_index, W_in, b_in, router_W, router_b, weak_W, weak_b, strong_W1, strong_b1, strong_W2, strong_b2, conf_W, conf_b, W_out, b_out):
        import jax, jax.numpy as jnp
        import numpy as np
        TOPK = 2
        N = x.shape[0]
        L = router_W.shape[0]
        src = edge_index[0]
        dst = edge_index[1]
        deg = jax.ops.segment_sum(jnp.ones(src.shape, x.dtype), dst, num_segments=N)
        deg = jnp.clip(deg, 1.0)[:, None]
        h = x @ W_in + b_in
        rows = jnp.arange(N)[:, None]
        for l in range(L):
            agg = jax.ops.segment_sum(h[src], dst, num_segments=N) / deg
            logits = jnp.concatenate([h, agg], axis=-1) @ router_W[l] + router_b[l]
            vals, idx = jax.lax.top_k(logits, TOPK)
            gates = jax.nn.softmax(vals, axis=-1)
            gate_dense = jnp.zeros_like(logits).at[rows, idx].set(gates)
            weak = jax.nn.relu(jnp.einsum('nh,ehf->nef', agg, weak_W[l]) + weak_b[l])
            sh = jax.nn.relu(jnp.einsum('nh,ehf->nef', agg, strong_W1[l]) + strong_b1[l])
            strong = jnp.einsum('nef,efh->neh', sh, strong_W2[l]) + strong_b2[l]
            experts = jnp.concatenate([weak, strong], axis=1)
            moe = jnp.einsum('ne,neh->nh', gate_dense, experts)
            conf = jax.nn.sigmoid(h @ conf_W[l] + conf_b[l])
            h = h + conf * moe
        return h @ W_out + b_out
    edge_index = jnp.stack([src, dst])
    h = jnp.maximum(_layernorm(x, axis=-1), 0.0)
    x = x + _L0_gnn_ref(h, edge_index, L0_gnn_weight, L0_gnn_w_ih, L0_gnn_w_hh, L0_gnn_b_ih, L0_gnn_b_hh)
    h = jnp.maximum(_layernorm(x, axis=-1), 0.0)
    x = x + _L1_gnn_ref(edge_index, h, L1_gnn_W0, L1_gnn_b0, L1_gnn_W1, L1_gnn_b1)
    h = jnp.maximum(_layernorm(x, axis=-1), 0.0)
    x = x + _L2_gnn_ref(h, L2_gnn_weight, L2_gnn_self_weight, edge_index, edge_type_8)
    h = jnp.maximum(_layernorm(x, axis=-1), 0.0)
    x = x + _L3_gnn_ref(h, edge_index, L3_gnn_W_in, L3_gnn_b_in, L3_gnn_router_W, L3_gnn_router_b, L3_gnn_weak_W, L3_gnn_weak_b, L3_gnn_strong_W1, L3_gnn_strong_b1, L3_gnn_strong_W2, L3_gnn_strong_b2, L3_gnn_conf_W, L3_gnn_conf_b, L3_gnn_W_out, L3_gnn_b_out)
    return x

_drawn_inputs = setup_inputs


def setup_inputs(seed=0):
    import zlib

    import numpy as np

    out = dict(_drawn_inputs(seed))
    spreads = {'L1_gnn_b0': (0.0, 0.8),
     'L1_gnn_b1': (0.0, 0.8),
     'L3_gnn_b_in': (0.0, 0.8),
     'L3_gnn_router_b': (0.0, 0.8),
     'L3_gnn_weak_b': (0.0, 0.8),
     'L3_gnn_strong_b1': (0.0, 0.8),
     'L3_gnn_strong_b2': (0.0, 0.8),
     'L3_gnn_conf_b': (0.0, 0.8),
     'L3_gnn_b_out': (0.0, 0.8)}
    factors = {'L3_gnn_strong_W1': 5.07, 'L3_gnn_strong_W2': 3.928, 'L3_gnn_conf_W': 5.239}
    for name, (base, spread) in spreads.items():
        noise = np.random.default_rng([zlib.crc32(name.encode()), seed]).standard_normal(out[name].shape)
        drawn = base * np.exp(spread * noise) if base else spread * noise
        out[name] = jnp.asarray(drawn.astype(out[name].dtype))
    for name, factor in factors.items():
        out[name] = (out[name] * factor).astype(out[name].dtype)
    return out
```

```python
from contextlib import ExitStack

import numpy as np
import concourse.bass as bass
from concourse import mybir

dt = mybir.dt
F32, F16, BF16, F8 = dt.float32, dt.float16, dt.bfloat16, dt.float8e4
I32, U16, U8 = dt.int32, dt.uint16, dt.uint8
ALU = mybir.AluOpType
ACT = mybir.ActivationFunctionType
AX = mybir.AxisListType

P = 128
BANK = 512
WN = 4
SLOTS = 2
ALIGN = 32
GW = 8
COUNT_MAX = 7
EPS = 1e-5
FIXED = 4096.0


def build_program(nc, x, src, dst, et, g_w, g_ih, g_hh, g_bih, g_bhh, c_w0, c_b0, c_w1, c_b1,
                  r_w, r_self, m_win, m_bin, m_rw, m_rb, m_ww, m_wb, m_w1, m_b1, m_w2, m_b2,
                  m_cw, m_cb, m_wout, m_bout, out):
    N, D = x.shape
    E = src.shape[0]
    NT = -(-N // P)
    NP = NT * P
    TAIL = N - (NT - 1) * P
    NW = -(-N // WN)
    NG = -(-NW // GW)
    NWP = NG * GW
    NC = NWP * WN
    U = SLOTS * GW
    WB = -(-NWP // P)
    WCOL = WN * NT
    SLOTN = SLOTS * P
    STRIP = P // WN // GW
    NREL = r_w.shape[0]
    CH = [(c, min(BANK, N - c)) for c in range(0, N, BANK)]
    EP = 125
    EC = E // EP
    LG = EC // ALIGN
    assert EC % ALIGN == 0 and D == P and NREL == 8
    NLG = E // ALIGN
    TROWS = -(-(NLG + 1) // 64) * 64
    EPAD = TROWS * ALIGN + SLOTN - E

    engines = {"pe": nc.tensor, "dve": nc.vector, "act": nc.scalar, "pool": nc.gpsimd, "sp": nc.sync}
    top = ExitStack()
    done = {k: top.enter_context(nc.semaphore(f"done_{k}")) for k in ("pe", "dve", "act", "pool")}
    count = {k: 0 for k in done}

    def tick(k, inst):
        count[k] += 1
        inst.then_inc(done[k], 1)
        return done[k], count[k]

    seen = {k: {} for k in engines}

    def need(k, *tokens):
        for t in tokens:
            if t is None:
                continue
            if isinstance(t, list):
                need(k, *t)
                continue
            sem, value = t
            if seen[k].get(sem.name, 0) < value:
                engines[k].wait_ge(sem, value)
                seen[k][sem.name] = value

    slots = {}

    def dma(k, name, out_, in_, **kw):
        if name not in slots:
            slots[name] = [top.enter_context(nc.semaphore(f"dma_{name}")), 0]
        s = slots[name]
        engines[k].dma_start(out_, in_, **kw).then_inc(s[0], 16)
        s[1] += 16
        return s[0], s[1]

    def gather(name, out_, table, idx):
        if name not in slots:
            slots[name] = [top.enter_context(nc.semaphore(f"dma_{name}")), 0]
        s = slots[name]
        nc.gpsimd.indirect_dma_start(out=out_, out_offset=None, in_=table,
                                     in_offset=bass.IndirectOffsetOnAxis(ap=idx, axis=0)).then_inc(s[0], 16)
        s[1] += 16
        return s[0], s[1]

    def V(inst):
        return tick("dve", inst)

    def S(inst):
        return tick("act", inst)

    def G(inst):
        return tick("pool", inst)

    def T(inst):
        return tick("pe", inst)

    def scope():
        return ExitStack()

    made = []

    def sbuf(ctx, name, shape, dtype):
        made.append(name)
        return ctx.enter_context(nc.sbuf_tensor(f"{name}_{len(made)}", shape, dtype))

    def barrier():
        nc.all_engine_barrier()

    vec, act, pool, pe, sp = nc.vector, nc.scalar, nc.gpsimd, nc.tensor, nc.sync

    epk = nc.dram_tensor("edge_words", (E + EPAD,), I32).ap()
    last_dram = nc.dram_tensor("last_dst", (NLG,), I32).ap()
    tbl = nc.dram_tensor("slot_table", (TROWS, SLOTN), I32).ap()
    pd = nc.dram_tensor("packed_counts", (NP, NP), I32).ap()
    sd = nc.dram_tensor("packed_sym", (NP, NP), I32).ap()
    deg_row = nc.dram_tensor("deg_row", (N,), F32).ap()
    dinv_row = nc.dram_tensor("dinv_row", (N,), F32).ap()
    invd_row = nc.dram_tensor("invd_row", (N,), F32).ap()
    SUMS = NREL * NP + P
    feat = nc.dram_tensor("features", (NP, D), F32).ap()
    sums = nc.dram_tensor("edge_sums", (SUMS, D), F32).ap()
    degs8 = nc.dram_tensor("type_degrees", (SUMS, D), F32).ap()
    ET = -(-E // P)
    lists = {n: nc.dram_tensor("list_" + n, (ET * P,), I32).ap() for n in ("src", "dst", "to_dst", "to_type_dst", "to_type_src")}
    xpark = nc.dram_tensor("x_parked", (P, NT * D), F32).ap()

    bank = [top.enter_context(nc.psum_tensor(f"bank{i}", [P, BANK], F32)) for i in range(8)]

    A = sbuf(top, "counts", [P, NT, NC], F8)
    ident = sbuf(top, "ident", [P, P], F32)
    ones_bf = sbuf(top, "ones_bf", [P, 1], BF16)
    ones_f = sbuf(top, "ones_f", [P, P], F32)
    zeros_i = sbuf(top, "zeros_i", [1, 4], F32)
    flag = sbuf(top, "flag", [1, 1], I32)
    xn = sbuf(top, "x_nodes", [P, NT, D], F32)

    t_ones = V(vec.memset(ones_f[:], 1.0))
    t_onesb = V(vec.memset(ones_bf[:], 1.0))
    need("pool", t_ones)
    t_ident = G(pool.affine_select(out=ident[:], in_=ones_f[:], compare_op=ALU.is_equal, fill=0.0, base=0,
                                   pattern=[[-1, P]], channel_multiplier=1))

    full = (NT - 1) * P
    t_xz = V(vec.memset(xn[:, NT - 1, :], 0.0))
    need("sp", t_xz)
    t_x = [dma("sp", "x_tail", xn[0:TAIL, NT - 1, :], x[full:N, :])]
    for i0 in range(0, NT - 1, 4):
        t_x.append(dma("sp", f"x_{i0}", xn[:, i0:i0 + 4, :],
                       x[i0 * P:(i0 + 4) * P, :].rearrange("(i p) f -> p i f", p=P)))

    with scope() as c1:
        thr = sbuf(c1, "thr", [P, WB], F32)
        row = sbuf(c1, "row", [P, WB], I32)
        with scope() as c0:
            ew = {n: sbuf(c0, f"e_{n}", [EP, EC], I32) for n in ("src", "dst", "et", "word")}
            pad = sbuf(c0, "pad", [1, EPAD], I32)
            last = sbuf(c0, "last", [EP, LG], I32)
            ld = [dma("sp", "l" + n, ew[n][:], a.rearrange("(p c) -> p c", p=EP))
                  for n, a in (("dst", dst), ("src", src), ("et", et))]
            t_pad = V(vec.memset(pad[:], 2130706432))
            need("dve", ld[0])
            t_last = V(vec.tensor_copy(last[:], ew["dst"][:, ALIGN - 1::ALIGN]))
            need("sp", t_last)
            t_ldr = dma("sp", "last_out", last_dram.rearrange("(p c) -> p c", p=EP), last[:])
            need("dve", t_last, *ld)
            t1 = V(vec.tensor_scalar(ew["dst"][:], ew["dst"][:], 15, None, ALU.logical_shift_left))
            t2 = V(vec.tensor_scalar(ew["et"][:], ew["et"][:], 12, None, ALU.logical_shift_left))
            need("dve", t1, t2)
            t3 = V(vec.tensor_tensor(ew["word"][:], ew["dst"][:], ew["et"][:], ALU.bitwise_or))
            need("dve", t3)
            t4 = V(vec.tensor_tensor(ew["word"][:], ew["word"][:], ew["src"][:], ALU.bitwise_or))
            need("act", t4, t_pad)
            t5 = [dma("act", "word_out", epk[0:E].rearrange("(p c) -> p c", p=EP), ew["word"][:]),
                  dma("act", "pad_out", epk[E:E + EPAD].rearrange("(a n) -> a n", a=1), pad[:])]
            need("act", t5)
            t_tbl = dma("act", "table", tbl, bass.AP(epk.tensor, 0, [[ALIGN, TROWS], [1, SLOTN]]))

            lastb = sbuf(c0, "lastb", [P, NLG], I32)
            lastf = sbuf(c0, "lastf", [P, NLG], F32)
            below = sbuf(c0, "below", [P, NLG], BF16)
            cnt = sbuf(c0, "cnt", [P, WB], F32)
            need("sp", t_ldr)
            t_lb = dma("sp", "last_in", lastb[:], bass.AP(last_dram.tensor, 0, [[0, P], [1, NLG]]))
            t_thr = G(pool.iota(thr[:], pattern=[[WN * P, WB]], base=0, channel_multiplier=WN,
                                allow_small_or_imprecise_dtypes=True))
            need("dve", t_lb, t_thr)
            t = V(vec.tensor_copy(lastf[:], lastb[:]))
            need("dve", t)
            for b in range(WB):
                t = V(vec.tensor_scalar(below[:], lastf[:], thr[:, b:b + 1], None, ALU.is_lt, ALU.add,
                                        accum_out=cnt[:, b:b + 1]))
                need("dve", t)
            t_row = V(vec.tensor_copy(row[:], cnt[:]))
            barrier()

        words = sbuf(c1, "words", [P, WB, SLOTN], I32)
        scal = sbuf(c1, "scal", [P, 3, NG + P // GW, SLOTS, GW], BF16)
        hits = sbuf(c1, "hits", [P, 1], F32)
        with scope() as c0:
            need("pool", t_row, t_tbl)
            t_g = [gather(f"win{b}", words[:, b, :], tbl, row[:, b:b + 1]) for b in range(WB)]
            fld = [sbuf(c0, f"fld{i}", [P, WB, SLOTN], F32) for i in range(3)]
            ti = [sbuf(c0, f"ti{i}", [P, WB, SLOTN], I32) for i in range(2)]
            tf = [sbuf(c0, f"tf{i}", [P, WB, SLOTN], F32) for i in range(3)]
            need("dve", *t_g)

            def v(inst):
                need("dve", V(inst))

            def shift_and(o, i, sh, mask, left=False):
                v(vec.tensor_scalar(o, i, sh, mask, ALU.logical_shift_right, ALU.bitwise_and))

            w_ = words[:]
            shift_and(ti[0][:], w_, 0, P - 1)
            v(vec.tensor_copy(fld[0][:], ti[0][:]))
            v(vec.tensor_scalar(ti[0][:], w_, 15, None, ALU.logical_shift_right))
            v(vec.tensor_copy(tf[0][:], ti[0][:]))
            v(vec.tensor_tensor(tf[0][:], tf[0][:], thr[:, :, None].to_broadcast([P, WB, SLOTN]), ALU.subtract))
            v(vec.tensor_scalar(tf[1][:], tf[0][:], 0.0, float(WN - 1), ALU.max, ALU.min))
            v(vec.tensor_tensor(tf[2][:], tf[0][:], tf[1][:], ALU.is_equal))
            v(vec.tensor_reduce(hits[:], tf[2][:], axis=AX.XY, op=ALU.add))
            v(vec.tensor_scalar(tf[2][:], tf[2][:], -1000.0, 1000.0, ALU.mult, ALU.add))
            shift_and(ti[0][:], w_, 7, 31)
            v(vec.tensor_copy(fld[1][:], ti[0][:]))
            v(vec.scalar_tensor_tensor(fld[1][:], tf[1][:], float(2 * NT), fld[1][:], ALU.mult, ALU.add))
            shift_and(ti[0][:], w_, 14, 1)
            v(vec.tensor_copy(tf[1][:], ti[0][:]))
            v(vec.scalar_tensor_tensor(fld[1][:], tf[1][:], float(NT), fld[1][:], ALU.mult, ALU.add))
            v(vec.tensor_tensor(fld[1][:], fld[1][:], tf[2][:], ALU.add))
            v(vec.tensor_scalar(fld[1][:], fld[1][:], 255.0, None, ALU.min))
            shift_and(ti[0][:], w_, 12, 3)
            v(vec.tensor_scalar(ti[1][:], ti[0][:], float(1 << 25), float(127 << 23), ALU.mult, ALU.add))
            v(vec.tensor_copy(fld[2][:], ti[1][:].bitcast(F32)))
            t_fld = (done["dve"], count["dve"])
            need("pe", t_fld, t_ident)
            free = [None] * 8
            n = 0
            t_sc = None
            for i in range(3):
                for b in range(WB):
                    for j in range(SLOTS):
                        k = n % 8
                        n += 1
                        need("pe", free[k])
                        tt = T(pe.transpose(bank[k][:, 0:P], fld[i][:, b, j * P:(j + 1) * P], ident[:]))
                        g0 = b * (P // GW)
                        o = scal[:, i, g0:g0 + P // GW, j, :]
                        src_ = bank[k][:, 0:P].rearrange("p (g w) -> p g w", w=GW)
                        if n % 2:
                            need("dve", tt)
                            free[k] = V(vec.tensor_copy(o, src_))
                        else:
                            need("act", tt)
                            free[k] = S(act.activation(o, src_, ACT.Copy))
            barrier()

        HC = 2 * WCOL
        cols = sbuf(c1, "cols", [P, HC, U], BF16)
        oh_s = [sbuf(c1, f"oh_s{i}", [P, P, U], BF16) for i in range(2)]
        oh_w = [sbuf(c1, f"oh_w{i}", [P, P, U], BF16) for i in range(2)]
        oh_c = [sbuf(c1, f"oh_c{i}", [P, HC, U], BF16) for i in range(2)]
        strip = [sbuf(c1, f"strip{i}", [P, NT, P], I32) for i in range(2)]
        sqsum = sbuf(c1, "sqsum", [P, NT, GW * WN], F32)
        sq = sbuf(c1, "sq", [P, NT, GW * WN], F32)
        t_am = G(pool.memset(sqsum[:], 0.0))
        t_cols = G(pool.iota(cols[:], pattern=[[1, HC], [0, U]], base=0, channel_multiplier=0,
                             allow_small_or_imprecise_dtypes=True))
        need("dve", t_cols)
        need("pool", t_am)
        AB, HB = (0, 1), (2, 3, 4, 5, 6, 7)
        free = [None] * 8
        hb = 0
        used = [None, None]
        strip_free = [None, None]
        strip_tok = []
        packed_out = []
        for g in range(NG):
            q = g % 2
            sc = [scal[:, i, g].rearrange("p j w -> p (j w)")[:, None, :] for i in range(3)]
            need("dve", used[q])
            V(vec.tensor_tensor(oh_c[q][:], cols[:], sc[1].to_broadcast([P, HC, U]), ALU.is_equal))
            t = V(vec.tensor_tensor(oh_s[q][:], cols[:, 0:P, :], sc[0].to_broadcast([P, P, U]), ALU.is_equal))
            need("dve", t)
            t_oh = V(vec.tensor_tensor(oh_w[q][:], oh_s[q][:], sc[2].to_broadcast([P, P, U]), ALU.mult))
            need("pe", t_oh)
            st = (g // STRIP) % 2
            if g % STRIP == 0:
                need("act", strip_free[st])
                if (g // STRIP) == NT - 1:
                    need("dve", strip_free[st])
                    need("act", V(vec.memset(strip[st][:], 0)))
            a_toks = []
            for w in range(GW):
                ab = AB[w // 4]
                if w % 4 == 0:
                    need("pe", free[ab])
                if w % 2 == 0:
                    hk = HB[hb % 6]
                    hb += 1
                    need("pe", free[hk])
                ao = bank[ab][:, (w % 4) * WCOL:(w % 4 + 1) * WCOL]
                ho = bank[hk][:, (w % 2) * HC:(w % 2 + 1) * HC]
                for j in range(SLOTS):
                    u = j * GW + w
                    for half in range(2):
                        rhs = oh_c[q][:, :, u].rearrange("p (d h s) -> p d h s", h=2, s=NT)[:, :, half, :]
                        t_a = pe.matmul(ao, oh_s[q][:, :, u], rhs, start=(j == 0 and half == 0),
                                        stop=(j == SLOTS - 1 and half == 1))
                    t_h = pe.matmul(ho, oh_w[q][:, :, u], oh_c[q][:, :, u], start=(j == 0), stop=(j == SLOTS - 1))
                if w % 4 == 3:
                    t_pa = T(t_a)
                if w % 2 == 1:
                    t_ph = T(t_h)
                    need("act", t_ph)
                    d0 = (g % STRIP) * GW * WN + (w - 1) * WN
                    o = strip[st][:, :, d0:d0 + 2 * WN].bitcast(U16).rearrange("p s (x h) -> p x h s", h=2)
                    free[hk] = S(act.activation(o, bank[hk][:, 0:2 * HC].rearrange(
                        "p (x h s) -> p x h s", h=2, s=NT), ACT.Copy))
                if w % 4 == 3:
                    need("act", t_pa)
                    d0 = g * GW * WN + (w - 3) * WN
                    free[ab] = S(act.activation(
                        A[:, :, d0:d0 + 4 * WN].rearrange("p s x -> p x s"),
                        bank[ab][:, 0:4 * WCOL].rearrange("p (x s) -> p x s", s=NT), ACT.Copy, saturate=False))
            used[q] = (done["pe"], count["pe"])
            t_a_evac = (done["act"], count["act"])
            need("pool", t_a_evac)
            ag = A[:, :, g * GW * WN:(g + 1) * GW * WN]
            need("pool", G(pool.tensor_tensor(sq[:], ag, ag, ALU.mult)))
            t_am = G(pool.tensor_tensor(sqsum[:], sqsum[:], sq[:], ALU.add))
            need("pool", t_am)
            if g % STRIP == STRIP - 1 or g == NG - 1:
                j = g // STRIP
                need("sp", t_a_evac)
                strip_free[st] = dma("sp", f"strip{st}", pd.rearrange("(i p) n -> p i n", p=P)[:, :, j * P:(j + 1) * P],
                                     strip[st][:])
                packed_out = [strip_free[0], strip_free[1]]

        chk = sbuf(c1, "chk", [P, 2], F32)
        chr_ = sbuf(c1, "chr", [1, 4], F32)
        need("dve", t_am)
        v(vec.tensor_reduce(chk[:, 0:1], sqsum[:], axis=AX.XY, op=ALU.max))
        need("pe", (done["dve"], count["dve"]))
        pe.matmul(bank[7][0:1, 0:1], hits[:], ones_f[:, 0:1], start=True, stop=True)
        t = T(pe.transpose(bank[6][0:1, 0:P], chk[:, 0:1], ident[:]))
        need("dve", t)
        v(vec.tensor_reduce(chr_[:, 0:1], bank[6][0:1, 0:P], axis=AX.X, op=ALU.max))
        v(vec.tensor_scalar(chr_[:, 1:2], chr_[:, 0:1], float((COUNT_MAX + 1) ** 2), None, ALU.is_lt))
        v(vec.tensor_scalar(chr_[:, 2:3], bank[7][0:1, 0:1], float(E), None, ALU.is_equal))
        v(vec.tensor_tensor(flag[:], chr_[:, 1:2], chr_[:, 2:3], ALU.mult))
        need("sp", *packed_out)
        barrier()

    def node_rows(ap):
        full = (NT - 1) * P
        return ap[0:full, :].rearrange("(i p) f -> p i f", p=P), ap[full:N, :]

    bank_free = [None] * 8
    scale_tmp = {}
    fast = True

    def feature_pair(ctx, name, width=D):
        if fast:
            return sbuf(ctx, name, [P, 2, NT, width], F16)
        return sbuf(ctx, name, [P, NT, width], F32)[:]

    def sum_all(nm):
        if not fast:
            scatter_sum(nm, sums, [("src", "to_dst")], NP)

    def now(k):
        return done[k], count[k]

    def v(inst):
        t_ = V(inst)
        need("dve", t_)
        return t_

    def s_(inst):
        t_ = S(inst)
        need("act", t_)
        return t_

    def rows_of(i):
        return P if i < NT - 1 else TAIL

    def tiles_of(ci):
        c, cw = CH[ci]
        return [(c // P + k, k) for k in range(-(-cw // P))]

    def layer_norm(hn):
        with scope() as c:
            sq_ = sbuf(c, "ln_sq", [P, NT, D], F32)
            st_ = sbuf(c, "ln_st", [P, 3, NT], F32)
            need("dve", *t_x)
            v(vec.tensor_reduce(st_[:, 0, :], xn[:], axis=AX.X, op=ALU.add))
            v(vec.tensor_scalar(st_[:, 0, :], st_[:, 0, :], 1.0 / D, None, ALU.mult))
            v(vec.tensor_tensor(hn[:], xn[:], st_[:, 0, :, None].to_broadcast([P, NT, D]), ALU.subtract))
            need("act", now("dve"))
            need("dve", S(act.activation(sq_[:], hn[:], ACT.Square)))
            v(vec.tensor_reduce(st_[:, 1, :], sq_[:], axis=AX.X, op=ALU.add))
            v(vec.tensor_scalar(st_[:, 1, :], st_[:, 1, :], 1.0 / D, EPS, ALU.mult, ALU.add))
            need("act", now("dve"))
            need("dve", S(act.activation(st_[:, 2, :], st_[:, 1, :], ACT.Sqrt)))
            v(vec.reciprocal(st_[:, 2, :], st_[:, 2, :]))
            v(vec.tensor_tensor(hn[:], hn[:], st_[:, 2, :, None].to_broadcast([P, NT, D]), ALU.mult))
            v(vec.tensor_scalar(hn[:], hn[:], 0.0, None, ALU.max))
            barrier()

    def split_fixed(h16, hn):
        if not fast:
            return [v(vec.tensor_scalar(h16, hn[:], FIXED, None, ALU.mult))]
        need("act", now("dve"))
        need("dve", S(act.activation(h16[:, 0], hn[:], ACT.Copy, scale=FIXED)))
        return [v(vec.scalar_tensor_tensor(h16[:, 1], hn[:], FIXED, h16[:, 0], ALU.mult, ALU.subtract))]

    def to_feature_rows(ht, hn, width=N):
        toks = []
        for i0 in range(0, NT, 4):
            k = 6 + (i0 // 4) % 2
            need("pe", bank_free[k], now("dve"))
            w_ = 0
            for i in range(i0, min(i0 + 4, NT)):
                r_ = rows_of(i)
                tt = pe.transpose(bank[k][:, w_:w_ + r_], hn[0:r_, i, :], ident[0:r_, 0:r_])
                w_ += r_
            need("act", T(tt))
            bank_free[k] = S(act.activation(ht[:, i0 * P:i0 * P + w_], bank[k][:, 0:w_], ACT.Copy))
            toks.append(bank_free[k])
        return toks[-1]

    def sum_edges(bk, h16, ci, tok):
        if not fast:
            return load_sums(bk, sums, 0, ci)
        c, cw = CH[ci]
        need("pe", bank_free[bk], tok)
        for i in range(NT):
            for part in range(2):
                m = pe.matmul(bank[bk][:, 0:cw], h16[:, part, i, :], A[:, i, c:c + cw],
                              start=(i == 0 and part == 0), stop=(i == NT - 1 and part == 1))
        return T(m)

    def node_tiles_to_bank(bk, src_, ci):
        c, cw = CH[ci]
        need("pe", bank_free[bk])
        for i, k in tiles_of(ci):
            r_ = rows_of(i)
            m = pe.transpose(bank[bk][0:r_, k * P:k * P + P], src_[:, k * P:k * P + r_], ident[:])
        return T(m)

    def chunk_rows(ci):
        ts = tiles_of(ci)
        return rows_of(ts[-1][0]) if len(ts) == 1 else P, ts[0][0], len(ts)

    def add_to_x(bk, ci, tok):
        r_, i0, n_ = chunk_rows(ci)
        need("dve", tok)
        o = xn[0:r_, i0:i0 + n_, :]
        bank_free[bk] = V(vec.tensor_tensor(o, o, bank[bk][0:r_, 0:n_ * P].rearrange("p (i f) -> p i f", f=D), ALU.add))
        return bank_free[bk]

    def split_from_bank(bk, h16, ci, tok, scale):
        r_, i0, n_ = chunk_rows(ci)
        s3 = bank[bk][0:r_, 0:n_ * P].rearrange("p (i f) -> p i f", f=D)
        if not fast:
            need("dve", tok)
            bank_free[bk] = v(vec.tensor_scalar(h16[0:r_, i0:i0 + n_, :], s3, scale, None, ALU.mult))
            return [bank_free[bk]]
        hi, lo = (h16[0:r_, part, i0:i0 + n_, :] for part in range(2))
        need("act", tok)
        t1_ = S(act.activation(hi, s3, ACT.Copy, scale=scale))
        need("dve", tok, t1_)
        bank_free[bk] = V(vec.scalar_tensor_tensor(lo, s3, scale, hi, ALU.mult, ALU.subtract))
        return [t1_, bank_free[bk]]

    def power_scale(m, sc_, inv_, work):
        v(vec.tensor_scalar(work, m, 1e-15, None, ALU.max))
        v(vec.tensor_scalar(work.bitcast(I32), work.bitcast(I32), 0x7F800000, None, ALU.bitwise_and))
        v(vec.tensor_scalar(sc_.bitcast(I32), work.bitcast(I32), -1.0, float((127 + 14 + 127) << 23), ALU.mult, ALU.add))
        v(vec.tensor_scalar(inv_.bitcast(I32), work.bitcast(I32), float(14 << 23), None, ALU.subtract))

    def make_lists(ctx):
        e_ = {k: sbuf(ctx, "l_" + k, [EP, EC], I32) for k in ("src", "dst", "et", "rd", "rs")}
        padc = sbuf(ctx, "l_pad", [1, 2, ET * P - E], I32)
        v(vec.memset(padc[:, 0, :], 0))
        v(vec.memset(padc[:, 1, :], NREL * NP))
        need("dve", *[dma("sp", "l_in_" + k, e_[k][:], a.rearrange("(p c) -> p c", p=EP))
                      for k, a in (("src", src), ("dst", dst), ("et", et))])
        for o, k in (("rd", "dst"), ("rs", "src")):
            v(vec.scalar_tensor_tensor(e_[o][:], e_["et"][:], float(NP), e_[k][:], ALU.mult, ALU.add))
        need("sp", now("dve"))
        out_ = []
        for name, k, pd_ in (("src", "src", 0), ("dst", "dst", 0), ("to_dst", "dst", 1),
                             ("to_type_dst", "rd", 1), ("to_type_src", "rs", 1)):
            out_.append(dma("sp", "lo_" + name, lists[name][0:E].rearrange("(p c) -> p c", p=EP), e_[k][:]))
            out_.append(dma("sp", "lp_" + name, lists[name][E:ET * P].rearrange("(a n) -> a n", a=1), padc[:, pd_, :]))
        need("sp", *out_)
        barrier()

    loop_sems = []

    def scatter_sum(nm, target, passes, rows):
        if not loop_sems:
            loop_sems.extend(top.enter_context(nc.semaphore("loop_" + k)) for k in ("dve", "pe", "feat", "sum", "put"))
        s_dve, s_pe, s_feat, s_sum, s_put = loop_sems
        with scope() as c:
            at = [4 * D]

            def take(width, dtype=F32):
                at[0] += width
                r = room[:, at[0] - width:at[0]]
                return r if dtype is F32 else r.bitcast(dtype)

            zero = take(NT * D)
            frm, to = take(ET, I32), take(ET, I32)
            low = take(P)
            spare = take(1)
            gi, si, wi = (take(1, I32) for _ in range(3))
            sf, rep = take(1), take(1)
            wide_, eq, before, msg, cur, new = (take(P) for _ in range(6))
            if nm is None:
                v(vec.memset(zero[:], 1.0))
                need("sp", now("dve"))
                t0 = dma("sp", "z_feat", feat.rearrange("(i p) f -> p i f", p=P), zero[:].rearrange("p (i f) -> p i f", f=D))
            else:
                need("sp", now("dve"), now("act"))
                t0 = dma("sp", "z_feat", feat.rearrange("(i p) f -> p i f", p=P), nm)
            need("dve", t0)
            need("sp", t0)
            v(vec.memset(zero[:], 0.0))
            need("sp", now("dve"))
            for r0 in range(0, rows, NP):
                need("sp", dma("sp", "z_zero", target[r0:r0 + NP, :].rearrange("(i p) f -> p i f", p=P),
                               zero[:].rearrange("p (i f) -> p i f", f=D)))
            need("sp", dma("sp", "z_zero", target[NREL * NP:SUMS, :], zero[:, 0:D]))
            need("pool", G(pool.affine_select(out=low[:], in_=ones_f[:], compare_op=ALU.is_gt, fill=0.0, base=0,
                                              pattern=[[-1, P]], channel_multiplier=1)))
            need("pool", G(pool.iota(spare[:], pattern=[[0, 1]], base=NREL * NP, channel_multiplier=1,
                                     allow_small_or_imprecise_dtypes=True)))
            for from_, to_ in passes:
                barrier()
                t0 = [dma("sp", "z_from", frm[:], lists[from_].rearrange("(p t) -> p t", p=P)),
                      dma("sp", "z_to", to[:], lists[to_].rearrange("(p t) -> p t", p=P))]
                need("sp", *t0)
                barrier()
                with nc.Fori(0, ET) as t_:
                    vec.tensor_copy(gi[:], frm[:, bass.ds(t_, 1)]).then_inc(s_dve, 1)
                    vec.tensor_copy(si[:], to[:, bass.ds(t_, 1)]).then_inc(s_dve, 1)
                    vec.wait_ge(s_dve, 2)
                    vec.tensor_copy(sf[:], si[:]).then_inc(s_dve, 1)
                    vec.wait_ge(s_dve, 3)
                    vec.tensor_copy(wide_[:], sf[:, 0:1].to_broadcast([P, P])).then_inc(s_dve, 1)
                    pool.wait_ge(s_dve, 2)
                    pool.indirect_dma_start(out=msg[:], out_offset=None, in_=feat,
                                            in_offset=bass.IndirectOffsetOnAxis(ap=gi[:], axis=0)).then_inc(s_feat, 16)
                    pool.indirect_dma_start(out=cur[:], out_offset=None, in_=target,
                                            in_offset=bass.IndirectOffsetOnAxis(ap=si[:], axis=0)).then_inc(s_sum, 16)
                    pe.wait_ge(s_dve, 4)
                    pe.matmul(bank[0][:, 0:P], wide_[:], ident[:], start=True, stop=True).then_inc(s_pe, 1)
                    vec.wait_ge(s_pe, 1)
                    vec.tensor_scalar(eq[:], bank[0][:, 0:P], sf[:, 0:1], None, ALU.is_equal).then_inc(s_dve, 1)
                    vec.wait_ge(s_dve, 5)
                    vec.tensor_tensor(before[:], eq[:], low[:], ALU.mult).then_inc(s_dve, 1)
                    vec.wait_ge(s_dve, 6)
                    vec.tensor_reduce(rep[:], before[:], axis=AX.X, op=ALU.max).then_inc(s_dve, 1)
                    vec.wait_ge(s_dve, 7)
                    vec.scalar_tensor_tensor(before[:, 0:1], spare[:], sf[:, 0:1], rep[:], ALU.subtract, ALU.mult).then_inc(s_dve, 1)
                    vec.wait_ge(s_dve, 8)
                    vec.tensor_tensor(wi[:], before[:, 0:1], sf[:], ALU.add).then_inc(s_dve, 1)
                    pe.wait_ge(s_dve, 9)
                    pe.wait_ge(s_feat, 16)
                    pe.matmul(bank[1][:, 0:P], eq[:], msg[:], start=True, stop=True).then_inc(s_pe, 1)
                    vec.wait_ge(s_pe, 2)
                    vec.wait_ge(s_sum, 16)
                    vec.tensor_tensor(new[:], bank[1][:, 0:P], cur[:], ALU.add).then_inc(s_dve, 1)
                    pool.wait_ge(s_dve, 10)
                    pool.indirect_dma_start(out=target, out_offset=bass.IndirectOffsetOnAxis(ap=wi[:], axis=0),
                                            in_=new[:], in_offset=None).then_inc(s_put, 16)
                    pool.wait_ge(s_put, 16)
                    barrier()
                    for s in loop_sems:
                        pool.sem_clear(s)
                    barrier()
            barrier()

    chunk_buf = {}

    def load_sums(bk, table, r0, ci):
        buf_ = chunk_buf["buf"]
        c_, cw = CH[ci]
        need("sp", chunk_buf.get("free"))
        R_, i0, n_ = chunk_rows(ci)
        a = r0 + i0 * P
        if n_ > 1:
            t0 = dma("sp", "z_chunk", buf_[:, 0:n_, :], table[a:a + n_ * P, :].rearrange("(i p) f -> p i f", p=P))
        else:
            t0 = dma("sp", "z_chunk", buf_[0:R_, 0, :], table[a:a + R_, :])
        need("pe", t0, bank_free[bk])
        for i, k in tiles_of(ci):
            r_ = rows_of(i)
            m = pe.transpose(bank[bk][:, k * P:k * P + r_], buf_[0:r_, k, :], ident[0:r_, 0:r_])
        chunk_buf["free"] = T(m)
        return chunk_buf["free"]

    def degrees():
        with scope() as c1:
            nd = sbuf(c1, "nd", [EP, 3, N // EP], F32)
            if fast:
                degs = sbuf(c1, "degs", [1, N], F32)
                for ci, (c, cw) in enumerate(CH):
                    need("pe", bank_free[ci % 8])
                    for i in range(NT):
                        m = pe.matmul(bank[ci % 8][0:1, 0:cw], ones_bf[:], A[:, i, c:c + cw], start=(i == 0), stop=(i == NT - 1))
                    need("dve", T(m))
                    t = bank_free[ci % 8] = V(vec.tensor_copy(degs[:, c:c + cw], bank[ci % 8][0:1, 0:cw]))
                need("sp", t)
                t = dma("sp", "deg_out", deg_row.rearrange("(a n) -> a n", a=1), degs[:])
            else:
                scatter_sum(None, sums, [("src", "to_dst")], NP)
                t = dma("sp", "deg_out", deg_row.rearrange("(p c) -> p c", p=EP),
                        bass.AP(sums.tensor, 0, [[N // EP * D, EP], [D, N // EP]]), allow_slow_non_contiguous=True)
            need("sp", t)
            t = dma("sp", "deg_in", nd[:, 0, :], deg_row.rearrange("(p c) -> p c", p=EP))
            need("dve", t)
            v(vec.tensor_scalar(nd[:, 1, :], nd[:, 0, :], 1.0, None, ALU.add))
            need("act", now("dve"))
            need("dve", S(act.activation(nd[:, 1, :], nd[:, 1, :], ACT.Sqrt)))
            v(vec.tensor_scalar(nd[:, 2, :], nd[:, 0, :], 1.0, None, ALU.max))
            v(vec.reciprocal(nd[:, 1:3, :], nd[:, 1:3, :]))
            need("sp", now("dve"))
            need("sp", dma("sp", "dinv_out", dinv_row.rearrange("(p c) -> p c", p=EP), nd[:, 1, :]),
                 dma("sp", "invd_out", invd_row.rearrange("(p c) -> p c", p=EP), nd[:, 2, :]))
            barrier()

    def symmetric_steps(ctx):
        rs = sbuf(ctx, "sym_rows", [P, NP], I32)
        cs = sbuf(ctx, "sym_cols", [P, NT, P], I32)
        pdv = pd.rearrange("(i p) n -> p i n", p=P)
        sdv = sd.rearrange("(i p) n -> p i n", p=P)
        free_rows = free_cols = None
        for j in range(NT):
            need("sp", free_rows)
            t_r = dma("sp", "sym_r", rs[:], pd[j * P:(j + 1) * P, :])
            need("sp", free_cols)
            t_c = dma("sp", "sym_c", cs[:], pdv[:, :, j * P:(j + 1) * P])
            yield
            need("pe", t_r)
            need("dve", t_c)
            for i0 in range(0, NT, 4):
                k = 6 + (i0 // 4) % 2
                n_ = min(4, NT - i0)
                need("pe", bank_free[k])
                for i in range(n_):
                    m = pe.transpose(bank[k][:, i * P:(i + 1) * P], rs[:, (i0 + i) * P:(i0 + i + 1) * P].bitcast(F32), ident[:])
                t_t = T(m)
                need("dve", t_t)
                o = cs[:, i0:i0 + n_, :].rearrange("p i n -> p (i n)").bitcast(U16)
                bank_free[k] = V(vec.tensor_tensor(o, o, bank[k][:, 0:n_ * P].bitcast(U16), ALU.add))
            free_rows = t_t
            need("sp", bank_free[k])
            free_cols = dma("sp", "sym_o", sdv[:, :, j * P:(j + 1) * P], cs[:])
        scale_tmp["sym"] = free_cols
        yield

    def step(bg):
        next(bg, None)

    def block_gru():
        with scope() as c:
            hn = sbuf(c, "g_hn", [P, NT, D], F32)
            layer_norm(hn)
            NL = g_w.shape[0]
            h16 = [feature_pair(c, f"g_h16{i}") for i in range(2)]
            ht = sbuf(c, "g_ht", [P, N], F32)
            wl = sbuf(c, "g_wl", [P, NL, D], F32)
            wt = {}
            raw = sbuf(c, "g_raw", [P, 3, D], F32)
            bb = sbuf(c, "g_b", [P, 3, 3], F32)
            t_wl = dma("act", "g_wl", wl[:], g_w.rearrange("l i o -> i l o"))
            t_b = [dma("act", "g_bi", bb[:, 0, :], g_bih.rearrange("(b o) -> o b", o=P), allow_slow_non_contiguous=True),
                   dma("act", "g_bh", bb[:, 1, :], g_bhh.rearrange("(b o) -> o b", o=P), allow_slow_non_contiguous=True)]
            t_tr = None
            for n_, a in (("ih", g_ih), ("hh", g_hh)):
                wt[n_] = sbuf(c, "g_w" + n_, [P, 3, D], F32)
                need("act", t_tr)
                t_raw = dma("act", "g_raw", raw[:], a.rearrange("(b o) i -> o b i", o=P))
                need("pe", t_raw, bank_free[7])
                for b in range(3):
                    m = pe.transpose(bank[7][:, b * P:(b + 1) * P], raw[:, b, :], ident[:])
                t_tr = T(m)
                need("act", t_tr)
                bank_free[7] = t_w = S(act.activation(wt[n_][:], bank[7][:, 0:3 * P].rearrange("p (b o) -> p b o", b=3), ACT.Copy))
            need("dve", *t_b)
            t_bb = v(vec.tensor_tensor(bb[:, 2, :], bb[:, 0, :], bb[:, 1, :], ALU.add))
            v(vec.tensor_tensor(xn[:], xn[:], hn[:], ALU.add))
            v(vec.memset(h16[1][:, :, NT - 1, :] if fast else h16[1][:, NT - 1, :], 0.0))
            t_h = split_fixed(h16[0], hn)
            t_ht = to_feature_rows(ht, hn)
            need("pe", t_wl, t_w, t_ht)
            need("act", t_bb)
            need("dve", t_ht)
            buf = {n_: [sbuf(c, f"g_{n_}{i}", [P, BANK], F32) for i in range(2)] for n_ in ("ag", "m", "r", "z", "t", "n")}
            bg = symmetric_steps(c) if fast else iter(())
            BR, BZ, BI, BH, BM, BT = 2, 3, 4, 5, 6, 7
            last_use = {}

            def gate(ci, l, t_agg):
                c_, cw = CH[ci]
                q = ci % 2
                ag, m_, r_, z_, t_, n_ = (buf[b][q][:, 0:cw] for b in ("ag", "m", "r", "z", "t", "n"))
                h_ = ht[:, c_:c_ + cw]
                need("act", t_agg, last_use.get(("pe", q)))
                bank_free[q] = t0 = S(act.activation(ag, bank[q][:, 0:cw], ACT.Copy, scale=1.0 / FIXED))
                need("pe", t0, bank_free[BM])
                t0 = T(pe.matmul(bank[BM][:, 0:cw], wl[:, l, :], ag, start=True, stop=True))
                need("act", t0)
                bank_free[BM] = t_m = S(act.activation(m_, bank[BM][:, 0:cw], ACT.Copy))
                need("pe", bank_free[BR], bank_free[BZ], bank_free[BI], bank_free[BH])
                pe.matmul(bank[BR][:, 0:cw], wt["hh"][:, 0, :], h_, start=True, stop=False)
                pe.matmul(bank[BZ][:, 0:cw], wt["hh"][:, 1, :], h_, start=True, stop=False)
                t_hh = T(pe.matmul(bank[BH][:, 0:cw], wt["hh"][:, 2, :], h_, start=True, stop=True))
                need("pe", t_m)
                t_r = T(pe.matmul(bank[BR][:, 0:cw], wt["ih"][:, 0, :], m_, start=False, stop=True))
                t_z = T(pe.matmul(bank[BZ][:, 0:cw], wt["ih"][:, 1, :], m_, start=False, stop=True))
                t_i = T(pe.matmul(bank[BI][:, 0:cw], wt["ih"][:, 2, :], m_, start=True, stop=True))
                last_use[("pe", q)] = t_i
                need("act", t_r, last_use.get(("dve", q)))
                bank_free[BR] = t0 = S(act.activation(r_, bank[BR][:, 0:cw], ACT.Sigmoid, bias=bb[:, 2, 0:1]))
                need("act", t_z)
                bank_free[BZ] = t_zz = S(act.activation(z_, bank[BZ][:, 0:cw], ACT.Sigmoid, bias=bb[:, 2, 1:2]))
                need("dve", t0, t_hh)
                bank_free[BH] = v(vec.scalar_tensor_tensor(t_, bank[BH][:, 0:cw], bb[:, 1, 2:3], r_, ALU.add, ALU.mult))
                need("dve", t_i)
                bank_free[BI] = t0 = v(vec.tensor_tensor(t_, t_, bank[BI][:, 0:cw], ALU.add))
                need("act", t0)
                t0 = S(act.activation(n_, t_, ACT.Tanh, bias=bb[:, 0, 2:3]))
                need("dve", t0)
                v(vec.tensor_tensor(t_, h_, n_, ALU.subtract))
                need("dve", t_zz)
                v(vec.tensor_tensor(t_, t_, z_, ALU.mult))
                last_use[("dve", q)] = t0 = v(vec.tensor_tensor(h_, t_, n_, ALU.add))
                return t0

            def finish(ci, l, t_new, toks):
                need("pe", t_new)
                c_, cw = CH[ci]
                t0 = node_tiles_to_bank(BT, ht[:, c_:c_ + cw], ci)
                if l == NL - 1:
                    add_to_x(BT, ci, t0)
                else:
                    toks += split_from_bank(BT, h16[(l + 1) % 2], ci, t0, FIXED)

            for l in range(NL):
                toks = []
                cur = h16[l % 2]
                sum_all(cur)
                t_agg = {0: sum_edges(0, cur, 0, t_h)}
                new = {}
                for ci in range(len(CH)):
                    if ci + 1 < len(CH):
                        t_agg[ci + 1] = sum_edges((ci + 1) % 2, cur, ci + 1, t_h)
                    new[ci] = gate(ci, l, t_agg[ci])
                    if ci:
                        finish(ci - 1, l, new[ci - 1], toks)
                    step(bg)
                finish(len(CH) - 1, l, new[len(CH) - 1], toks)
                t_h = toks
            for _ in bg:
                pass
            barrier()

    def block_gcn():
        with scope() as c:
            hn = sbuf(c, "c_hn", [P, NT, D], F32)
            layer_norm(hn)
            h16 = feature_pair(c, "c_h16")
            yt = sbuf(c, "c_yt", [P, N], F32)
            dinv = sbuf(c, "c_dinv", [P, N], F32)
            w01 = [sbuf(c, f"c_w{i}", [P, D], F32) for i in range(2)]
            b01 = sbuf(c, "c_b", [P, 2], F32)
            mx = sbuf(c, "c_mx", [P, len(CH)], F32)
            sc = sbuf(c, "c_sc", [P, 4], F32)
            buf = {n_: [sbuf(c, f"c_{n_}{i}", [P, BANK], F32) for i in range(2)] for n_ in ("ag", "t", "o")}
            ld = [dma("sp", "c_w0", w01[0][:], c_w0), dma("sp", "c_w1", w01[1][:], c_w1),
                  dma("act", "c_b0", b01[:, 0:1], c_b0.rearrange("(p a) -> p a", a=1)),
                  dma("act", "c_b1", b01[:, 1:2], c_b1.rearrange("(p a) -> p a", a=1)),
                  dma("sp", "c_dinv", dinv[:], bass.AP(dinv_row.tensor, 0, [[0, P], [1, N]]))]
            t_h = split_fixed(h16, hn)
            for k in ("pe", "act", "dve"):
                need(k, *ld)
            use = {}
            sum_all(h16)
            t_agg = {0: sum_edges(0, h16, 0, t_h)}
            for ci, (c_, cw) in enumerate(CH):
                if ci + 1 < len(CH):
                    t_agg[ci + 1] = sum_edges((ci + 1) % 2, h16, ci + 1, t_h)
                q = ci % 2
                ag, t_ = buf["ag"][q][:, 0:cw], buf["t"][q][:, 0:cw]
                y_ = yt[:, c_:c_ + cw]
                need("act", t_agg[ci], use.get(("ag", q)), use.get(("t", q)))
                bank_free[q] = t0 = S(act.activation(ag, bank[q][:, 0:cw], ACT.Copy, scale=1.0 / FIXED))
                need("pe", t0, bank_free[2 + q])
                use[("ag", q)] = t0 = T(pe.matmul(bank[2 + q][:, 0:cw], w01[0][:], ag, start=True, stop=True))
                need("act", t0)
                bank_free[2 + q] = t0 = S(act.activation(t_, bank[2 + q][:, 0:cw], ACT.Identity, bias=b01[:, 0:1]))
                need("dve", t0)
                use[("t", q)] = v(vec.tensor_tensor(y_, t_, dinv[:, c_:c_ + cw], ALU.mult))
                v(vec.tensor_reduce(mx[:, ci:ci + 1], y_, axis=AX.X, op=ALU.max, apply_absolute_value=True))
            v(vec.tensor_reduce(sc[:, 0:1], mx[:], axis=AX.X, op=ALU.max))
            power_scale(sc[:, 0:1], sc[:, 1:2], sc[:, 2:3], sc[:, 3:4])
            t_h = [(done["pe"], count["pe"])]
            toks = []
            for ci, (c_, cw) in enumerate(CH):
                q = ci % 2
                t_ = buf["t"][q][:, 0:cw]
                need("dve", use.get(("tr", q)))
                t0 = v(vec.tensor_scalar(t_, yt[:, c_:c_ + cw], sc[:, 1:2], None, ALU.mult))
                need("pe", t0)
                t0 = use[("tr", q)] = node_tiles_to_bank(6 + q, t_, ci)
                need("act", t_h)
                toks += split_from_bank(6 + q, h16, ci, t0, 1.0)
            sum_all(h16)
            t_agg = {0: sum_edges(0, h16, 0, toks)}
            for ci, (c_, cw) in enumerate(CH):
                if ci + 1 < len(CH):
                    t_agg[ci + 1] = sum_edges((ci + 1) % 2, h16, ci + 1, toks)
                q = ci % 2
                ag, o_ = buf["ag"][q][:, 0:cw], buf["o"][q][:, 0:cw]
                need("dve", t_agg[ci], use.get(("ag", q)))
                bank_free[q] = v(vec.scalar_tensor_tensor(ag, bank[q][:, 0:cw], sc[:, 2:3], yt[:, c_:c_ + cw],
                                                          ALU.mult, ALU.add))
                t0 = v(vec.tensor_tensor(ag, ag, dinv[:, c_:c_ + cw], ALU.mult))
                need("pe", t0, bank_free[2 + q])
                use[("ag", q)] = t0 = T(pe.matmul(bank[2 + q][:, 0:cw], w01[1][:], ag, start=True, stop=True))
                need("act", t0, use.get(("o", q)))
                bank_free[2 + q] = t0 = S(act.activation(o_, bank[2 + q][:, 0:cw], ACT.Identity, bias=b01[:, 1:2]))
                need("pe", t0)
                use[("o", q)] = t0 = node_tiles_to_bank(6 + q, o_, ci)
                add_to_x(6 + q, ci, t0)
            barrier()

    def block_relations():
        PT = 5
        with scope() as c:
            hn = sbuf(c, "r_hn", [P, NT, D], F32)
            layer_norm(hn)
            h16 = feature_pair(c, "r_h16")
            ht = sbuf(c, "r_ht", [P, N], F32)
            wr = sbuf(c, "r_w", [P, NREL, D], F32)
            ws = sbuf(c, "r_ws", [P, D], F32)
            sel = sbuf(c, "r_sel", [P, 4, P], F32)
            ones32 = sbuf(c, "r_ones", [P, 32], BF16)
            wd = [sbuf(c, f"r_wd{i}", [P, PT, BANK], I32) for i in range(2)]
            f8 = [sbuf(c, f"r_f8{i}", [P, PT, 4 * BANK], F8) for i in range(2)]
            acc = sbuf(c, "r_acc", [P, 2, BANK], I32)
            accb = sbuf(c, "r_accb", [P, 2, 4 * BANK], BF16)
            rd = sbuf(c, "r_rd", [P, BANK], F32)
            bc = [sbuf(c, f"r_bc{i}", [P, BANK], F32) for i in range(2)]
            ags = [sbuf(c, f"r_ags{i}", [P, BANK], F32) for i in range(2)]
            ot = sbuf(c, "r_ot", [P, BANK], F32)
            ld = [dma("sp", "r_wr", wr[:], r_w.rearrange("r i o -> i r o")), dma("sp", "r_ws", ws[:], r_self)]
            v(vec.memset(ones32[:], 1.0))
            need("pool", G(pool.memset(sel[:], 0.0)))
            need("pe", G(pool.affine_select(out=sel[:], in_=sel[:], compare_op=ALU.not_equal, fill=1.0, base=0,
                                            pattern=[[-32, 4], [0, P]], channel_multiplier=1)))
            t_h = split_fixed(h16, hn)
            t_ht = to_feature_rows(ht, hn)
            need("pe", t_h, t_ht, now("dve"), *ld)
            if not fast:
                both = [("src", "to_type_dst"), ("dst", "to_type_src")]
                scatter_sum(None, degs8, both, NREL * NP)
                scatter_sum(h16, sums, both, NREL * NP)
            sdv = sd.rearrange("(i p) n -> p i n", p=P)
            BD, BO, BX = 4, 6, 7
            use = {}
            n_piece = 0
            need("sp", scale_tmp.get("sym"))
            acc_free = accb_free = rd_free = ot_free = None

            def relation(ci, h, k, t_sum):
                q, cw = k % 2, CH[ci][1]
                need("dve", t_sum, use.get(("ags", q)))
                bank_free[k] = use[("bc", q)] = t0 = v(vec.scalar_tensor_tensor(
                    ags[q][:, 0:cw], bank[k][:, 0:cw], 1.0 / FIXED, bc[q][:, 0:cw], ALU.mult, ALU.mult))
                need("pe", t0)
                if h == 0 and k == 0:
                    need("pe", bank_free[BO])
                use[("ags", q)] = T(pe.matmul(bank[BO][:, 0:cw], wr[:, 2 * k + h, :], ags[q][:, 0:cw],
                                              start=(h == 0 and k == 0), stop=False))

            for ci, (c_, cw) in enumerate(CH):
                for h in range(2):
                    if not fast:
                        for k in range(4):
                            q = k % 2
                            t0 = load_sums(7, degs8, (2 * k + h) * NP, ci)
                            need("dve", t0, use.get(("bc", q)))
                            bank_free[7] = v(vec.tensor_scalar(bc[q][:, 0:cw], bank[7][:, 0:cw], 1.0, None, ALU.max))
                            v(vec.reciprocal(bc[q][:, 0:cw], bc[q][:, 0:cw]))
                            relation(ci, h, k, load_sums(k, sums, (2 * k + h) * NP, ci))
                        continue
                    need("pool", acc_free)
                    need("pool", G(pool.memset(acc[:], 0)))
                    for k in range(4):
                        need("pe", bank_free[k])
                    for p0 in range(0, NT, PT):
                        q = n_piece % 2
                        n_piece += 1
                        need("sp", use.get(("wd", q)))
                        t0 = dma("sp", f"r_wd{q}", wd[q][:, :, 0:cw], sdv[:, p0:p0 + PT, c_:c_ + cw])
                        need("dve", t0)
                        t0 = v(vec.tensor_scalar(wd[q][:, :, 0:cw], wd[q][:, :, 0:cw], 4 * h, 0x0F0F0F0F,
                                                 ALU.logical_shift_right, ALU.bitwise_and))
                        need("dve", use.get(("f8", q)))
                        t1_ = v(vec.tensor_copy(f8[q][:, :, 0:4 * cw], wd[q][:, :, 0:cw].bitcast(U8), saturate=False))
                        need("pool", t0)
                        for i in range(PT):
                            g_ = 0 if p0 + i < 13 else 1
                            t_p = G(pool.tensor_tensor(acc[:, g_, 0:cw], acc[:, g_, 0:cw], wd[q][:, i, 0:cw], ALU.add))
                            need("pool", t_p)
                        use[("wd", q)] = [t_p, t1_]
                        need("pe", t1_)
                        for i in range(PT):
                            for part in range(2):
                                for k in range(4):
                                    m = pe.matmul(bank[k][:, 0:cw], h16[:, part, p0 + i, :],
                                                  f8[q][:, i, 0:4 * cw].rearrange("p (n k) -> p n k", k=4)[:, :, k],
                                                  start=(p0 + i == 0 and part == 0),
                                                  stop=(p0 + i == NT - 1 and part == 1))
                        use[("f8", q)] = t_mm = T(m)
                    need("dve", t_p, accb_free)
                    acc_free = v(vec.tensor_copy(accb[:, :, 0:4 * cw], acc[:, :, 0:cw].bitcast(U8)))
                    need("pe", acc_free, bank_free[BD])
                    for k in range(4):
                        for g_ in range(2):
                            m = pe.matmul(bank[BD][32 * k:32 * k + 32, 0:cw], ones32[:],
                                          accb[:, g_, 0:4 * cw].rearrange("p (n k) -> p n k", k=4)[:, :, k],
                                          start=(g_ == 0), stop=(g_ == 1))
                    accb_free = t0 = T(m)
                    need("dve", t0, rd_free)
                    bank_free[BD] = v(vec.tensor_scalar(rd[:, 0:cw], bank[BD][:, 0:cw], 1.0, None, ALU.max))
                    t0 = v(vec.reciprocal(rd[:, 0:cw], rd[:, 0:cw]))
                    need("pe", t0)
                    for k in range(4):
                        q = k % 2
                        bb_ = (5, 7)[q]
                        need("pe", bank_free[bb_])
                        rd_free = t0 = T(pe.matmul(bank[bb_][:, 0:cw], sel[:, k, :], rd[:, 0:cw], start=True, stop=True))
                        need("act", t0, use.get(("bc", q)))
                        bank_free[bb_] = t0 = S(act.activation(bc[q][:, 0:cw], bank[bb_][:, 0:cw], ACT.Copy))
                        need("dve", t0)
                        relation(ci, h, k, t_mm)
                t0 = T(pe.matmul(bank[BO][:, 0:cw], ws[:], ht[:, c_:c_ + cw], start=False, stop=True))
                need("act", t0, ot_free)
                bank_free[BO] = t0 = S(act.activation(ot[:, 0:cw], bank[BO][:, 0:cw], ACT.Copy))
                need("pe", t0)
                ot_free = t0 = node_tiles_to_bank(BX, ot[:, 0:cw], ci)
                add_to_x(BX, ci, t0)
            barrier()

    def block_experts():
        NLAY, H = m_rw.shape[0], m_win.shape[1]
        KB = H // P
        NWK, NSG = m_ww.shape[1], m_w1.shape[1]
        NE = NWK + NSG
        FB = m_w1.shape[3] // P
        with scope() as c:
            h2 = sbuf(c, "m_h", [P, NT, H], F32)
            bcast = sbuf(c, "m_bias", [P, NE * H], F32)
            agg = sbuf(c, "m_agg", [P, KB, BANK], F32)
            hT = sbuf(c, "m_hT", [P, KB, BANK], F32)
            rw = sbuf(c, "m_rw", [P, 2 * KB, NE + 1], F32)
            rb = sbuf(c, "m_rb", [P, NE + 1], F32)
            sc = sbuf(c, "m_sc", [P, 4], F32)
            wout = sbuf(c, "m_wo", [P, KB, D], F32)
            bout = sbuf(c, "m_bo", [P, D], F32)
            prio = sbuf(c, "m_prio", [P, NE], F32)
            t_prio = G(pool.iota(prio[:], pattern=[[-1, NE]], base=NE, channel_multiplier=0,
                                 allow_small_or_imprecise_dtypes=True))
            t_wo = [dma("act", "m_wo", wout[:], m_wout.rearrange("(k p) o -> p k o", p=P)),
                    dma("act", "m_bo", bout[:], bass.AP(m_bout.tensor, m_bout.offset, [[0, P], [1, D]]))]
            with scope() as c0:
                hn = sbuf(c0, "m_hn", [P, NT, D], F32)
                layer_norm(hn)
                need("sp", now("dve"))
                t_park = dma("sp", "park", xpark, xn[:].rearrange("p i f -> p (i f)"))
                win = sbuf(c0, "m_win", [P, H], F32)
                bin_ = sbuf(c0, "m_bin", [P, H], F32)
                xT = [sbuf(c0, f"m_xT{i}", [P, BANK], F32) for i in range(2)]
                ld = [dma("act", "m_win", win[:], m_win),
                      dma("act", "m_bin", bin_[:], bass.AP(m_bin.tensor, m_bin.offset, [[0, P], [1, H]]))]
                need("pe", now("dve"), *ld)
                need("dve", *ld)
                xt_free = [None, None]
                for i0 in range(0, NT, 4):
                    q = (i0 // 4) % 2
                    n_ = min(4, NT - i0)
                    need("pe", bank_free[6 + q])
                    for k in range(n_):
                        m = pe.transpose(bank[6 + q][:, k * P:(k + 1) * P], hn[:, i0 + k, :], ident[:])
                    need("act", T(m), xt_free[q])
                    bank_free[6 + q] = t0 = S(act.activation(xT[q][:, 0:n_ * P], bank[6 + q][:, 0:n_ * P], ACT.Copy))
                    need("pe", t0)
                    for k in range(n_):
                        b_ = (i0 + k) % 6
                        need("pe", bank_free[b_])
                        xt_free[q] = t0 = T(pe.matmul(bank[b_][:, 0:H], xT[q][:, k * P:(k + 1) * P], win[:], start=True, stop=True))
                        need("dve", t0)
                        bank_free[b_] = V(vec.tensor_tensor(h2[:, i0 + k, :], bank[b_][:, 0:H], bin_[:], ALU.add))
                need("sp", t_park)
                barrier()
            with scope() as c0:
                h16 = feature_pair(c0, "m_h16", H)
                ww = sbuf(c0, "m_ww", [P, KB, NWK * H], F32)
                w1 = sbuf(c0, "m_w1", [P, NSG, KB, FB * P], F32)
                w2 = sbuf(c0, "m_w2", [P, NSG, FB, H], F32)
                b1 = sbuf(c0, "m_b1", [P, NSG * FB], F32)
                NSH = 2 * FB
                xroom = xn[:].rearrange("p i f -> p (i f)")
                n_room = min(NSH, NT * D // BANK)
                sh = [xroom[:, i * BANK:(i + 1) * BANK] for i in range(n_room)]
                sh += [sbuf(c0, f"m_sh{i}", [P, BANK], F32) for i in range(NSH - n_room)]
                wtmp = sbuf(c0, "m_wtmp", [P, 2 * H], F32)
                tmp = [wtmp[:, i * H:(i + 1) * H] for i in range(2)]
                invd = sbuf(c0, "m_invd", [P, BANK], F32)
                lg = sbuf(c0, "m_lg", [P, 4, NE + 1], F32)
                rt = [sbuf(c0, f"m_rt{i}", [P, 4, NE], F32) for i in range(5)]
                sm = sbuf(c0, "m_sm", [P, 10, 4], F32)
                gates = [sbuf(c0, f"m_g{i}", [P, 4, NE], F32) for i in range(2)]
                v(vec.memset(rw[:, KB:2 * KB, NE:NE + 1], 0.0))
                for l in range(NLAY):
                    ld_r = [dma("act", "m_rw", rw[:, :, 0:NE], m_rw[l].rearrange("(k p) e -> p k e", p=P)),
                            dma("act", "m_cw", rw[:, 0:KB, NE:NE + 1], m_cw[l].rearrange("(k p) e -> p k e", p=P), allow_slow_non_contiguous=True),
                            dma("act", "m_rb", rb[:, 0:NE], bass.AP(m_rb.tensor, m_rb.offset + l * NE, [[0, P], [1, NE]])),
                            dma("act", "m_cb", rb[:, NE:NE + 1], bass.AP(m_cb.tensor, m_cb.offset + l, [[0, P], [1, 1]]))]
                    ld_w1 = [dma("sp", f"m_w1{e}", w1[:, e], m_w1[l, e].rearrange("(k p) f -> p k f", p=P)) for e in range(NSG)]
                    ld_b1 = dma("act", "m_b1", b1[:], m_b1[l].rearrange("e (k p) -> p (e k)", p=P), allow_slow_non_contiguous=True)
                    ld_w2 = [dma("sp", f"m_w2{e}", w2[:, e], m_w2[l, e].rearrange("(k p) h -> p k h", p=P)) for e in range(NSG)]
                    ld_ww = [dma("sp", f"m_ww{e}", ww[:, :, e * H:(e + 1) * H], m_ww[l, e].rearrange("(k p) h -> p k h", p=P)) for e in range(NWK)]
                    ld_bb = [dma("act", "m_wb", bcast[:, 0:NWK * H], bass.AP(m_wb.tensor, m_wb.offset + l * NWK * H, [[0, P], [1, NWK * H]])),
                             dma("act", "m_b2", bcast[:, NWK * H:NE * H], bass.AP(m_b2.tensor, m_b2.offset + l * NSG * H, [[0, P], [1, NSG * H]]))]
                    v(vec.tensor_reduce(sc[:, 0:1], h2[:], axis=AX.XY, op=ALU.max, apply_absolute_value=True))
                    need("pe", now("dve"), bank_free[6], bank_free[7])
                    t0 = T(pe.transpose(bank[6][0:1, 0:P], sc[:, 0:1], ident[:]))
                    need("dve", t0)
                    t0 = v(vec.tensor_reduce(sc[0:1, 1:2], bank[6][0:1, 0:P], axis=AX.X, op=ALU.max))
                    need("pe", t0)
                    t0 = T(pe.matmul(bank[7][:, 0:1], ones_f[0:1, :], sc[0:1, 1:2], start=True, stop=True))
                    need("dve", t0)
                    v(vec.tensor_copy(sc[:, 0:1], bank[7][:, 0:1]))
                    power_scale(sc[:, 0:1], sc[:, 1:2], sc[:, 2:3], sc[:, 3:4])
                    bank_free[6] = bank_free[7] = now("dve")
                    need("act", now("dve"))
                    t_h = []
                    if not fast:
                        t_h = [v(vec.tensor_scalar(h16, h2[:], sc[:, 1:2], None, ALU.mult))]
                    for i0 in range(0, NT, 5) if fast else ():
                        hs = h2[:, i0:i0 + 5, :]
                        t0 = S(act.activation(h16[:, 0, i0:i0 + 5, :], hs, ACT.Copy, scale=sc[:, 1:2]))
                        need("dve", t0)
                        t_h.append(V(vec.scalar_tensor_tensor(h16[:, 1, i0:i0 + 5, :], hs, sc[:, 1:2],
                                                              h16[:, 0, i0:i0 + 5, :], ALU.mult, ALU.subtract)))
                    use = {}
                    t_route = {}
                    t_agg = {}

                    def edges(ci):
                        c_, cw = CH[ci]
                        for kb in range(KB):
                            if not fast:
                                t_agg[(ci, kb)] = load_sums(kb, block_sums[kb], 0, ci)
                                continue
                            need("pe", bank_free[kb])
                            for i in range(NT):
                                need("pe", t_h[i // 5])
                                for part in range(2):
                                    m = pe.matmul(bank[kb][:, 0:cw], h16[:, part, i, kb * P:(kb + 1) * P],
                                                  A[:, i, c_:c_ + cw], start=(i == 0 and part == 0),
                                                  stop=(i == NT - 1 and part == 1))
                            t_agg[(ci, kb)] = T(m)

                    def front(ci):
                        c_, cw = CH[ci]
                        ts = tiles_of(ci)
                        for kb in range(KB):
                            b_ = 2 + kb
                            need("pe", bank_free[b_], now("dve"))
                            for i, k in ts:
                                m = pe.transpose(bank[b_][:, k * P:(k + 1) * P], h2[:, i, kb * P:(kb + 1) * P], ident[:])
                            need("act", T(m), use.get("hT"))
                            wd_ = len(ts) * P
                            bank_free[b_] = t_hT = S(act.activation(hT[:, kb, 0:wd_], bank[b_][:, 0:wd_], ACT.Copy))
                        need("sp", use.get("invd"))
                        t0 = dma("sp", "invd", invd[:, 0:cw], bass.AP(invd_row.tensor, c_, [[0, P], [1, cw]]))
                        need("dve", t0, use.get("agg"))
                        for kb in range(KB):
                            need("dve", t_agg[(ci, kb)])
                            bank_free[kb] = use["invd"] = v(vec.scalar_tensor_tensor(
                                agg[:, kb, 0:cw], bank[kb][:, 0:cw], sc[:, 2:3], invd[:, 0:cw], ALU.mult, ALU.mult))
                        need("pe", use["invd"], t_hT, bank_free[2], *ld_r)
                        for i, k in ts:
                            r_ = rows_of(i)
                            for kk in range(2 * KB):
                                lhs = (hT if kk < KB else agg)[:, kk % KB, k * P:k * P + r_]
                                m = pe.matmul(bank[2][0:r_, k * (NE + 1):(k + 1) * (NE + 1)], lhs, rw[:, kk, :],
                                              start=(kk == 0), stop=(kk == 2 * KB - 1))
                        use["hT"] = t0 = T(m)
                        R_, _, n_ = chunk_rows(ci)
                        need("dve", t0, *ld_r)
                        need("dve", t_prio)
                        lg_ = lg[0:R_, 0:n_, :]
                        l_ = lg[0:R_, 0:n_, 0:NE]
                        v(vec.tensor_tensor(lg_, bank[2][0:R_, 0:n_ * (NE + 1)].rearrange("p (t e) -> p t e", e=NE + 1),
                                            rb[0:R_, None, :].to_broadcast([R_, n_, NE + 1]), ALU.add))
                        bank_free[2] = now("dve")
                        o1, o2, l2, e_ = (r[0:R_, 0:n_, :] for r in rt[0:4])
                        S1 = [sm[0:R_, i_, 0:n_] for i_ in range(10)]

                        def wide(a):
                            return a[:, :, None].to_broadcast([R_, n_, NE])

                        def pick(logits, top_, first, o):
                            v(vec.tensor_reduce(top_, logits, axis=AX.X, op=ALU.max))
                            v(vec.tensor_tensor(e_, logits, wide(top_), ALU.is_equal))
                            v(vec.tensor_tensor(e_, e_, prio[0:R_, None, :].to_broadcast([R_, n_, NE]), ALU.mult))
                            v(vec.tensor_reduce(first, e_, axis=AX.X, op=ALU.max))
                            v(vec.tensor_tensor(o, e_, wide(first), ALU.is_equal))

                        pick(l_, S1[0], S1[1], o1)
                        v(vec.scalar_tensor_tensor(l2, o1, -3e38, l_, ALU.mult, ALU.add))
                        pick(l2, S1[2], S1[3], o2)
                        v(vec.tensor_tensor(S1[4], S1[2], S1[0], ALU.subtract))
                        v(vec.tensor_scalar(S1[5], lg[0:R_, 0:n_, NE], -1.0, 80.0, ALU.mult, ALU.min))
                        need("act", now("dve"))
                        t0 = S(act.activation(sm[0:R_, 6:8, 0:n_], sm[0:R_, 4:6, 0:n_], ACT.Exp))
                        need("dve", t0)
                        v(vec.tensor_scalar(sm[0:R_, 8:10, 0:n_], sm[0:R_, 6:8, 0:n_], 1.0, None, ALU.add))
                        v(vec.reciprocal(sm[0:R_, 8:10, 0:n_], sm[0:R_, 8:10, 0:n_]))
                        v(vec.tensor_tensor(S1[8], S1[8], S1[9], ALU.mult))
                        v(vec.tensor_tensor(S1[6], S1[6], S1[8], ALU.mult))
                        g_ = gates[ci % 2][0:R_, 0:n_, :]
                        need("dve", use.get(("g", ci % 2)))
                        v(vec.tensor_tensor(o1, o1, wide(S1[8]), ALU.mult))
                        v(vec.tensor_tensor(o2, o2, wide(S1[6]), ALU.mult))
                        t_route[ci] = v(vec.tensor_tensor(g_, o1, o2, ALU.add))

                    n_sh = [0]
                    blk = {}

                    def hidden(ci, e):
                        c_, cw = CH[ci]
                        need("pe", ld_w1[e])
                        need("act", ld_b1)
                        for f in range(FB):
                            b_ = 4 + n_sh[0] % 2
                            s_i = n_sh[0] % NSH
                            n_sh[0] += 1
                            need("pe", bank_free[b_])
                            for kb in range(KB):
                                m = pe.matmul(bank[b_][:, 0:cw], w1[:, e, kb, f * P:(f + 1) * P], agg[:, kb, 0:cw],
                                              start=(kb == 0), stop=(kb == KB - 1))
                            t0 = use["agg"] = T(m)
                            need("act", t0, use.get(("sh", s_i)))
                            bank_free[b_] = t0 = S(act.activation(sh[s_i][:, 0:cw], bank[b_][:, 0:cw], ACT.Relu,
                                                                  bias=b1[:, e * FB + f:e * FB + f + 1]))
                            blk[(e, f)] = (s_i, t0)

                    def strong(ci, e):
                        need("pe", ld_w2[e])
                        need("dve", *ld_bb)
                        for i, k in tiles_of(ci):
                            r_ = rows_of(i)
                            b_ = 6 + k % 2
                            need("pe", bank_free[b_])
                            for f in range(FB):
                                s_i, t0 = blk[(e, f)]
                                need("pe", t0)
                                m = pe.matmul(bank[b_][0:r_, 0:H], sh[s_i][:, k * P:k * P + r_], w2[:, e, f, :],
                                              start=(f == 0), stop=(f == FB - 1))
                            t0 = T(m)
                            for f in range(FB):
                                use[("sh", blk[(e, f)][0])] = t0
                            q = k % 2
                            ge = NWK + e
                            need("dve", t0, t_route[ci])
                            bank_free[b_] = v(vec.tensor_tensor(tmp[q][0:r_, :], bank[b_][0:r_, 0:H],
                                                                bcast[0:r_, ge * H:(ge + 1) * H], ALU.add))
                            use[("g", ci % 2)] = v(vec.scalar_tensor_tensor(
                                h2[0:r_, i, :], tmp[q][0:r_, :], gates[ci % 2][0:r_, k, ge:ge + 1], h2[0:r_, i, :],
                                ALU.mult, ALU.add))

                    def weak(ci):
                        need("pe", *ld_ww)
                        for i, k in tiles_of(ci):
                            r_ = rows_of(i)
                            for pr in range(NWK * H // BANK):
                                b_ = 2 + pr % 2
                                need("pe", bank_free[b_])
                                for kb in range(KB):
                                    m = pe.matmul(bank[b_][0:r_, :], agg[:, kb, k * P:k * P + r_],
                                                  ww[:, kb, pr * BANK:(pr + 1) * BANK], start=(kb == 0), stop=(kb == KB - 1))
                                use["agg"] = t0 = T(m)
                                need("dve", t0)
                                bank_free[b_] = t0 = v(vec.tensor_tensor(wtmp[0:r_, :], bank[b_][0:r_, :],
                                                                         bcast[0:r_, pr * BANK:(pr + 1) * BANK], ALU.add))
                                for x_ in range(BANK // H):
                                    e = pr * (BANK // H) + x_
                                    w_ = wtmp[0:r_, x_ * H:(x_ + 1) * H]
                                    v(vec.tensor_scalar(w_, w_, 0.0, gates[ci % 2][0:r_, k, e:e + 1], ALU.max, ALU.mult))
                                    use[("g", ci % 2)] = v(vec.tensor_tensor(h2[0:r_, i, :], h2[0:r_, i, :], w_, ALU.add))

                    block_sums = [sums, degs8]
                    if not fast:
                        for kb in range(KB):
                            scatter_sum(h16[:, :, kb * P:(kb + 1) * P], block_sums[kb], [("src", "to_dst")], NP)
                    edges(0)
                    for ci in range(len(CH)):
                        front(ci)
                        hidden(ci, 0)
                        if ci + 1 < len(CH):
                            edges(ci + 1)
                        for e in range(NSG):
                            if e + 1 < NSG:
                                hidden(ci, e + 1)
                            strong(ci, e)
                        weak(ci)
                    barrier()
                barrier()
            with scope() as c0:
                xr = xn
                t_x = dma("sp", "unpark", xr[:].rearrange("p i f -> p (i f)"), xpark)
                need("dve", t_x, *t_wo)
                need("pe", *t_wo)
                out_full, out_tail = node_rows(out)
                t_o = []
                hf = {}
                for ci in range(len(CH)):
                    ts = tiles_of(ci)
                    for kb in range(KB):
                        b_ = 2 + kb
                        need("pe", bank_free[b_])
                        for i, k in ts:
                            m = pe.transpose(bank[b_][:, k * P:(k + 1) * P], h2[:, i, kb * P:(kb + 1) * P], ident[:])
                        wd_ = len(ts) * P
                        need("act", T(m), hf.get("hT"))
                        bank_free[b_] = t0 = S(act.activation(hT[:, kb, 0:wd_], bank[b_][:, 0:wd_], ACT.Copy))
                    need("pe", t0)
                    for i, k in ts:
                        r_ = rows_of(i)
                        b_ = 4 + i % 2
                        need("pe", bank_free[b_])
                        for kb in range(KB):
                            m = pe.matmul(bank[b_][0:r_, 0:D], hT[:, kb, k * P:k * P + r_], wout[:, kb, :],
                                          start=(kb == 0), stop=(kb == KB - 1))
                        hf["hT"] = t0 = T(m)
                        need("dve", t0)
                        bank_free[b_] = v(vec.tensor_tensor(xr[0:r_, i, :], xr[0:r_, i, :], bank[b_][0:r_, 0:D], ALU.add))
                        t0 = v(vec.tensor_tensor(xr[0:r_, i, :], xr[0:r_, i, :], bout[0:r_, :], ALU.add))
                    need("sp", t0)
                    i0, n_ = ts[0][0], len(ts)
                    if i0 == NT - 1:
                        t_o.append(dma("sp", f"out{ci}", out_tail, xr[0:TAIL, i0, :]))
                    else:
                        t_o.append(dma("sp", f"out{ci}", out_full[:, i0:i0 + n_, :], xr[:, i0:i0 + n_, :]))
                need("sp", *t_o)
                barrier()

    def network():
        with scope() as c:
            if not fast:
                with scope() as c0:
                    make_lists(c0)
                chunk_buf["buf"] = room[:, 0:4 * D].rearrange("p (i f) -> p i f", f=D)
            degrees()
            block_gru()
            block_gcn()
            block_relations()
            block_experts()

    room = A[:].rearrange("p i c -> p (i c)").bitcast(F32)
    for k in engines:
        seen[k] = {}
    ok = nc.values_load(flag[0:1, 0:1], min_val=0, max_val=1)
    at_branch = dict(count)
    slots_at_branch = {n_: s[1] for n_, s in slots.items()}
    with nc.If(ok == 1):
        network()
    with nc.Else():
        count.update(at_branch)
        for n_, s in slots.items():
            s[1] = slots_at_branch.get(n_, 0)
        for k in engines:
            seen[k] = {}
        bank_free[:] = [None] * 8
        scale_tmp.clear()
        fast = False
        network()
    top.close()


_INS = ["x", "src", "dst", "edge_type_8", "L0_gnn_weight", "L0_gnn_w_ih", "L0_gnn_w_hh", "L0_gnn_b_ih",
        "L0_gnn_b_hh", "L1_gnn_W0", "L1_gnn_b0", "L1_gnn_W1", "L1_gnn_b1", "L2_gnn_weight", "L2_gnn_self_weight",
        "L3_gnn_W_in", "L3_gnn_b_in", "L3_gnn_router_W", "L3_gnn_router_b", "L3_gnn_weak_W", "L3_gnn_weak_b",
        "L3_gnn_strong_W1", "L3_gnn_strong_b1", "L3_gnn_strong_W2", "L3_gnn_strong_b2", "L3_gnn_conf_W",
        "L3_gnn_conf_b", "L3_gnn_W_out", "L3_gnn_b_out"]


def kernel(**inputs):
    import concourse.bacc as bacc
    from concourse.bass_utils import run_bass_kernel_spmd

    nc = bacc.Bacc("TRN2", target_bir_lowering=False, num_devices=1)
    arrays, args = {}, []
    for name in _INS:
        a = np.ascontiguousarray(inputs[name])
        arrays["in_" + name] = a
        args.append(nc.dram_tensor("in_" + name, a.shape, dt.from_np(a.dtype), kind="ExternalInput").ap())
    out = nc.dram_tensor("out", arrays["in_x"].shape, F32, kind="ExternalOutput").ap()
    build_program(nc, *args, out)
    r = run_bass_kernel_spmd(nc, [arrays], core_ids=[0])
    return r.results[0]["out"]
```

```python
from contextlib import ExitStack

import numpy as np
import concourse.bass as bass
from concourse import mybir

dt = mybir.dt
F32, F16, BF16, F8 = dt.float32, dt.float16, dt.bfloat16, dt.float8e4
I32, U16, U8 = dt.int32, dt.uint16, dt.uint8
ALU = mybir.AluOpType
ACT = mybir.ActivationFunctionType
AX = mybir.AxisListType

P = 128
BANK = 512
WN = 4
SLOTS = 2
ALIGN = 32
GW = 8
COUNT_MAX = 7
EPS = 1e-5
FIXED = 4096.0


def build_program(nc, x, src, dst, et, g_w, g_ih, g_hh, g_bih, g_bhh, c_w0, c_b0, c_w1, c_b1,
                  r_w, r_self, m_win, m_bin, m_rw, m_rb, m_ww, m_wb, m_w1, m_b1, m_w2, m_b2,
                  m_cw, m_cb, m_wout, m_bout, out):
    N, D = x.shape
    E = src.shape[0]
    NT = -(-N // P)
    NP = NT * P
    TAIL = N - (NT - 1) * P
    NW = -(-N // WN)
    NG = -(-NW // GW)
    NWP = NG * GW
    NC = NWP * WN
    U = SLOTS * GW
    WB = -(-NWP // P)
    WCOL = WN * NT
    SLOTN = SLOTS * P
    STRIP = P // WN // GW
    NREL = r_w.shape[0]
    CH = [(c, min(BANK, N - c)) for c in range(0, N, BANK)]
    EP = 125
    EC = E // EP
    LG = EC // ALIGN
    assert EC % ALIGN == 0 and D == P and NREL == 8
    NLG = E // ALIGN
    TROWS = -(-(NLG + 1) // 64) * 64
    EPAD = TROWS * ALIGN + SLOTN - E

    engines = {"pe": nc.tensor, "dve": nc.vector, "act": nc.scalar, "pool": nc.gpsimd, "sp": nc.sync}
    top = ExitStack()
    done = {k: top.enter_context(nc.semaphore(f"done_{k}")) for k in ("pe", "dve", "act", "pool")}
    count = {k: 0 for k in done}

    def tick(k, inst):
        count[k] += 1
        inst.then_inc(done[k], 1)
        return done[k], count[k]

    seen = {k: {} for k in engines}

    def need(k, *tokens):
        for t in tokens:
            if t is None:
                continue
            if isinstance(t, list):
                need(k, *t)
                continue
            sem, value = t
            if seen[k].get(sem.name, 0) < value:
                engines[k].wait_ge(sem, value)
                seen[k][sem.name] = value

    slots = {}

    def dma(k, name, out_, in_, **kw):
        if name not in slots:
            slots[name] = [top.enter_context(nc.semaphore(f"dma_{name}")), 0]
        s = slots[name]
        engines[k].dma_start(out_, in_, **kw).then_inc(s[0], 16)
        s[1] += 16
        return s[0], s[1]

    def gather(name, out_, table, idx):
        if name not in slots:
            slots[name] = [top.enter_context(nc.semaphore(f"dma_{name}")), 0]
        s = slots[name]
        nc.gpsimd.indirect_dma_start(out=out_, out_offset=None, in_=table,
                                     in_offset=bass.IndirectOffsetOnAxis(ap=idx, axis=0)).then_inc(s[0], 16)
        s[1] += 16
        return s[0], s[1]

    def V(inst):
        return tick("dve", inst)

    def S(inst):
        return tick("act", inst)

    def G(inst):
        return tick("pool", inst)

    def T(inst):
        return tick("pe", inst)

    def scope():
        return ExitStack()

    made = []

    def sbuf(ctx, name, shape, dtype):
        made.append(name)
        return ctx.enter_context(nc.sbuf_tensor(f"{name}_{len(made)}", shape, dtype))

    def barrier():
        nc.all_engine_barrier()

    vec, act, pool, pe, sp = nc.vector, nc.scalar, nc.gpsimd, nc.tensor, nc.sync

    epk = nc.dram_tensor("edge_words", (E + EPAD,), I32).ap()
    last_dram = nc.dram_tensor("last_dst", (NLG,), I32).ap()
    tbl = nc.dram_tensor("slot_table", (TROWS, SLOTN), I32).ap()
    pd = nc.dram_tensor("packed_counts", (NP, NP), I32).ap()
    sd = nc.dram_tensor("packed_sym", (NP, NP), I32).ap()
    deg_row = nc.dram_tensor("deg_row", (N,), F32).ap()
    dinv_row = nc.dram_tensor("dinv_row", (N,), F32).ap()
    invd_row = nc.dram_tensor("invd_row", (N,), F32).ap()
    SUMS = NREL * NP + P
    feat = nc.dram_tensor("features", (NP, D), F32).ap()
    sums = nc.dram_tensor("edge_sums", (SUMS, D), F32).ap()
    degs8 = nc.dram_tensor("type_degrees", (SUMS, D), F32).ap()
    ET = -(-E // P)
    lists = {n: nc.dram_tensor("list_" + n, (ET * P,), I32).ap() for n in ("src", "dst", "to_dst", "to_type_dst", "to_type_src")}
    xpark = nc.dram_tensor("x_parked", (P, NT * D), F32).ap()

    bank = [top.enter_context(nc.psum_tensor(f"bank{i}", [P, BANK], F32)) for i in range(8)]

    A = sbuf(top, "counts", [P, NT, NC], F8)
    ident = sbuf(top, "ident", [P, P], F32)
    ones_bf = sbuf(top, "ones_bf", [P, 1], BF16)
    ones_f = sbuf(top, "ones_f", [P, P], F32)
    zeros_i = sbuf(top, "zeros_i", [1, 4], F32)
    flag = sbuf(top, "flag", [1, 1], I32)
    xn = sbuf(top, "x_nodes", [P, NT, D], F32)

    t_ones = V(vec.memset(ones_f[:], 1.0))
    t_onesb = V(vec.memset(ones_bf[:], 1.0))
    need("pool", t_ones)
    t_ident = G(pool.affine_select(out=ident[:], in_=ones_f[:], compare_op=ALU.is_equal, fill=0.0, base=0,
                                   pattern=[[-1, P]], channel_multiplier=1))

    full = (NT - 1) * P
    t_xz = V(vec.memset(xn[:, NT - 1, :], 0.0))
    need("sp", t_xz)
    t_x = [dma("sp", "x_tail", xn[0:TAIL, NT - 1, :], x[full:N, :])]
    for i0 in range(0, NT - 1, 4):
        t_x.append(dma("sp", f"x_{i0}", xn[:, i0:i0 + 4, :],
                       x[i0 * P:(i0 + 4) * P, :].rearrange("(i p) f -> p i f", p=P)))

    with scope() as c1:
        thr = sbuf(c1, "thr", [P, WB], F32)
        row = sbuf(c1, "row", [P, WB], I32)
        with scope() as c0:
            ew = {n: sbuf(c0, f"e_{n}", [EP, EC], I32) for n in ("src", "dst", "et", "word")}
            pad = sbuf(c0, "pad", [1, EPAD], I32)
            last = sbuf(c0, "last", [EP, LG], I32)
            ld = [dma("sp", "l" + n, ew[n][:], a.rearrange("(p c) -> p c", p=EP))
                  for n, a in (("dst", dst), ("src", src), ("et", et))]
            t_pad = V(vec.memset(pad[:], 2130706432))
            need("dve", ld[0])
            t_last = V(vec.tensor_copy(last[:], ew["dst"][:, ALIGN - 1::ALIGN]))
            need("sp", t_last)
            t_ldr = dma("sp", "last_out", last_dram.rearrange("(p c) -> p c", p=EP), last[:])
            need("dve", t_last, *ld)
            t1 = V(vec.tensor_scalar(ew["dst"][:], ew["dst"][:], 15, None, ALU.logical_shift_left))
            t2 = V(vec.tensor_scalar(ew["et"][:], ew["et"][:], 12, None, ALU.logical_shift_left))
            need("dve", t1, t2)
            t3 = V(vec.tensor_tensor(ew["word"][:], ew["dst"][:], ew["et"][:], ALU.bitwise_or))
            need("dve", t3)
            t4 = V(vec.tensor_tensor(ew["word"][:], ew["word"][:], ew["src"][:], ALU.bitwise_or))
            need("act", t4, t_pad)
            t5 = [dma("act", "word_out", epk[0:E].rearrange("(p c) -> p c", p=EP), ew["word"][:]),
                  dma("act", "pad_out", epk[E:E + EPAD].rearrange("(a n) -> a n", a=1), pad[:])]
            need("act", t5)
            t_tbl = dma("act", "table", tbl, bass.AP(epk.tensor, 0, [[ALIGN, TROWS], [1, SLOTN]]))

            lastb = sbuf(c0, "lastb", [P, NLG], I32)
            lastf = sbuf(c0, "lastf", [P, NLG], F32)
            below = sbuf(c0, "below", [P, NLG], BF16)
            cnt = sbuf(c0, "cnt", [P, WB], F32)
            need("sp", t_ldr)
            t_lb = dma("sp", "last_in", lastb[:], bass.AP(last_dram.tensor, 0, [[0, P], [1, NLG]]))
            t_thr = G(pool.iota(thr[:], pattern=[[WN * P, WB]], base=0, channel_multiplier=WN,
                                allow_small_or_imprecise_dtypes=True))
            need("dve", t_lb, t_thr)
            t = V(vec.tensor_copy(lastf[:], lastb[:]))
            need("dve", t)
            for b in range(WB):
                t = V(vec.tensor_scalar(below[:], lastf[:], thr[:, b:b + 1], None, ALU.is_lt, ALU.add,
                                        accum_out=cnt[:, b:b + 1]))
                need("dve", t)
            t_row = V(vec.tensor_copy(row[:], cnt[:]))
            barrier()

        words = sbuf(c1, "words", [P, WB, SLOTN], I32)
        scal = sbuf(c1, "scal", [P, 3, NG + P // GW, SLOTS, GW], BF16)
        hits = sbuf(c1, "hits", [P, 1], F32)
        with scope() as c0:
            need("pool", t_row, t_tbl)
            t_g = [gather(f"win{b}", words[:, b, :], tbl, row[:, b:b + 1]) for b in range(WB)]
            fld = [sbuf(c0, f"fld{i}", [P, WB, SLOTN], F32) for i in range(3)]
            ti = [sbuf(c0, f"ti{i}", [P, WB, SLOTN], I32) for i in range(2)]
            tf = [sbuf(c0, f"tf{i}", [P, WB, SLOTN], F32) for i in range(3)]
            need("dve", *t_g)

            def v(inst):
                need("dve", V(inst))

            def shift_and(o, i, sh, mask, left=False):
                v(vec.tensor_scalar(o, i, sh, mask, ALU.logical_shift_right, ALU.bitwise_and))

            w_ = words[:]
            shift_and(ti[0][:], w_, 0, P - 1)
            v(vec.tensor_copy(fld[0][:], ti[0][:]))
            v(vec.tensor_scalar(ti[0][:], w_, 15, None, ALU.logical_shift_right))
            v(vec.tensor_copy(tf[0][:], ti[0][:]))
            v(vec.tensor_tensor(tf[0][:], tf[0][:], thr[:, :, None].to_broadcast([P, WB, SLOTN]), ALU.subtract))
            v(vec.tensor_scalar(tf[1][:], tf[0][:], 0.0, float(WN - 1), ALU.max, ALU.min))
            v(vec.tensor_tensor(tf[2][:], tf[0][:], tf[1][:], ALU.is_equal))
            v(vec.tensor_reduce(hits[:], tf[2][:], axis=AX.XY, op=ALU.add))
            v(vec.tensor_scalar(tf[2][:], tf[2][:], -1000.0, 1000.0, ALU.mult, ALU.add))
            shift_and(ti[0][:], w_, 7, 31)
            v(vec.tensor_copy(fld[1][:], ti[0][:]))
            v(vec.scalar_tensor_tensor(fld[1][:], tf[1][:], float(2 * NT), fld[1][:], ALU.mult, ALU.add))
            shift_and(ti[0][:], w_, 14, 1)
            v(vec.tensor_copy(tf[1][:], ti[0][:]))
            v(vec.scalar_tensor_tensor(fld[1][:], tf[1][:], float(NT), fld[1][:], ALU.mult, ALU.add))
            v(vec.tensor_tensor(fld[1][:], fld[1][:], tf[2][:], ALU.add))
            v(vec.tensor_scalar(fld[1][:], fld[1][:], 255.0, None, ALU.min))
            shift_and(ti[0][:], w_, 12, 3)
            v(vec.tensor_scalar(ti[1][:], ti[0][:], float(1 << 25), float(127 << 23), ALU.mult, ALU.add))
            v(vec.tensor_copy(fld[2][:], ti[1][:].bitcast(F32)))
            t_fld = (done["dve"], count["dve"])
            need("pe", t_fld, t_ident)
            free = [None] * 8
            n = 0
            t_sc = None
            for i in range(3):
                for b in range(WB):
                    for j in range(SLOTS):
                        k = n % 8
                        n += 1
                        need("pe", free[k])
                        tt = T(pe.transpose(bank[k][:, 0:P], fld[i][:, b, j * P:(j + 1) * P], ident[:]))
                        g0 = b * (P // GW)
                        o = scal[:, i, g0:g0 + P // GW, j, :]
                        src_ = bank[k][:, 0:P].rearrange("p (g w) -> p g w", w=GW)
                        if n % 2:
                            need("dve", tt)
                            free[k] = V(vec.tensor_copy(o, src_))
                        else:
                            need("act", tt)
                            free[k] = S(act.activation(o, src_, ACT.Copy))
            barrier()

        HC = 2 * WCOL
        cols = sbuf(c1, "cols", [P, HC, U], BF16)
        oh_s = [sbuf(c1, f"oh_s{i}", [P, P, U], BF16) for i in range(2)]
        oh_w = [sbuf(c1, f"oh_w{i}", [P, P, U], BF16) for i in range(2)]
        oh_c = [sbuf(c1, f"oh_c{i}", [P, HC, U], BF16) for i in range(2)]
        strip = [sbuf(c1, f"strip{i}", [P, NT, P], I32) for i in range(2)]
        sqsum = sbuf(c1, "sqsum", [P, NT, GW * WN], F32)
        sq = sbuf(c1, "sq", [P, NT, GW * WN], F32)
        t_am = G(pool.memset(sqsum[:], 0.0))
        t_cols = G(pool.iota(cols[:], pattern=[[1, HC], [0, U]], base=0, channel_multiplier=0,
                             allow_small_or_imprecise_dtypes=True))
        need("dve", t_cols)
        need("pool", t_am)
        AB, HB = (0, 1), (2, 3, 4, 5, 6, 7)
        free = [None] * 8
        hb = 0
        used = [None, None]
        strip_free = [None, None]
        strip_tok = []
        packed_out = []
        for g in range(NG):
            q = g % 2
            sc = [scal[:, i, g].rearrange("p j w -> p (j w)")[:, None, :] for i in range(3)]
            need("dve", used[q])
            V(vec.tensor_tensor(oh_c[q][:], cols[:], sc[1].to_broadcast([P, HC, U]), ALU.is_equal))
            t = V(vec.tensor_tensor(oh_s[q][:], cols[:, 0:P, :], sc[0].to_broadcast([P, P, U]), ALU.is_equal))
            need("dve", t)
            t_oh = V(vec.tensor_tensor(oh_w[q][:], oh_s[q][:], sc[2].to_broadcast([P, P, U]), ALU.mult))
            need("pe", t_oh)
            st = (g // STRIP) % 2
            if g % STRIP == 0:
                need("act", strip_free[st])
                if (g // STRIP) == NT - 1:
                    need("dve", strip_free[st])
                    need("act", V(vec.memset(strip[st][:], 0)))
            a_toks = []
            for w in range(GW):
                ab = AB[w // 4]
                if w % 4 == 0:
                    need("pe", free[ab])
                if w % 2 == 0:
                    hk = HB[hb % 6]
                    hb += 1
                    need("pe", free[hk])
                ao = bank[ab][:, (w % 4) * WCOL:(w % 4 + 1) * WCOL]
                ho = bank[hk][:, (w % 2) * HC:(w % 2 + 1) * HC]
                for j in range(SLOTS):
                    u = j * GW + w
                    for half in range(2):
                        rhs = oh_c[q][:, :, u].rearrange("p (d h s) -> p d h s", h=2, s=NT)[:, :, half, :]
                        t_a = pe.matmul(ao, oh_s[q][:, :, u], rhs, start=(j == 0 and half == 0),
                                        stop=(j == SLOTS - 1 and half == 1))
                    t_h = pe.matmul(ho, oh_w[q][:, :, u], oh_c[q][:, :, u], start=(j == 0), stop=(j == SLOTS - 1))
                if w % 4 == 3:
                    t_pa = T(t_a)
                if w % 2 == 1:
                    t_ph = T(t_h)
                    need("act", t_ph)
                    d0 = (g % STRIP) * GW * WN + (w - 1) * WN
                    o = strip[st][:, :, d0:d0 + 2 * WN].bitcast(U16).rearrange("p s (x h) -> p x h s", h=2)
                    free[hk] = S(act.activation(o, bank[hk][:, 0:2 * HC].rearrange(
                        "p (x h s) -> p x h s", h=2, s=NT), ACT.Copy))
                if w % 4 == 3:
                    need("act", t_pa)
                    d0 = g * GW * WN + (w - 3) * WN
                    free[ab] = S(act.activation(
                        A[:, :, d0:d0 + 4 * WN].rearrange("p s x -> p x s"),
                        bank[ab][:, 0:4 * WCOL].rearrange("p (x s) -> p x s", s=NT), ACT.Copy, saturate=False))
            used[q] = (done["pe"], count["pe"])
            t_a_evac = (done["act"], count["act"])
            need("pool", t_a_evac)
            ag = A[:, :, g * GW * WN:(g + 1) * GW * WN]
            need("pool", G(pool.tensor_tensor(sq[:], ag, ag, ALU.mult)))
            t_am = G(pool.tensor_tensor(sqsum[:], sqsum[:], sq[:], ALU.add))
            need("pool", t_am)
            if g % STRIP == STRIP - 1 or g == NG - 1:
                j = g // STRIP
                need("sp", t_a_evac)
                strip_free[st] = dma("sp", f"strip{st}", pd.rearrange("(i p) n -> p i n", p=P)[:, :, j * P:(j + 1) * P],
                                     strip[st][:])
                packed_out = [strip_free[0], strip_free[1]]

        chk = sbuf(c1, "chk", [P, 2], F32)
        chr_ = sbuf(c1, "chr", [1, 4], F32)
        need("dve", t_am)
        v(vec.tensor_reduce(chk[:, 0:1], sqsum[:], axis=AX.XY, op=ALU.max))
        need("pe", (done["dve"], count["dve"]))
        pe.matmul(bank[7][0:1, 0:1], hits[:], ones_f[:, 0:1], start=True, stop=True)
        t = T(pe.transpose(bank[6][0:1, 0:P], chk[:, 0:1], ident[:]))
        need("dve", t)
        v(vec.tensor_reduce(chr_[:, 0:1], bank[6][0:1, 0:P], axis=AX.X, op=ALU.max))
        v(vec.tensor_scalar(chr_[:, 1:2], chr_[:, 0:1], float((COUNT_MAX + 1) ** 2), None, ALU.is_lt))
        v(vec.tensor_scalar(chr_[:, 2:3], bank[7][0:1, 0:1], float(E), None, ALU.is_equal))
        v(vec.tensor_tensor(flag[:], chr_[:, 1:2], chr_[:, 2:3], ALU.mult))
        need("sp", *packed_out)
        barrier()

    def node_rows(ap):
        full = (NT - 1) * P
        return ap[0:full, :].rearrange("(i p) f -> p i f", p=P), ap[full:N, :]

    bank_free = [None] * 8
    scale_tmp = {}
    fast = True

    def feature_pair(ctx, name, width=D):
        if fast:
            return sbuf(ctx, name, [P, 2, NT, width], F16)
        return sbuf(ctx, name, [P, NT, width], F32)[:]

    def sum_all(nm):
        if not fast:
            scatter_sum(nm, sums, [("src", "to_dst")])

    def now(k):
        return done[k], count[k]

    def v(inst):
        t_ = V(inst)
        need("dve", t_)
        return t_

    def s_(inst):
        t_ = S(inst)
        need("act", t_)
        return t_

    def rows_of(i):
        return P if i < NT - 1 else TAIL

    def tiles_of(ch):
        c, cw = ch
        return [(c // P + k, k) for k in range(-(-cw // P))]

    def layer_norm(hn):
        with scope() as c:
            sq_ = sbuf(c, "ln_sq", [P, NT, D], F32)
            st_ = sbuf(c, "ln_st", [P, 3, NT], F32)
            need("dve", *t_x)
            v(vec.tensor_reduce(st_[:, 0, :], xn[:], axis=AX.X, op=ALU.add))
            v(vec.tensor_scalar(st_[:, 0, :], st_[:, 0, :], 1.0 / D, None, ALU.mult))
            v(vec.tensor_tensor(hn[:], xn[:], st_[:, 0, :, None].to_broadcast([P, NT, D]), ALU.subtract))
            need("act", now("dve"))
            need("dve", S(act.activation(sq_[:], hn[:], ACT.Square)))
            v(vec.tensor_reduce(st_[:, 1, :], sq_[:], axis=AX.X, op=ALU.add))
            v(vec.tensor_scalar(st_[:, 1, :], st_[:, 1, :], 1.0 / D, EPS, ALU.mult, ALU.add))
            need("act", now("dve"))
            need("dve", S(act.activation(st_[:, 2, :], st_[:, 1, :], ACT.Sqrt)))
            v(vec.reciprocal(st_[:, 2, :], st_[:, 2, :]))
            v(vec.tensor_tensor(hn[:], hn[:], st_[:, 2, :, None].to_broadcast([P, NT, D]), ALU.mult))
            v(vec.tensor_scalar(hn[:], hn[:], 0.0, None, ALU.max))
            barrier()

    def split_fixed(h16, hn):
        if not fast:
            return [v(vec.tensor_scalar(h16, hn[:], FIXED, None, ALU.mult))]
        need("act", now("dve"))
        need("dve", S(act.activation(h16[:, 0], hn[:], ACT.Copy, scale=FIXED)))
        return [v(vec.scalar_tensor_tensor(h16[:, 1], hn[:], FIXED, h16[:, 0], ALU.mult, ALU.subtract))]

    def to_feature_rows(ht, hn, width=N):
        toks = []
        for i0 in range(0, NT, 4):
            k = 6 + (i0 // 4) % 2
            need("pe", bank_free[k], now("dve"))
            w_ = 0
            for i in range(i0, min(i0 + 4, NT)):
                r_ = rows_of(i)
                tt = pe.transpose(bank[k][:, w_:w_ + r_], hn[0:r_, i, :], ident[0:r_, 0:r_])
                w_ += r_
            need("act", T(tt))
            bank_free[k] = S(act.activation(ht[:, i0 * P:i0 * P + w_], bank[k][:, 0:w_], ACT.Copy))
            toks.append(bank_free[k])
        return toks[-1]

    def sum_edges(bk, h16, ch, tok, before=None, aside=None):
        if not fast:
            need("pe", *tok.values())
            return load_sums(bk, sums, 0, ch)
        c, cw = ch
        need("pe", bank_free[bk])
        for i in range(NT):
            if before and i in before:
                before[i]()
            need("pe", tok[i])
            if aside is not None and i % 2 == 1 and cw == BANK:
                step(aside)
            for part in range(2):
                m = pe.matmul(bank[bk][:, 0:cw], h16[:, part, i, :], A[:, i, c:c + cw],
                              start=(i == 0 and part == 0), stop=(i == NT - 1 and part == 1))
        return T(m)

    def node_tiles_to_bank(bk, src_, ch):
        need("pe", bank_free[bk])
        for i, k in tiles_of(ch):
            r_ = rows_of(i)
            m = pe.transpose(bank[bk][0:r_, k * P:k * P + P], src_[:, k * P:k * P + r_], ident[:])
        return T(m)

    def chunk_rows(ch):
        ts = tiles_of(ch)
        return rows_of(ts[-1][0]), ts[0][0], len(ts)

    def add_to_x(bk, ch, tok):
        r_, i0, n_ = chunk_rows(ch)
        need("dve", tok)
        o = xn[0:r_, i0:i0 + n_, :]
        bank_free[bk] = V(vec.tensor_tensor(o, o, bank[bk][0:r_, 0:n_ * P].rearrange("p (i f) -> p i f", f=D), ALU.add))
        return bank_free[bk]

    def split_from_bank(bk, h16, ch, tok, scale):
        r_, i0, n_ = chunk_rows(ch)
        s3 = bank[bk][0:r_, 0:n_ * P].rearrange("p (i f) -> p i f", f=D)
        if not fast:
            need("dve", tok)
            bank_free[bk] = v(vec.tensor_scalar(h16[0:r_, i0:i0 + n_, :], s3, scale, None, ALU.mult))
            return [bank_free[bk]]
        hi, lo = (h16[0:r_, part, i0:i0 + n_, :] for part in range(2))
        need("act", tok)
        t1_ = S(act.activation(hi, s3, ACT.Copy, scale=scale))
        need("dve", tok, t1_)
        bank_free[bk] = V(vec.scalar_tensor_tensor(lo, s3, scale, hi, ALU.mult, ALU.subtract))
        return [t1_, bank_free[bk]]

    def power_scale(m, sc_, inv_, work):
        v(vec.tensor_scalar(work, m, 1e-15, None, ALU.max))
        v(vec.tensor_scalar(work.bitcast(I32), work.bitcast(I32), 0x7F800000, None, ALU.bitwise_and))
        v(vec.tensor_scalar(sc_.bitcast(I32), work.bitcast(I32), -1.0, float((127 + 14 + 127) << 23), ALU.mult, ALU.add))
        v(vec.tensor_scalar(inv_.bitcast(I32), work.bitcast(I32), float(14 << 23), None, ALU.subtract))

    def make_lists(ctx):
        e_ = {k: sbuf(ctx, "l_" + k, [EP, EC], I32) for k in ("src", "dst", "et", "rd", "rs")}
        padc = sbuf(ctx, "l_pad", [1, 2, ET * P - E], I32)
        v(vec.memset(padc[:, 0, :], 0))
        v(vec.memset(padc[:, 1, :], NREL * NP))
        need("dve", *[dma("sp", "l_in_" + k, e_[k][:], a.rearrange("(p c) -> p c", p=EP))
                      for k, a in (("src", src), ("dst", dst), ("et", et))])
        for o, k in (("rd", "dst"), ("rs", "src")):
            v(vec.scalar_tensor_tensor(e_[o][:], e_["et"][:], float(NP), e_[k][:], ALU.mult, ALU.add))
        need("sp", now("dve"))
        out_ = []
        for name, k, pd_ in (("src", "src", 0), ("dst", "dst", 0), ("to_dst", "dst", 1),
                             ("to_type_dst", "rd", 1), ("to_type_src", "rs", 1)):
            out_.append(dma("sp", "lo_" + name, lists[name][0:E].rearrange("(p c) -> p c", p=EP), e_[k][:]))
            out_.append(dma("sp", "lp_" + name, lists[name][E:ET * P].rearrange("(a n) -> a n", a=1), padc[:, pd_, :]))
        need("sp", *out_)
        barrier()

    loop_sems = []

    def scatter_sum(nm, target, passes):
        if not loop_sems:
            loop_sems.extend(top.enter_context(nc.semaphore("loop_" + k)) for k in ("dve", "pe", "feat", "sum", "put"))
        s_dve, s_pe, s_feat, s_sum, s_put = loop_sems
        with scope() as c:
            at = [4 * D]

            def take(width, dtype=F32):
                at[0] += width
                r = room[:, at[0] - width:at[0]]
                return r if dtype is F32 else r.bitcast(dtype)

            zero = take(NT * D)
            frm, to = take(ET, I32), take(ET, I32)
            low = take(P)
            spare = take(1)
            gi, si, wi = (take(1, I32) for _ in range(3))
            sf, rep = take(1), take(1)
            wide_, eq, before, msg, cur, new = (take(P) for _ in range(6))
            if nm is None:
                v(vec.memset(zero[:], 1.0))
                need("sp", now("dve"))
                t0 = dma("sp", "z_feat", feat.rearrange("(i p) f -> p i f", p=P), zero[:].rearrange("p (i f) -> p i f", f=D))
            else:
                need("sp", now("dve"), now("act"))
                t0 = dma("sp", "z_feat", feat.rearrange("(i p) f -> p i f", p=P), nm)
            need("dve", t0)
            need("sp", t0)
            v(vec.memset(zero[:], 0.0))
            need("sp", now("dve"))
            for r0 in range(0, NREL * NP, NP):
                need("sp", dma("sp", "z_zero", target[r0:r0 + NP, :].rearrange("(i p) f -> p i f", p=P),
                               zero[:].rearrange("p (i f) -> p i f", f=D)))
            need("sp", dma("sp", "z_zero", target[NREL * NP:SUMS, :], zero[:, 0:D]))
            need("pool", G(pool.affine_select(out=low[:], in_=ones_f[:], compare_op=ALU.is_gt, fill=0.0, base=0,
                                              pattern=[[-1, P]], channel_multiplier=1)))
            need("pool", G(pool.iota(spare[:], pattern=[[0, 1]], base=NREL * NP, channel_multiplier=1,
                                     allow_small_or_imprecise_dtypes=True)))
            for from_, to_ in passes:
                barrier()
                t0 = [dma("sp", "z_from", frm[:], lists[from_].rearrange("(p t) -> p t", p=P)),
                      dma("sp", "z_to", to[:], lists[to_].rearrange("(p t) -> p t", p=P))]
                need("sp", *t0)
                barrier()
                with nc.Fori(0, ET) as t_:
                    vec.tensor_copy(gi[:], frm[:, bass.ds(t_, 1)]).then_inc(s_dve, 1)
                    vec.tensor_copy(si[:], to[:, bass.ds(t_, 1)]).then_inc(s_dve, 1)
                    vec.wait_ge(s_dve, 2)
                    vec.tensor_copy(sf[:], si[:]).then_inc(s_dve, 1)
                    vec.wait_ge(s_dve, 3)
                    vec.tensor_copy(wide_[:], sf[:, 0:1].to_broadcast([P, P])).then_inc(s_dve, 1)
                    pool.wait_ge(s_dve, 2)
                    pool.indirect_dma_start(out=msg[:], out_offset=None, in_=feat,
                                            in_offset=bass.IndirectOffsetOnAxis(ap=gi[:], axis=0)).then_inc(s_feat, 16)
                    pool.indirect_dma_start(out=cur[:], out_offset=None, in_=target,
                                            in_offset=bass.IndirectOffsetOnAxis(ap=si[:], axis=0)).then_inc(s_sum, 16)
                    pe.wait_ge(s_dve, 4)
                    pe.matmul(bank[0][:, 0:P], wide_[:], ident[:], start=True, stop=True).then_inc(s_pe, 1)
                    vec.wait_ge(s_pe, 1)
                    vec.tensor_scalar(eq[:], bank[0][:, 0:P], sf[:, 0:1], None, ALU.is_equal).then_inc(s_dve, 1)
                    vec.wait_ge(s_dve, 5)
                    vec.tensor_tensor(before[:], eq[:], low[:], ALU.mult).then_inc(s_dve, 1)
                    vec.wait_ge(s_dve, 6)
                    vec.tensor_reduce(rep[:], before[:], axis=AX.X, op=ALU.max).then_inc(s_dve, 1)
                    vec.wait_ge(s_dve, 7)
                    vec.scalar_tensor_tensor(before[:, 0:1], spare[:], sf[:, 0:1], rep[:], ALU.subtract, ALU.mult).then_inc(s_dve, 1)
                    vec.wait_ge(s_dve, 8)
                    vec.tensor_tensor(wi[:], before[:, 0:1], sf[:], ALU.add).then_inc(s_dve, 1)
                    pe.wait_ge(s_dve, 9)
                    pe.wait_ge(s_feat, 16)
                    pe.matmul(bank[1][:, 0:P], eq[:], msg[:], start=True, stop=True).then_inc(s_pe, 1)
                    vec.wait_ge(s_pe, 2)
                    vec.wait_ge(s_sum, 16)
                    vec.tensor_tensor(new[:], bank[1][:, 0:P], cur[:], ALU.add).then_inc(s_dve, 1)
                    pool.wait_ge(s_dve, 10)
                    pool.indirect_dma_start(out=target, out_offset=bass.IndirectOffsetOnAxis(ap=wi[:], axis=0),
                                            in_=new[:], in_offset=None).then_inc(s_put, 16)
                    pool.wait_ge(s_put, 16)
                    pool.wait_ge(s_feat, 16)
                    pool.wait_ge(s_sum, 16)
                    barrier()
                    pool.dma_reset(range(s_feat.num, s_put.num + 1))
                    for s in loop_sems:
                        pool.sem_clear(s)
                    barrier()
            barrier()

    chunk_buf = {}

    def load_sums(bk, table, r0, ch, at_col=0):
        buf_ = chunk_buf["buf"]
        need("sp", chunk_buf.get("free"))
        R_, i0, n_ = chunk_rows(ch)
        a = r0 + i0 * P
        if n_ > 1:
            t0 = dma("sp", "z_chunk", buf_[:, 0:n_, :], table[a:a + n_ * P, :].rearrange("(i p) f -> p i f", p=P))
        else:
            t0 = dma("sp", "z_chunk", buf_[0:R_, 0, :], table[a:a + R_, :])
        need("pe", t0, bank_free[bk])
        for i, k in tiles_of(ch):
            r_ = rows_of(i)
            m = pe.transpose(bank[bk][:, at_col + k * P:at_col + k * P + r_], buf_[0:r_, k, :], ident[0:r_, 0:r_])
        chunk_buf["free"] = T(m)
        return chunk_buf["free"]

    def degrees():
        with scope() as c1:
            nd = sbuf(c1, "nd", [EP, 3, N // EP], F32)
            if fast:
                degs = sbuf(c1, "degs", [1, N], F32)
                for ci, (c, cw) in enumerate(CH):
                    need("pe", bank_free[ci % 8])
                    for i in range(NT):
                        m = pe.matmul(bank[ci % 8][0:1, 0:cw], ones_bf[:], A[:, i, c:c + cw], start=(i == 0), stop=(i == NT - 1))
                    need("dve", T(m))
                    t = bank_free[ci % 8] = V(vec.tensor_copy(degs[:, c:c + cw], bank[ci % 8][0:1, 0:cw]))
                need("sp", t)
                t = dma("sp", "deg_out", deg_row.rearrange("(a n) -> a n", a=1), degs[:])
            else:
                scatter_sum(None, sums, [("src", "to_dst")])
                t = dma("sp", "deg_out", deg_row.rearrange("(p c) -> p c", p=EP),
                        bass.AP(sums.tensor, 0, [[N // EP * D, EP], [D, N // EP]]), allow_slow_non_contiguous=True)
            need("sp", t)
            t = dma("sp", "deg_in", nd[:, 0, :], deg_row.rearrange("(p c) -> p c", p=EP))
            need("dve", t)
            v(vec.tensor_scalar(nd[:, 1, :], nd[:, 0, :], 1.0, None, ALU.add))
            need("act", now("dve"))
            need("dve", S(act.activation(nd[:, 1, :], nd[:, 1, :], ACT.Sqrt)))
            v(vec.tensor_scalar(nd[:, 2, :], nd[:, 0, :], 1.0, None, ALU.max))
            v(vec.reciprocal(nd[:, 1:3, :], nd[:, 1:3, :]))
            need("sp", now("dve"))
            need("sp", dma("sp", "dinv_out", dinv_row.rearrange("(p c) -> p c", p=EP), nd[:, 1, :]),
                 dma("sp", "invd_out", invd_row.rearrange("(p c) -> p c", p=EP), nd[:, 2, :]))
            barrier()

    def symmetric_steps(ctx):
        cuts = [(0, 7), (7, 6), (13, 6), (19, 6)]
        pieces = [(j, i0, n_) for j in range(NT) for i0, n_ in cuts]
        R = 3
        rs = [sbuf(ctx, f"sym_rows{r}", [P, 7 * P], I32) for r in range(R)]
        cs = [sbuf(ctx, f"sym_cols{r}", [P, 7, P], I32) for r in range(R)]
        pdv = pd.rearrange("(i p) n -> p i n", p=P)
        sdv = sd.rearrange("(i p) n -> p i n", p=P)
        rows_free, cols_free, loaded = [None] * R, [None] * R, {}

        def load(n):
            if n >= len(pieces):
                return
            j, i0, n_ = pieces[n]
            r = n % R
            need("sp", rows_free[r])
            t_r = dma("sp", f"sym_r{r}", rs[r][:, 0:n_ * P], pd[j * P:(j + 1) * P, i0 * P:(i0 + n_) * P])
            need("sp", cols_free[r])
            loaded[n] = t_r, dma("sp", f"sym_c{r}", cs[r][:, 0:n_, :], pdv[:, i0:i0 + n_, j * P:(j + 1) * P])

        load(0)
        load(1)
        for n, (j, i0, n_) in enumerate(pieces):
            r = n % R
            load(n + 2)
            yield
            t_r, t_c = loaded.pop(n)
            need("pe", t_r)
            need("dve", t_c)
            for g0 in range(0, n_, 4):
                k = 6 + (g0 // 4) % 2
                g = min(4, n_ - g0)
                need("pe", bank_free[k])
                for i in range(g):
                    m = pe.transpose(bank[k][:, i * P:(i + 1) * P], rs[r][:, (g0 + i) * P:(g0 + i + 1) * P].bitcast(F32), ident[:])
                t_t = rows_free[r] = T(m)
                need("dve", t_t)
                o = cs[r][:, g0:g0 + g, :].rearrange("p i n -> p (i n)").bitcast(U16)
                bank_free[k] = V(vec.tensor_tensor(o, o, bank[k][:, 0:g * P].bitcast(U16), ALU.add))
                if g0 + 4 < n_:
                    yield
            need("sp", bank_free[k], bank_free[6 + (k + 1) % 2])
            cols_free[r] = dma("sp", f"sym_o{r}", sdv[:, i0:i0 + n_, j * P:(j + 1) * P], cs[r][:, 0:n_, :])
        scale_tmp["sym"] = [t for t in cols_free]
        yield

    def step(bg):
        next(bg, None)

    def block_gru():
        with scope() as c:
            hn = sbuf(c, "g_hn", [P, NT, D], F32)
            layer_norm(hn)
            NL = g_w.shape[0]
            h16 = [feature_pair(c, f"g_h16{i}") for i in range(2)]
            ht = sbuf(c, "g_ht", [P, N], F32)
            wl = sbuf(c, "g_wl", [P, NL, D], F32)
            wt = {}
            raw = sbuf(c, "g_raw", [P, 3, D], F32)
            bb = sbuf(c, "g_b", [P, 3, 3], F32)
            t_wl = dma("act", "g_wl", wl[:], g_w.rearrange("l i o -> i l o"))
            t_b = [dma("act", "g_bi", bb[:, 0, :], g_bih.rearrange("(b o) -> o b", o=P), allow_slow_non_contiguous=True),
                   dma("act", "g_bh", bb[:, 1, :], g_bhh.rearrange("(b o) -> o b", o=P), allow_slow_non_contiguous=True)]
            t_tr = None
            for n_, a in (("ih", g_ih), ("hh", g_hh)):
                wt[n_] = sbuf(c, "g_w" + n_, [P, 3, D], F32)
                need("act", t_tr)
                t_raw = dma("act", "g_raw", raw[:], a.rearrange("(b o) i -> o b i", o=P))
                need("pe", t_raw, bank_free[7])
                for b in range(3):
                    m = pe.transpose(bank[7][:, b * P:(b + 1) * P], raw[:, b, :], ident[:])
                t_tr = T(m)
                need("act", t_tr)
                bank_free[7] = t_w = S(act.activation(wt[n_][:], bank[7][:, 0:3 * P].rearrange("p (b o) -> p b o", b=3), ACT.Copy))
            need("dve", *t_b)
            t_bb = v(vec.tensor_tensor(bb[:, 2, :], bb[:, 0, :], bb[:, 1, :], ALU.add))
            v(vec.tensor_tensor(xn[:], xn[:], hn[:], ALU.add))
            v(vec.memset(h16[1][:, :, NT - 1, :] if fast else h16[1][:, NT - 1, :], 0.0))
            t_h = split_fixed(h16[0], hn)
            t_ht = to_feature_rows(ht, hn)
            need("pe", t_wl, t_w, t_ht)
            need("act", t_bb)
            need("dve", t_ht)
            buf = {n_: [sbuf(c, f"g_{n_}{i}", [P, BANK], F32) for i in range(2)] for n_ in ("ag", "m", "r", "z", "t", "n")}
            bg = symmetric_steps(c) if fast else iter(())
            BR, BZ, BI, BH, BM, BT = 2, 3, 4, 5, 6, 7
            last_use = {}

            def gate(ci, l, t_agg):
                c_, cw = CH[ci]
                q = ci % 2
                ag, m_, r_, z_, t_, n_ = (buf[b][q][:, 0:cw] for b in ("ag", "m", "r", "z", "t", "n"))
                h_ = ht[:, c_:c_ + cw]
                need("act", t_agg, last_use.get(("pe", q)))
                bank_free[q] = t0 = S(act.activation(ag, bank[q][:, 0:cw], ACT.Copy, scale=1.0 / FIXED))
                need("pe", t0, bank_free[BM])
                t0 = T(pe.matmul(bank[BM][:, 0:cw], wl[:, l, :], ag, start=True, stop=True))
                need("act", t0)
                bank_free[BM] = t_m = S(act.activation(m_, bank[BM][:, 0:cw], ACT.Copy))
                need("pe", bank_free[BR], bank_free[BZ], bank_free[BI], bank_free[BH])
                pe.matmul(bank[BR][:, 0:cw], wt["hh"][:, 0, :], h_, start=True, stop=False)
                pe.matmul(bank[BZ][:, 0:cw], wt["hh"][:, 1, :], h_, start=True, stop=False)
                t_hh = T(pe.matmul(bank[BH][:, 0:cw], wt["hh"][:, 2, :], h_, start=True, stop=True))
                need("pe", t_m)
                t_r = T(pe.matmul(bank[BR][:, 0:cw], wt["ih"][:, 0, :], m_, start=False, stop=True))
                t_z = T(pe.matmul(bank[BZ][:, 0:cw], wt["ih"][:, 1, :], m_, start=False, stop=True))
                t_i = T(pe.matmul(bank[BI][:, 0:cw], wt["ih"][:, 2, :], m_, start=True, stop=True))
                last_use[("pe", q)] = t_i
                need("act", t_r, last_use.get(("dve", q)))
                bank_free[BR] = t0 = S(act.activation(r_, bank[BR][:, 0:cw], ACT.Sigmoid, bias=bb[:, 2, 0:1]))
                need("act", t_z)
                bank_free[BZ] = t_zz = S(act.activation(z_, bank[BZ][:, 0:cw], ACT.Sigmoid, bias=bb[:, 2, 1:2]))
                need("dve", t0, t_hh)
                bank_free[BH] = v(vec.scalar_tensor_tensor(t_, bank[BH][:, 0:cw], bb[:, 1, 2:3], r_, ALU.add, ALU.mult))
                need("dve", t_i)
                bank_free[BI] = t0 = v(vec.tensor_tensor(t_, t_, bank[BI][:, 0:cw], ALU.add))
                need("act", t0)
                t0 = S(act.activation(n_, t_, ACT.Tanh, bias=bb[:, 0, 2:3]))
                need("dve", t0)
                v(vec.tensor_tensor(t_, h_, n_, ALU.subtract))
                need("dve", t_zz)
                v(vec.tensor_tensor(t_, t_, z_, ALU.mult))
                last_use[("dve", q)] = t0 = v(vec.tensor_tensor(h_, t_, n_, ALU.add))
                return t0

            def finish(ci, l, t_new, toks):
                need("pe", t_new)
                c_, cw = CH[ci]
                t0 = node_tiles_to_bank(BT, ht[:, c_:c_ + cw], CH[ci])
                if l == NL - 1:
                    add_to_x(BT, CH[ci], t0)
                else:
                    t0 = split_from_bank(BT, h16[(l + 1) % 2], CH[ci], t0, FIXED)
                    toks.update({i: t0 for i, _ in tiles_of(CH[ci])})

            tok = {i: t_h for i in range(NT)}
            LC = len(CH) - 1
            for l in range(NL):
                toks = {}
                new = {}
                cur, nxt = h16[l % 2], h16[(l + 1) % 2]
                if l == 0 or not fast:
                    sum_all(cur)
                    t_agg = {0: sum_edges(0, cur, CH[0], tok, aside=bg)}
                for ci in range(len(CH)):
                    if ci < LC:
                        t_agg[ci + 1] = sum_edges((ci + 1) % 2, cur, CH[ci + 1], tok, aside=bg)
                    new[ci] = gate(ci, l, t_agg[ci])
                    if 0 < ci < LC:
                        finish(ci - 1, l, new[ci - 1], toks)
                    step(bg)
                last_two = [lambda c=c: finish(c, l, new[c], toks) for c in (LC - 1, LC)]
                if fast and l < NL - 1:
                    t_agg = {0: sum_edges(0, nxt, CH[0], toks, aside=bg, before={
                        tiles_of(CH[LC - 1])[0][0]: last_two[0], tiles_of(CH[LC])[0][0]: last_two[1]})}
                else:
                    last_two[0]()
                    last_two[1]()
                tok = toks
            for _ in bg:
                pass
            barrier()

    def block_gcn():
        with scope() as c:
            hn = sbuf(c, "c_hn", [P, NT, D], F32)
            layer_norm(hn)
            h16 = feature_pair(c, "c_h16")
            yt = sbuf(c, "c_yt", [P, N], F32)
            dinv = sbuf(c, "c_dinv", [P, N], F32)
            w01 = [sbuf(c, f"c_w{i}", [P, D], F32) for i in range(2)]
            b01 = sbuf(c, "c_b", [P, 2], F32)
            mx = sbuf(c, "c_mx", [P, len(CH)], F32)
            sc = sbuf(c, "c_sc", [P, 4], F32)
            buf = {n_: [sbuf(c, f"c_{n_}{i}", [P, BANK], F32) for i in range(2)] for n_ in ("ag", "t", "o")}
            ld = [dma("sp", "c_w0", w01[0][:], c_w0), dma("sp", "c_w1", w01[1][:], c_w1),
                  dma("act", "c_b0", b01[:, 0:1], c_b0.rearrange("(p a) -> p a", a=1)),
                  dma("act", "c_b1", b01[:, 1:2], c_b1.rearrange("(p a) -> p a", a=1)),
                  dma("sp", "c_dinv", dinv[:], bass.AP(dinv_row.tensor, 0, [[0, P], [1, N]]))]
            t_h = split_fixed(h16, hn)
            for k in ("pe", "act", "dve"):
                need(k, *ld)
            use = {}
            sum_all(h16)
            tok = {i: t_h for i in range(NT)}
            t_agg = {0: sum_edges(0, h16, CH[0], tok)}
            for ci, (c_, cw) in enumerate(CH):
                if ci + 1 < len(CH):
                    t_agg[ci + 1] = sum_edges((ci + 1) % 2, h16, CH[ci + 1], tok)
                q = ci % 2
                ag, t_ = buf["ag"][q][:, 0:cw], buf["t"][q][:, 0:cw]
                y_ = yt[:, c_:c_ + cw]
                need("act", t_agg[ci], use.get(("ag", q)), use.get(("t", q)))
                bank_free[q] = t0 = S(act.activation(ag, bank[q][:, 0:cw], ACT.Copy, scale=1.0 / FIXED))
                need("pe", t0, bank_free[2 + q])
                use[("ag", q)] = t0 = T(pe.matmul(bank[2 + q][:, 0:cw], w01[0][:], ag, start=True, stop=True))
                need("act", t0)
                bank_free[2 + q] = t0 = S(act.activation(t_, bank[2 + q][:, 0:cw], ACT.Identity, bias=b01[:, 0:1]))
                need("dve", t0)
                use[("t", q)] = v(vec.tensor_tensor(y_, t_, dinv[:, c_:c_ + cw], ALU.mult))
                v(vec.tensor_reduce(mx[:, ci:ci + 1], y_, axis=AX.X, op=ALU.max, apply_absolute_value=True))
            v(vec.tensor_reduce(sc[:, 0:1], mx[:], axis=AX.X, op=ALU.max))
            power_scale(sc[:, 0:1], sc[:, 1:2], sc[:, 2:3], sc[:, 3:4])
            t_h = [(done["pe"], count["pe"])]
            toks = {}
            for ci, (c_, cw) in enumerate(CH):
                q = ci % 2
                t_ = buf["t"][q][:, 0:cw]
                need("dve", use.get(("tr", q)))
                t0 = v(vec.tensor_scalar(t_, yt[:, c_:c_ + cw], sc[:, 1:2], None, ALU.mult))
                need("pe", t0)
                t0 = use[("tr", q)] = node_tiles_to_bank(6 + q, t_, CH[ci])
                need("act", t_h)
                t0 = split_from_bank(6 + q, h16, CH[ci], t0, 1.0)
                toks.update({i: t0 for i, _ in tiles_of(CH[ci])})
            sum_all(h16)
            t_agg = {0: sum_edges(0, h16, CH[0], toks)}
            for ci, (c_, cw) in enumerate(CH):
                if ci + 1 < len(CH):
                    t_agg[ci + 1] = sum_edges((ci + 1) % 2, h16, CH[ci + 1], toks)
                q = ci % 2
                ag, o_ = buf["ag"][q][:, 0:cw], buf["o"][q][:, 0:cw]
                need("dve", t_agg[ci], use.get(("ag", q)))
                bank_free[q] = v(vec.scalar_tensor_tensor(ag, bank[q][:, 0:cw], sc[:, 2:3], yt[:, c_:c_ + cw],
                                                          ALU.mult, ALU.add))
                t0 = v(vec.tensor_tensor(ag, ag, dinv[:, c_:c_ + cw], ALU.mult))
                need("pe", t0, bank_free[2 + q])
                use[("ag", q)] = t0 = T(pe.matmul(bank[2 + q][:, 0:cw], w01[1][:], ag, start=True, stop=True))
                need("act", t0, use.get(("o", q)))
                bank_free[2 + q] = t0 = S(act.activation(o_, bank[2 + q][:, 0:cw], ACT.Identity, bias=b01[:, 1:2]))
                need("pe", t0)
                use[("o", q)] = t0 = node_tiles_to_bank(6 + q, o_, CH[ci])
                add_to_x(6 + q, CH[ci], t0)
            barrier()

    def block_relations():
        PT = 5
        RW = BANK // 2
        WRING, RING = 4, 3
        ACT_PIECES = (3 * PT,)
        CR = [(c, min(RW, N - c)) for c in range(0, N, RW)]
        with scope() as c:
            hn = sbuf(c, "r_hn", [P, NT, D], F32)
            layer_norm(hn)
            h16 = feature_pair(c, "r_h16")
            ht = sbuf(c, "r_ht", [P, N], F32)
            wr = sbuf(c, "r_w", [P, NREL, D], F32)
            ws = sbuf(c, "r_ws", [P, D], F32)
            wd = [sbuf(c, f"r_wd{i}", [P, PT, RW], I32) for i in range(WRING)]
            f8 = [sbuf(c, f"r_f8{i}", [P, PT, 4 * RW], F8) for i in range(RING)]
            acc = [sbuf(c, f"r_acc{i}", [P, 2, RW], I32) for i in range(2)]
            accb = sbuf(c, "r_accb", [P, 2, 4 * RW], BF16)
            dg = sbuf(c, "r_dg", [P, 2, 4], F32)
            ags = sbuf(c, "r_ags", [P, 4, RW], F32)
            ld = [dma("sp", "r_wr", wr[:], r_w.rearrange("r i o -> i r o")), dma("sp", "r_ws", ws[:], r_self)]
            t_h = split_fixed(h16, hn)
            t_ht = to_feature_rows(ht, hn)
            need("pe", t_h, t_ht, t_onesb, now("dve"), *ld)
            if not fast:
                both = [("src", "to_type_dst"), ("dst", "to_type_src")]
                scatter_sum(None, degs8, both)
                scatter_sum(h16, sums, both)
            sdv = sd.rearrange("(i p) n -> p i n", p=P)
            BD, BW, BS = 4, (5, 6), 7
            use = {}
            need("sp", *scale_tmp.get("sym", ()))

            def finish_unit(ch, h, t_mm, t_acc, pair, q):
                c_, cw = ch
                ts = tiles_of(ch)
                if fast:
                    need("act", t_mm, use.get("ags"))
                    for b in range(2):
                        bank_free[pair[b]] = t_ags = S(act.activation(
                            ags[:, 2 * b:2 * b + 2, 0:cw],
                            bank[pair[b]][:, 0:2 * cw].rearrange("p (k n) -> p k n", k=2), ACT.Copy, scale=1.0 / FIXED))
                    need("dve", t_acc, use.get("accb"))
                    use[("acc", q)] = t0 = v(vec.tensor_copy(accb[:, :, 0:4 * cw], acc[q][:, :, 0:cw].bitcast(U8)))
                    yield
                    need("pe", t0, bank_free[BD])
                    for i, t in ts:
                        r_ = rows_of(i)
                        for k in range(4):
                            for g_ in range(2):
                                m = pe.matmul(bank[BD][0:r_, 4 * t + k:4 * t + k + 1],
                                              accb[:, g_, 0:4 * cw].rearrange("p (n k) -> p n k", k=4)[:, t * P:t * P + r_, k],
                                              ones_bf[:, 0:1], start=(g_ == 0), stop=(g_ == 1))
                    use["accb"] = t0 = T(m)
                    need("dve", t0, use.get("dg"))
                    r_, _, n_ = chunk_rows(ch)
                    bank_free[BD] = v(vec.tensor_scalar(dg[0:r_, 0:n_, :], bank[BD][0:r_, 0:4 * n_].rearrange(
                        "p (t k) -> p t k", k=4), 1.0, None, ALU.max))
                else:
                    need("act", use.get("ags"))
                    for k in range(4):
                        t0 = load_sums(pair[k // 2], sums, (2 * k + h) * NP, ch, at_col=(k % 2) * cw)
                        need("act", t0)
                        bank_free[pair[k // 2]] = t_ags = S(act.activation(
                            ags[:, k, 0:cw], bank[pair[k // 2]][:, (k % 2) * cw:(k % 2 + 1) * cw], ACT.Copy, scale=1.0 / FIXED))
                    need("sp", use.get("dg"))
                    for i, t in ts:
                        r_ = rows_of(i)
                        for k in range(4):
                            row_ = (2 * k + h) * NP + i * P
                            need("dve", dma("sp", "r_dg", dg[0:r_, t, k:k + 1], degs8[row_:row_ + r_, 0:1],
                                            allow_slow_non_contiguous=True))
                            need("sp", (slots["r_dg"][0], slots["r_dg"][1]))
                    r_, _, n_ = chunk_rows(ch)
                    v(vec.tensor_scalar(dg[0:r_, 0:n_, :], dg[0:r_, 0:n_, :], 1.0, None, ALU.max))
                v(vec.reciprocal(dg[0:r_, 0:n_, :], dg[0:r_, 0:n_, :]))
                yield
                need("pe", t_ags)
                for i, t in ts:
                    r_ = rows_of(i)
                    b_ = BW[t]
                    need("pe", bank_free[b_])
                    for k in range(4):
                        m = pe.matmul(bank[b_][0:r_, k * D:(k + 1) * D], ags[:, k, t * P:t * P + r_], wr[:, 2 * k + h, :],
                                      start=True, stop=True)
                    use["ags"] = t0 = T(m)
                    need("dve", t0)
                    for k in range(4):
                        use["dg"] = bank_free[b_] = v(vec.scalar_tensor_tensor(
                            xn[0:r_, i, :], bank[b_][0:r_, k * D:(k + 1) * D], dg[0:r_, t, k:k + 1], xn[0:r_, i, :],
                            ALU.mult, ALU.add))
                    yield
                if h == 0:
                    need("pe", bank_free[BS])
                    for i, t in ts:
                        r_ = rows_of(i)
                        m = pe.matmul(bank[BS][0:r_, t * D:(t + 1) * D], ht[:, c_ + t * P:c_ + t * P + r_], ws[:],
                                      start=True, stop=True)
                    t0 = T(m)
                    need("dve", t0)
                    for i, t in ts:
                        r_ = rows_of(i)
                        bank_free[BS] = v(vec.tensor_tensor(xn[0:r_, i, :], xn[0:r_, i, :], bank[BS][0:r_, t * D:(t + 1) * D], ALU.add))
                yield

            tail = iter(())
            units = [(ch, h) for ch in CR for h in range(2)]
            pieces = [(u, p0) for u in range(len(units) if fast else 0) for p0 in range(0, NT, PT)]
            ready, t_acc = {}, {}

            def fetch(n):
                if n < len(pieces):
                    u, p0 = pieces[n]
                    c_, cw = units[u][0]
                    q = n % WRING
                    need("sp", *use.get(("wd", q), ()))
                    ready[("wd", n)] = dma("sp", f"r_wd{q}", wd[q][:, :, 0:cw], sdv[:, p0:p0 + PT, c_:c_ + cw])

            def spread(n):
                if n >= len(pieces):
                    return
                u, p0 = pieces[n]
                (c_, cw), h = units[u]
                q, r, qa = n % WRING, n % RING, u % 2
                if p0 == 0:
                    need("pool", use.get(("acc", qa)))
                    need("pool", G(pool.memset(acc[qa][:], 0)))
                need("dve", ready.pop(("wd", n)))
                t0 = v(vec.tensor_scalar(wd[q][:, :, 0:cw], wd[q][:, :, 0:cw], 4 * h, 0x0F0F0F0F,
                                         ALU.logical_shift_right, ALU.bitwise_and))
                bytes_ = wd[q][:, :, 0:cw].bitcast(U8)
                if p0 in ACT_PIECES:
                    need("act", t0, use.get(("f8", r)))
                    t1_ = S(act.activation(f8[r][:, :, 0:4 * cw], bytes_, ACT.Copy, saturate=False))
                else:
                    need("dve", use.get(("f8", r)))
                    t1_ = V(vec.tensor_copy(f8[r][:, :, 0:4 * cw], bytes_, saturate=False))
                need("pool", t0)
                for i in range(PT):
                    g_ = 0 if p0 + i < 13 else 1
                    t_acc[u] = G(pool.tensor_tensor(acc[qa][:, g_, 0:cw], acc[qa][:, g_, 0:cw], wd[q][:, i, 0:cw], ALU.add))
                    need("pool", t_acc[u])
                use[("wd", q)] = [t_acc[u], t1_]
                ready[("f8", n)] = t1_

            if not fast:
                for ch, h in units:
                    for _ in finish_unit(ch, h, None, None, (0, 1), 0):
                        pass
            for n in range(3):
                fetch(n)
            spread(0)
            spread(1)
            for n, (u, p0) in enumerate(pieces):
                (c_, cw), h = units[u]
                pair = (0, 1) if u % 2 == 0 else (2, 3)
                r = n % RING
                fetch(n + 3)
                need("pe", bank_free[pair[0]], bank_free[pair[1]], ready.pop(("f8", n)))
                for i in range(PT):
                    f_ = f8[r][:, i, 0:4 * cw].rearrange("p (n k) -> p k n", k=4)
                    for part in range(2):
                        for b in range(2):
                            m = pe.matmul(bank[pair[b]][:, 0:2 * cw], h16[:, part, p0 + i, :], f_[:, 2 * b:2 * b + 2, :],
                                          start=(p0 + i == 0 and part == 0),
                                          stop=(p0 + i == NT - 1 and part == 1))
                use[("f8", r)] = t_mm = T(m)
                spread(n + 2)
                next(tail, None)
                if p0 + PT == NT:
                    for _ in tail:
                        pass
                    tail = finish_unit(units[u][0], h, t_mm, t_acc[u], pair, u % 2)
            for _ in tail:
                pass
            barrier()

    def block_experts():
        NLAY, H = m_rw.shape[0], m_win.shape[1]
        KB = H // P
        NWK, NSG = m_ww.shape[1], m_w1.shape[1]
        NE = NWK + NSG
        FB = m_w1.shape[3] // P
        with scope() as c:
            h2 = sbuf(c, "m_h", [P, NT, H], F32)
            bcast = sbuf(c, "m_bias", [P, NE * H], F32)
            agg = sbuf(c, "m_agg", [P, KB, BANK], F32)
            hT = sbuf(c, "m_hT", [P, KB, BANK], F32)
            rw = sbuf(c, "m_rw", [P, 2 * KB, NE + 1], F32)
            rb = sbuf(c, "m_rb", [P, NE + 1], F32)
            sc = sbuf(c, "m_sc", [P, 4], F32)
            hmax = sbuf(c, "m_hmax", [P, len(CH)], F32)
            wout = sbuf(c, "m_wo", [P, KB, D], F32)
            bout = sbuf(c, "m_bo", [P, D], F32)
            prio = sbuf(c, "m_prio", [P, NE], F32)
            t_prio = G(pool.iota(prio[:], pattern=[[-1, NE]], base=NE, channel_multiplier=0,
                                 allow_small_or_imprecise_dtypes=True))
            t_wo = [dma("act", "m_wo", wout[:], m_wout.rearrange("(k p) o -> p k o", p=P)),
                    dma("act", "m_bo", bout[:], bass.AP(m_bout.tensor, m_bout.offset, [[0, P], [1, D]]))]
            with scope() as c0:
                hn = sbuf(c0, "m_hn", [P, NT, D], F32)
                layer_norm(hn)
                need("sp", now("dve"))
                t_park = dma("sp", "park", xpark, xn[:].rearrange("p i f -> p (i f)"))
                win = sbuf(c0, "m_win", [P, H], F32)
                bin_ = sbuf(c0, "m_bin", [P, H], F32)
                xT = [sbuf(c0, f"m_xT{i}", [P, BANK], F32) for i in range(2)]
                ld = [dma("act", "m_win", win[:], m_win),
                      dma("act", "m_bin", bin_[:], bass.AP(m_bin.tensor, m_bin.offset, [[0, P], [1, H]]))]
                need("pe", now("dve"), *ld)
                need("dve", *ld)
                xt_free = [None, None]
                for i0 in range(0, NT, 4):
                    q = (i0 // 4) % 2
                    n_ = min(4, NT - i0)
                    need("pe", bank_free[6 + q])
                    for k in range(n_):
                        m = pe.transpose(bank[6 + q][:, k * P:(k + 1) * P], hn[:, i0 + k, :], ident[:])
                    need("act", T(m), xt_free[q])
                    bank_free[6 + q] = t0 = S(act.activation(xT[q][:, 0:n_ * P], bank[6 + q][:, 0:n_ * P], ACT.Copy))
                    need("pe", t0)
                    for k in range(n_):
                        b_ = (i0 + k) % 6
                        need("pe", bank_free[b_])
                        xt_free[q] = t0 = T(pe.matmul(bank[b_][:, 0:H], xT[q][:, k * P:(k + 1) * P], win[:], start=True, stop=True))
                        need("dve", t0)
                        bank_free[b_] = V(vec.tensor_tensor(h2[:, i0 + k, :], bank[b_][:, 0:H], bin_[:], ALU.add))
                need("sp", t_park)
                barrier()
            with scope() as c0:
                h16 = feature_pair(c0, "m_h16", H)
                ww = sbuf(c0, "m_ww", [P, KB, NWK * H], F32)
                w1 = sbuf(c0, "m_w1", [P, NSG, KB, FB * P], F32)
                w2 = sbuf(c0, "m_w2", [P, NSG, FB, H], F32)
                b1 = sbuf(c0, "m_b1", [P, NSG * FB], F32)
                NSH = 2 * FB
                xroom = xn[:].rearrange("p i f -> p (i f)")
                n_room = min(NSH, NT * D // BANK)
                sh = [xroom[:, i * BANK:(i + 1) * BANK] for i in range(n_room)]
                sh += [sbuf(c0, f"m_sh{i}", [P, BANK], F32) for i in range(NSH - n_room)]
                wtmp = sbuf(c0, "m_wtmp", [P, 2 * H], F32)
                tmp = [wtmp[:, i * H:(i + 1) * H] for i in range(2)]
                invd = sbuf(c0, "m_invd", [P, BANK], F32)
                lg = sbuf(c0, "m_lg", [P, 4, NE + 1], F32)
                rt = [sbuf(c0, f"m_rt{i}", [P, 4, NE], F32) for i in range(5)]
                sm = sbuf(c0, "m_sm", [P, 10, 4], F32)
                gates = [sbuf(c0, f"m_g{i}", [P, 4, NE], F32) for i in range(2)]
                v(vec.memset(rw[:, KB:2 * KB, NE:NE + 1], 0.0))
                for l in range(NLAY):
                    ld_r = [dma("act", "m_rw", rw[:, :, 0:NE], m_rw[l].rearrange("(k p) e -> p k e", p=P)),
                            dma("act", "m_cw", rw[:, 0:KB, NE:NE + 1], m_cw[l].rearrange("(k p) e -> p k e", p=P), allow_slow_non_contiguous=True),
                            dma("act", "m_rb", rb[:, 0:NE], bass.AP(m_rb.tensor, m_rb.offset + l * NE, [[0, P], [1, NE]])),
                            dma("act", "m_cb", rb[:, NE:NE + 1], bass.AP(m_cb.tensor, m_cb.offset + l, [[0, P], [1, 1]]))]
                    ld_w1 = [dma("sp", f"m_w1{e}", w1[:, e], m_w1[l, e].rearrange("(k p) f -> p k f", p=P)) for e in range(NSG)]
                    ld_b1 = dma("act", "m_b1", b1[:], m_b1[l].rearrange("e (k p) -> p (e k)", p=P), allow_slow_non_contiguous=True)
                    ld_w2 = [dma("sp", f"m_w2{e}", w2[:, e], m_w2[l, e].rearrange("(k p) h -> p k h", p=P)) for e in range(NSG)]
                    ld_ww = [dma("sp", f"m_ww{e}", ww[:, :, e * H:(e + 1) * H], m_ww[l, e].rearrange("(k p) h -> p k h", p=P)) for e in range(NWK)]
                    ld_bb = [dma("act", "m_wb", bcast[:, 0:NWK * H], bass.AP(m_wb.tensor, m_wb.offset + l * NWK * H, [[0, P], [1, NWK * H]])),
                             dma("act", "m_b2", bcast[:, NWK * H:NE * H], bass.AP(m_b2.tensor, m_b2.offset + l * NSG * H, [[0, P], [1, NSG * H]]))]
                    if l == 0:
                        v(vec.tensor_reduce(sc[:, 0:1], h2[:], axis=AX.XY, op=ALU.max, apply_absolute_value=True))
                    else:
                        v(vec.tensor_reduce(sc[:, 0:1], hmax[:], axis=AX.X, op=ALU.max))
                    need("pe", now("dve"), bank_free[6], bank_free[7])
                    t0 = T(pe.transpose(bank[6][0:1, 0:P], sc[:, 0:1], ident[:]))
                    need("dve", t0)
                    t0 = v(vec.tensor_reduce(sc[0:1, 1:2], bank[6][0:1, 0:P], axis=AX.X, op=ALU.max))
                    need("pe", t0)
                    t0 = T(pe.matmul(bank[7][:, 0:1], ones_f[0:1, :], sc[0:1, 1:2], start=True, stop=True))
                    need("dve", t0)
                    v(vec.tensor_copy(sc[:, 0:1], bank[7][:, 0:1]))
                    power_scale(sc[:, 0:1], sc[:, 1:2], sc[:, 2:3], sc[:, 3:4])
                    bank_free[6] = bank_free[7] = now("dve")
                    need("act", now("dve"))
                    t_h = []
                    if not fast:
                        t_h = [v(vec.tensor_scalar(h16, h2[:], sc[:, 1:2], None, ALU.mult))]
                    for i0 in range(0, NT, 5) if fast else ():
                        hs = h2[:, i0:i0 + 5, :]
                        t0 = S(act.activation(h16[:, 0, i0:i0 + 5, :], hs, ACT.Copy, scale=sc[:, 1:2]))
                        need("dve", t0)
                        t_h.append(V(vec.scalar_tensor_tensor(h16[:, 1, i0:i0 + 5, :], hs, sc[:, 1:2],
                                                              h16[:, 0, i0:i0 + 5, :], ALU.mult, ALU.subtract)))
                    use = {}
                    t_route = {}
                    t_agg = {}

                    def edges(ci):
                        c_, cw = CH[ci]
                        for kb in range(KB):
                            if not fast:
                                t_agg[(ci, kb)] = load_sums(kb, block_sums[kb], 0, CH[ci])
                                continue
                            need("pe", bank_free[kb])
                            for i in range(NT):
                                need("pe", t_h[i // 5])
                                for part in range(2):
                                    m = pe.matmul(bank[kb][:, 0:cw], h16[:, part, i, kb * P:(kb + 1) * P],
                                                  A[:, i, c_:c_ + cw], start=(i == 0 and part == 0),
                                                  stop=(i == NT - 1 and part == 1))
                            t_agg[(ci, kb)] = T(m)

                    def turn(ci):
                        c_, cw = CH[ci]
                        ts = tiles_of(CH[ci])
                        for kb in range(KB):
                            b_ = 2 + kb
                            need("pe", bank_free[b_])
                            for i, k in ts:
                                m = pe.transpose(bank[b_][:, k * P:(k + 1) * P], h2[:, i, kb * P:(kb + 1) * P], ident[:])
                            need("act", T(m), use.get("hT"))
                            wd_ = len(ts) * P
                            bank_free[b_] = use["t_hT"] = S(act.activation(hT[:, kb, 0:wd_], bank[b_][:, 0:wd_], ACT.Copy))
                        need("sp", use.get("invd"))
                        use["t_invd"] = dma("sp", "invd", invd[:, 0:cw], bass.AP(invd_row.tensor, c_, [[0, P], [1, cw]]))

                    def mean(ci):
                        c_, cw = CH[ci]
                        need("dve", use["t_invd"], use.get("agg"))
                        for kb in range(KB):
                            need("dve", t_agg[(ci, kb)])
                            bank_free[kb] = use["invd"] = v(vec.scalar_tensor_tensor(
                                agg[:, kb, 0:cw], bank[kb][:, 0:cw], sc[:, 2:3], invd[:, 0:cw], ALU.mult, ALU.mult))

                    def route(ci):
                        ts = tiles_of(CH[ci])
                        need("pe", use["invd"], use["t_hT"], bank_free[2], *ld_r)
                        for i, k in ts:
                            r_ = rows_of(i)
                            for kk in range(2 * KB):
                                lhs = (hT if kk < KB else agg)[:, kk % KB, k * P:k * P + r_]
                                m = pe.matmul(bank[2][0:r_, k * (NE + 1):(k + 1) * (NE + 1)], lhs, rw[:, kk, :],
                                              start=(kk == 0), stop=(kk == 2 * KB - 1))
                        use["hT"] = t0 = T(m)
                        R_, _, n_ = chunk_rows(CH[ci])
                        need("dve", t0, *ld_r)
                        need("dve", t_prio)
                        lg_ = lg[0:R_, 0:n_, :]
                        l_ = lg[0:R_, 0:n_, 0:NE]
                        v(vec.tensor_tensor(lg_, bank[2][0:R_, 0:n_ * (NE + 1)].rearrange("p (t e) -> p t e", e=NE + 1),
                                            rb[0:R_, None, :].to_broadcast([R_, n_, NE + 1]), ALU.add))
                        bank_free[2] = now("dve")
                        o1, o2, l2, e_ = (r[0:R_, 0:n_, :] for r in rt[0:4])
                        S1 = [sm[0:R_, i_, 0:n_] for i_ in range(10)]

                        def wide(a):
                            return a[:, :, None].to_broadcast([R_, n_, NE])

                        def pick(logits, top_, first, o):
                            v(vec.tensor_reduce(top_, logits, axis=AX.X, op=ALU.max))
                            v(vec.tensor_tensor(e_, logits, wide(top_), ALU.is_equal))
                            v(vec.tensor_tensor(e_, e_, prio[0:R_, None, :].to_broadcast([R_, n_, NE]), ALU.mult))
                            v(vec.tensor_reduce(first, e_, axis=AX.X, op=ALU.max))
                            v(vec.tensor_tensor(o, e_, wide(first), ALU.is_equal))

                        pick(l_, S1[0], S1[1], o1)
                        v(vec.scalar_tensor_tensor(l2, o1, -3e38, l_, ALU.mult, ALU.add))
                        pick(l2, S1[2], S1[3], o2)
                        v(vec.tensor_tensor(S1[4], S1[2], S1[0], ALU.subtract))
                        v(vec.tensor_scalar(S1[5], lg[0:R_, 0:n_, NE], -1.0, 80.0, ALU.mult, ALU.min))
                        need("act", now("dve"))
                        t0 = S(act.activation(sm[0:R_, 6:8, 0:n_], sm[0:R_, 4:6, 0:n_], ACT.Exp))
                        need("dve", t0)
                        v(vec.tensor_scalar(sm[0:R_, 8:10, 0:n_], sm[0:R_, 6:8, 0:n_], 1.0, None, ALU.add))
                        v(vec.reciprocal(sm[0:R_, 8:10, 0:n_], sm[0:R_, 8:10, 0:n_]))
                        v(vec.tensor_tensor(S1[8], S1[8], S1[9], ALU.mult))
                        v(vec.tensor_tensor(S1[6], S1[6], S1[8], ALU.mult))
                        g_ = gates[ci % 2][0:R_, 0:n_, :]
                        need("dve", use.get(("g", ci % 2)))
                        v(vec.tensor_tensor(o1, o1, wide(S1[8]), ALU.mult))
                        v(vec.tensor_tensor(o2, o2, wide(S1[6]), ALU.mult))
                        t_route[ci] = v(vec.tensor_tensor(g_, o1, o2, ALU.add))

                    n_sh = [0]
                    blk = {}

                    def hidden(ci, e):
                        c_, cw = CH[ci]
                        need("pe", ld_w1[e])
                        need("act", ld_b1)
                        for f in range(FB):
                            b_ = 4 + n_sh[0] % 2
                            s_i = n_sh[0] % NSH
                            n_sh[0] += 1
                            need("pe", bank_free[b_])
                            for kb in range(KB):
                                m = pe.matmul(bank[b_][:, 0:cw], w1[:, e, kb, f * P:(f + 1) * P], agg[:, kb, 0:cw],
                                              start=(kb == 0), stop=(kb == KB - 1))
                            t0 = use["agg"] = T(m)
                            need("act", t0, use.get(("sh", s_i)))
                            bank_free[b_] = t0 = S(act.activation(sh[s_i][:, 0:cw], bank[b_][:, 0:cw], ACT.Relu,
                                                                  bias=b1[:, e * FB + f:e * FB + f + 1]))
                            blk[(e, f)] = (s_i, t0)

                    def strong(ci, e):
                        need("pe", ld_w2[e])
                        need("dve", *ld_bb)
                        for i, k in tiles_of(CH[ci]):
                            r_ = rows_of(i)
                            b_ = 6 + k % 2
                            need("pe", bank_free[b_])
                            for f in range(FB):
                                s_i, t0 = blk[(e, f)]
                                need("pe", t0)
                                m = pe.matmul(bank[b_][0:r_, 0:H], sh[s_i][:, k * P:k * P + r_], w2[:, e, f, :],
                                              start=(f == 0), stop=(f == FB - 1))
                            t0 = T(m)
                            for f in range(FB):
                                use[("sh", blk[(e, f)][0])] = t0
                            q = k % 2
                            ge = NWK + e
                            need("dve", t0, t_route[ci])
                            bank_free[b_] = v(vec.tensor_tensor(tmp[q][0:r_, :], bank[b_][0:r_, 0:H],
                                                                bcast[0:r_, ge * H:(ge + 1) * H], ALU.add))
                            use[("g", ci % 2)] = v(vec.scalar_tensor_tensor(
                                h2[0:r_, i, :], tmp[q][0:r_, :], gates[ci % 2][0:r_, k, ge:ge + 1], h2[0:r_, i, :],
                                ALU.mult, ALU.add))

                    def weak(ci):
                        need("pe", *ld_ww)
                        need("dve", *ld_bb)
                        need("dve", t_route[ci])
                        for i, k in tiles_of(CH[ci]):
                            r_ = rows_of(i)
                            for pr in range(NWK * H // BANK):
                                b_ = 2 + pr % 2
                                need("pe", bank_free[b_])
                                for kb in range(KB):
                                    m = pe.matmul(bank[b_][0:r_, :], agg[:, kb, k * P:k * P + r_],
                                                  ww[:, kb, pr * BANK:(pr + 1) * BANK], start=(kb == 0), stop=(kb == KB - 1))
                                use["agg"] = t0 = T(m)
                                need("dve", t0)
                                bank_free[b_] = t0 = v(vec.tensor_tensor(wtmp[0:r_, :], bank[b_][0:r_, :],
                                                                         bcast[0:r_, pr * BANK:(pr + 1) * BANK], ALU.add))
                                for x_ in range(BANK // H):
                                    e = pr * (BANK // H) + x_
                                    w_ = wtmp[0:r_, x_ * H:(x_ + 1) * H]
                                    v(vec.tensor_scalar(w_, w_, 0.0, gates[ci % 2][0:r_, k, e:e + 1], ALU.max, ALU.mult))
                                    use[("g", ci % 2)] = v(vec.tensor_tensor(h2[0:r_, i, :], h2[0:r_, i, :], w_, ALU.add))

                    block_sums = [sums, degs8]
                    if not fast:
                        for kb in range(KB):
                            scatter_sum(h16[:, :, kb * P:(kb + 1) * P], block_sums[kb], [("src", "to_dst")])
                    edges(0)
                    turn(0)
                    mean(0)
                    for ci in range(len(CH)):
                        more = ci + 1 < len(CH)
                        route(ci)
                        hidden(ci, 0)
                        if more:
                            edges(ci + 1)
                            turn(ci + 1)
                        weak(ci)
                        for e in range(1, NSG):
                            hidden(ci, e)
                            if e < NSG - 1:
                                strong(ci, e - 1)
                        if more:
                            mean(ci + 1)
                        strong(ci, NSG - 2)
                        strong(ci, NSG - 1)
                        i0, n_ = tiles_of(CH[ci])[0][0], len(tiles_of(CH[ci]))
                        v(vec.tensor_reduce(hmax[:, ci:ci + 1], h2[:, i0:i0 + n_, :], axis=AX.XY, op=ALU.max,
                                            apply_absolute_value=True))
                    barrier()
                barrier()
            with scope() as c0:
                xr = xn
                t_x = dma("sp", "unpark", xr[:].rearrange("p i f -> p (i f)"), xpark)
                need("dve", t_x, *t_wo)
                need("pe", *t_wo)
                out_full, out_tail = node_rows(out)
                t_o = []
                hf = {}
                for ci in range(len(CH)):
                    ts = tiles_of(CH[ci])
                    for kb in range(KB):
                        b_ = 2 + kb
                        need("pe", bank_free[b_])
                        for i, k in ts:
                            m = pe.transpose(bank[b_][:, k * P:(k + 1) * P], h2[:, i, kb * P:(kb + 1) * P], ident[:])
                        wd_ = len(ts) * P
                        need("act", T(m), hf.get("hT"))
                        bank_free[b_] = t0 = S(act.activation(hT[:, kb, 0:wd_], bank[b_][:, 0:wd_], ACT.Copy))
                    need("pe", t0)
                    for i, k in ts:
                        r_ = rows_of(i)
                        b_ = 4 + i % 2
                        need("pe", bank_free[b_])
                        for kb in range(KB):
                            m = pe.matmul(bank[b_][0:r_, 0:D], hT[:, kb, k * P:k * P + r_], wout[:, kb, :],
                                          start=(kb == 0), stop=(kb == KB - 1))
                        hf["hT"] = t0 = T(m)
                        need("dve", t0)
                        bank_free[b_] = v(vec.tensor_tensor(xr[0:r_, i, :], xr[0:r_, i, :], bank[b_][0:r_, 0:D], ALU.add))
                        t0 = v(vec.tensor_tensor(xr[0:r_, i, :], xr[0:r_, i, :], bout[0:r_, :], ALU.add))
                    need("sp", t0)
                    i0, n_ = ts[0][0], len(ts)
                    if i0 == NT - 1:
                        t_o.append(dma("sp", f"out{ci}", out_tail, xr[0:TAIL, i0, :]))
                    else:
                        t_o.append(dma("sp", f"out{ci}", out_full[:, i0:i0 + n_, :], xr[:, i0:i0 + n_, :]))
                need("sp", *t_o)
                barrier()

    def network():
        with scope() as c:
            if not fast:
                with scope() as c0:
                    make_lists(c0)
                chunk_buf["buf"] = room[:, 0:4 * D].rearrange("p (i f) -> p i f", f=D)
            degrees()
            block_gru()
            block_gcn()
            block_relations()
            block_experts()

    room = A[:].rearrange("p i c -> p (i c)").bitcast(F32)
    for k in engines:
        seen[k] = {}
    ok = nc.values_load(flag[0:1, 0:1], min_val=0, max_val=1)
    at_branch = dict(count)
    slots_at_branch = {n_: s[1] for n_, s in slots.items()}
    with nc.If(ok == 1):
        network()
    with nc.Else():
        count.update(at_branch)
        for n_, s in slots.items():
            s[1] = slots_at_branch.get(n_, 0)
        for k in engines:
            seen[k] = {}
        bank_free[:] = [None] * 8
        scale_tmp.clear()
        fast = False
        network()
    top.close()


_INS = ["x", "src", "dst", "edge_type_8", "L0_gnn_weight", "L0_gnn_w_ih", "L0_gnn_w_hh", "L0_gnn_b_ih",
        "L0_gnn_b_hh", "L1_gnn_W0", "L1_gnn_b0", "L1_gnn_W1", "L1_gnn_b1", "L2_gnn_weight", "L2_gnn_self_weight",
        "L3_gnn_W_in", "L3_gnn_b_in", "L3_gnn_router_W", "L3_gnn_router_b", "L3_gnn_weak_W", "L3_gnn_weak_b",
        "L3_gnn_strong_W1", "L3_gnn_strong_b1", "L3_gnn_strong_W2", "L3_gnn_strong_b2", "L3_gnn_conf_W",
        "L3_gnn_conf_b", "L3_gnn_W_out", "L3_gnn_b_out"]


def kernel(**inputs):
    import concourse.bacc as bacc
    from concourse.bass_utils import run_bass_kernel_spmd

    nc = bacc.Bacc("TRN2", target_bir_lowering=False, num_devices=1)
    arrays, args = {}, []
    for name in _INS:
        a = np.ascontiguousarray(inputs[name])
        arrays["in_" + name] = a
        args.append(nc.dram_tensor("in_" + name, a.shape, dt.from_np(a.dtype), kind="ExternalInput").ap())
    out = nc.dram_tensor("out", arrays["in_x"].shape, F32, kind="ExternalOutput").ap()
    build_program(nc, *args, out)
    r = run_bass_kernel_spmd(nc, [arrays], core_ids=[0])
    return r.results[0]["out"]
```

```python
from contextlib import ExitStack

import numpy as np
import concourse.bass as bass
from concourse import mybir

dt = mybir.dt
F32, F16, BF16, F8 = dt.float32, dt.float16, dt.bfloat16, dt.float8e4
I32, U16, U8 = dt.int32, dt.uint16, dt.uint8
ALU = mybir.AluOpType
ACT = mybir.ActivationFunctionType
AX = mybir.AxisListType

P = 128
BANK = 512
WN = 5
SLOTS = 2
ALIGN = 32
GW = 8
COUNT_SCALE = 0.25
COUNT_MAX = 7
EPS = 1e-5
FIXED = 4096.0


def build_program(nc, x, src, dst, et, g_w, g_ih, g_hh, g_bih, g_bhh, c_w0, c_b0, c_w1, c_b1,
                  r_w, r_self, m_win, m_bin, m_rw, m_rb, m_ww, m_wb, m_w1, m_b1, m_w2, m_b2,
                  m_cw, m_cb, m_wout, m_bout, out):
    N, D = x.shape
    E = src.shape[0]
    NT = -(-N // P)
    NP = NT * P
    TAIL = N - (NT - 1) * P
    NW = -(-N // WN)
    NG = -(-NW // GW)
    NWP = NG * GW
    NC = NWP * WN
    U = SLOTS * GW
    WB = -(-NWP // P)
    WCOL = WN * NT
    SLOTN = SLOTS * P
    STRIP = 4
    SW = STRIP * GW * WN
    NSTR = -(-NG // STRIP)
    assert NSTR * SW == NP and 4 * WCOL <= BANK
    NREL = r_w.shape[0]
    CH = [(c, min(BANK, N - c)) for c in range(0, N, BANK)]
    EP = 125
    EC = E // EP
    LG = EC // ALIGN
    assert EC % ALIGN == 0 and D == P and NREL == 8
    NLG = E // ALIGN
    TROWS = -(-(NLG + 1) // 64) * 64
    EPAD = TROWS * ALIGN + SLOTN - E

    engines = {"pe": nc.tensor, "dve": nc.vector, "act": nc.scalar, "pool": nc.gpsimd, "sp": nc.sync}
    top = ExitStack()
    done = {k: top.enter_context(nc.semaphore(f"done_{k}")) for k in ("pe", "dve", "act", "pool")}
    count = {k: 0 for k in done}

    def tick(k, inst):
        count[k] += 1
        inst.then_inc(done[k], 1)
        return done[k], count[k]

    seen = {k: {} for k in engines}

    def need(k, *tokens):
        for t in tokens:
            if t is None:
                continue
            if isinstance(t, list):
                need(k, *t)
                continue
            sem, value = t
            if seen[k].get(sem.name, 0) < value:
                engines[k].wait_ge(sem, value)
                seen[k][sem.name] = value

    slots = {}

    def dma(k, name, out_, in_, **kw):
        if name not in slots:
            slots[name] = [top.enter_context(nc.semaphore(f"dma_{name}")), 0]
        s = slots[name]
        engines[k].dma_start(out_, in_, **kw).then_inc(s[0], 16)
        s[1] += 16
        return s[0], s[1]

    def gather(name, out_, table, idx):
        if name not in slots:
            slots[name] = [top.enter_context(nc.semaphore(f"dma_{name}")), 0]
        s = slots[name]
        nc.gpsimd.indirect_dma_start(out=out_, out_offset=None, in_=table,
                                     in_offset=bass.IndirectOffsetOnAxis(ap=idx, axis=0)).then_inc(s[0], 16)
        s[1] += 16
        return s[0], s[1]

    def V(inst):
        return tick("dve", inst)

    def S(inst):
        return tick("act", inst)

    def G(inst):
        return tick("pool", inst)

    def T(inst):
        return tick("pe", inst)

    def scope():
        return ExitStack()

    made = []


    def sbuf(ctx, name, shape, dtype):
        made.append(name)
        return ctx.enter_context(nc.sbuf_tensor(f"{name}_{len(made)}", shape, dtype))

    def barrier():
        nc.all_engine_barrier()

    vec, act, pool, pe, sp = nc.vector, nc.scalar, nc.gpsimd, nc.tensor, nc.sync

    epk = nc.dram_tensor("edge_words", (E + EPAD,), I32).ap()
    last_dram = nc.dram_tensor("last_dst", (NLG,), I32).ap()
    tbl = nc.dram_tensor("slot_table", (TROWS, SLOTN), I32).ap()
    pd = nc.dram_tensor("packed_counts", (NP, NP), I32).ap()
    sd = nc.dram_tensor("packed_sym", (NP, NP), I32).ap()
    deg_row = nc.dram_tensor("deg_row", (N,), F32).ap()
    dinv_row = nc.dram_tensor("dinv_row", (N,), F32).ap()
    invd_row = nc.dram_tensor("invd_row", (N,), F32).ap()
    SUMS = NREL * NP + P
    feat = nc.dram_tensor("features", (NP, D), F32).ap()
    sums = nc.dram_tensor("edge_sums", (SUMS, D), F32).ap()
    degs8 = nc.dram_tensor("type_degrees", (SUMS, D), F32).ap()
    ET = -(-E // P)
    lists = {n: nc.dram_tensor("list_" + n, (ET * P,), I32).ap() for n in ("src", "dst", "to_dst", "to_type_dst", "to_type_src")}
    xpark = nc.dram_tensor("x_parked", (P, NT * D), F32).ap()

    bank = [top.enter_context(nc.psum_tensor(f"bank{i}", [P, BANK], F32)) for i in range(8)]

    A = sbuf(top, "counts", [P, NT, NC], F8)
    ident = sbuf(top, "ident", [P, P], F32)
    ones_bf = sbuf(top, "ones_bf", [P, 1], BF16)
    ones_f = sbuf(top, "ones_f", [P, P], F32)
    flag = sbuf(top, "flag", [1, 1], I32)
    xn = sbuf(top, "x_nodes", [P, NT, D], F32)

    t_ones = V(vec.memset(ones_f[:], 1.0))
    t_onesb = V(vec.memset(ones_bf[:], 1.0))
    need("pool", t_ones)
    t_ident = G(pool.affine_select(out=ident[:], in_=ones_f[:], compare_op=ALU.is_equal, fill=0.0, base=0,
                                   pattern=[[-1, P]], channel_multiplier=1))

    full = (NT - 1) * P
    t_xz = V(vec.memset(xn[:, NT - 1, :], 0.0))
    need("sp", t_xz)
    t_x = [dma("sp", "x_tail", xn[0:TAIL, NT - 1, :], x[full:N, :])]
    for i0 in range(0, NT - 1, 4):
        t_x.append(dma("sp", f"x_{i0}", xn[:, i0:i0 + 4, :],
                       x[i0 * P:(i0 + 4) * P, :].rearrange("(i p) f -> p i f", p=P)))

    with scope() as c1:
        thr = sbuf(c1, "thr", [P, WB], F32)
        row = sbuf(c1, "row", [P, WB], I32)
        with scope() as c0:
            ew = {n: sbuf(c0, f"e_{n}", [EP, EC], I32) for n in ("src", "dst", "et", "word")}
            pad = sbuf(c0, "pad", [1, EPAD], I32)
            last = sbuf(c0, "last", [EP, LG], I32)
            ld = [dma("sp", "l" + n, ew[n][:], a.rearrange("(p c) -> p c", p=EP))
                  for n, a in (("dst", dst), ("src", src), ("et", et))]
            t_pad = V(vec.memset(pad[:], 2130706432))
            need("dve", ld[0])
            t_last = V(vec.tensor_copy(last[:], ew["dst"][:, ALIGN - 1::ALIGN]))
            need("sp", t_last)
            t_ldr = dma("sp", "last_out", last_dram.rearrange("(p c) -> p c", p=EP), last[:])
            need("dve", t_last, *ld)
            t1 = V(vec.tensor_scalar(ew["dst"][:], ew["dst"][:], 15, None, ALU.logical_shift_left))
            t2 = V(vec.tensor_scalar(ew["et"][:], ew["et"][:], 12, None, ALU.logical_shift_left))
            need("dve", t1, t2)
            t3 = V(vec.tensor_tensor(ew["word"][:], ew["dst"][:], ew["et"][:], ALU.bitwise_or))
            need("dve", t3)
            t4 = V(vec.tensor_tensor(ew["word"][:], ew["word"][:], ew["src"][:], ALU.bitwise_or))
            need("act", t4, t_pad)
            t5 = [dma("act", "word_out", epk[0:E].rearrange("(p c) -> p c", p=EP), ew["word"][:]),
                  dma("act", "pad_out", epk[E:E + EPAD].rearrange("(a n) -> a n", a=1), pad[:])]
            need("act", t5)
            t_tbl = dma("act", "table", tbl, bass.AP(epk.tensor, 0, [[ALIGN, TROWS], [1, SLOTN]]))

            lastb = sbuf(c0, "lastb", [P, NLG], I32)
            lastf = sbuf(c0, "lastf", [P, NLG], F32)
            below = sbuf(c0, "below", [P, NLG], BF16)
            cnt = sbuf(c0, "cnt", [P, WB], F32)
            need("sp", t_ldr)
            t_lb = dma("sp", "last_in", lastb[:], bass.AP(last_dram.tensor, 0, [[0, P], [1, NLG]]))
            t_thr = G(pool.iota(thr[:], pattern=[[WN * P, WB]], base=0, channel_multiplier=WN,
                                allow_small_or_imprecise_dtypes=True))
            need("dve", t_lb, t_thr)
            t = V(vec.tensor_copy(lastf[:], lastb[:]))
            need("dve", t)
            for b in range(WB):
                t = V(vec.tensor_scalar(below[:], lastf[:], thr[:, b:b + 1], None, ALU.is_lt, ALU.add,
                                        accum_out=cnt[:, b:b + 1]))
                need("dve", t)
            t_row = V(vec.tensor_copy(row[:], cnt[:]))
            barrier()

        words = sbuf(c1, "words", [P, WB, SLOTN], I32)
        scal = sbuf(c1, "scal", [P, 3, NG + P // GW, SLOTS, GW], BF16)
        hits = sbuf(c1, "hits", [P, 1], F32)
        with scope() as c0:
            need("pool", t_row, t_tbl)
            t_g = [gather(f"win{b}", words[:, b, :], tbl, row[:, b:b + 1]) for b in range(WB)]
            fld = [sbuf(c0, f"fld{i}", [P, WB, SLOTN], F32) for i in range(3)]
            ti = [sbuf(c0, f"ti{i}", [P, WB, SLOTN], I32) for i in range(2)]
            tf = [sbuf(c0, f"tf{i}", [P, WB, SLOTN], F32) for i in range(3)]
            need("dve", *t_g)

            def v(inst):
                need("dve", V(inst))

            def shift_and(o, i, sh, mask, left=False):
                v(vec.tensor_scalar(o, i, sh, mask, ALU.logical_shift_right, ALU.bitwise_and))

            w_ = words[:]
            shift_and(ti[0][:], w_, 0, P - 1)
            v(vec.tensor_copy(fld[0][:], ti[0][:]))
            v(vec.tensor_scalar(ti[0][:], w_, 15, None, ALU.logical_shift_right))
            v(vec.tensor_copy(tf[0][:], ti[0][:]))
            v(vec.tensor_tensor(tf[0][:], tf[0][:], thr[:, :, None].to_broadcast([P, WB, SLOTN]), ALU.subtract))
            v(vec.tensor_scalar(tf[1][:], tf[0][:], 0.0, float(WN - 1), ALU.max, ALU.min))
            v(vec.tensor_tensor(tf[2][:], tf[0][:], tf[1][:], ALU.is_equal))
            v(vec.tensor_reduce(hits[:], tf[2][:], axis=AX.XY, op=ALU.add))
            v(vec.tensor_scalar(tf[2][:], tf[2][:], -1000.0, 1000.0, ALU.mult, ALU.add))
            shift_and(ti[0][:], w_, 7, 31)
            v(vec.tensor_copy(fld[1][:], ti[0][:]))
            v(vec.scalar_tensor_tensor(fld[1][:], tf[1][:], float(2 * NT), fld[1][:], ALU.mult, ALU.add))
            shift_and(ti[0][:], w_, 14, 1)
            v(vec.tensor_copy(tf[1][:], ti[0][:]))
            v(vec.scalar_tensor_tensor(fld[1][:], tf[1][:], float(NT), fld[1][:], ALU.mult, ALU.add))
            v(vec.tensor_tensor(fld[1][:], fld[1][:], tf[2][:], ALU.add))
            v(vec.tensor_scalar(fld[1][:], fld[1][:], 255.0, None, ALU.min))
            shift_and(ti[0][:], w_, 12, 3)
            v(vec.tensor_scalar(ti[1][:], ti[0][:], float(1 << 25), float(127 << 23), ALU.mult, ALU.add))
            v(vec.tensor_copy(fld[2][:], ti[1][:].bitcast(F32)))
            t_fld = (done["dve"], count["dve"])
            need("pe", t_fld, t_ident)
            free = [None] * 8
            n = 0
            t_sc = None
            for i in range(3):
                for b in range(WB):
                    for j in range(SLOTS):
                        k = n % 8
                        n += 1
                        need("pe", free[k])
                        tt = T(pe.transpose(bank[k][:, 0:P], fld[i][:, b, j * P:(j + 1) * P], ident[:]))
                        g0 = b * (P // GW)
                        o = scal[:, i, g0:g0 + P // GW, j, :]
                        src_ = bank[k][:, 0:P].rearrange("p (g w) -> p g w", w=GW)
                        if n % 2:
                            need("dve", tt)
                            free[k] = V(vec.tensor_copy(o, src_))
                        else:
                            need("act", tt)
                            free[k] = S(act.activation(o, src_, ACT.Copy))
            barrier()

        HC = 2 * WCOL
        cols = sbuf(c1, "cols", [P, HC, U], BF16)
        oh_s = [sbuf(c1, f"oh_s{i}", [P, P, U], BF16) for i in range(2)]
        oh_w = [sbuf(c1, f"oh_w{i}", [P, P, U], BF16) for i in range(2)]
        oh_c = [sbuf(c1, f"oh_c{i}", [P, HC, U], BF16) for i in range(2)]
        strip = [sbuf(c1, f"strip{i}", [P, NT, SW], I32) for i in range(2)]
        codes, found = (sbuf(c1, n_, [P, NT, SW // 4], I32) for n_ in ("codes", "found"))
        need("dve", V(vec.memset(codes[:], 0)))
        degs = sbuf(c1, "degs", [1, NP], F32)
        t_cols = G(pool.iota(cols[:], pattern=[[1, HC], [0, U]], base=0, channel_multiplier=0,
                             allow_small_or_imprecise_dtypes=True))
        need("dve", t_cols)
        evacuated = {}

        def with_strip(j, tok):
            c_ = j * SW
            w_ = min(SW, NC - c_)
            need("pe", tok, free[DB])
            for i in range(NT):
                m = pe.matmul(bank[DB][0:1, 0:w_], ones_bf[:], A[:, i, c_:c_ + w_], start=(i == 0), stop=(i == NT - 1))
            need("act", T(m))
            free[DB] = S(act.activation(degs[:, c_:c_ + w_], bank[DB][0:1, 0:w_], ACT.Copy, scale=1.0 / COUNT_SCALE))
            need("dve", tok)
            o = codes[:, :, 0:w_ // 4]
            v(vec.tensor_tensor(o, o, A[:, :, c_:c_ + w_].bitcast(I32), ALU.bitwise_or))

        AB, HB, DB = (0, 1), (2, 3, 4, 5, 6), 7
        free = [None] * 8
        hb = 0
        used = [None, None]
        strip_free = [None, None]
        strip_tok = []
        packed_out = []
        for g in range(NG):
            q = g % 2
            sc = [scal[:, i, g].rearrange("p j w -> p (j w)")[:, None, :] for i in range(3)]
            need("dve", used[q])
            V(vec.tensor_tensor(oh_c[q][:], cols[:], sc[1].to_broadcast([P, HC, U]), ALU.is_equal))
            t = V(vec.tensor_tensor(oh_s[q][:], cols[:, 0:P, :], sc[0].to_broadcast([P, P, U]), ALU.is_equal))
            need("dve", t)
            t_oh = V(vec.tensor_tensor(oh_w[q][:], oh_s[q][:], sc[2].to_broadcast([P, P, U]), ALU.mult))
            need("pe", t_oh)
            st = (g // STRIP) % 2
            if g % STRIP == 0:
                need("act", strip_free[st])
                if (g // STRIP) == NSTR - 1:
                    need("dve", strip_free[st])
                    need("act", V(vec.memset(strip[st][:], 0)))
            a_toks = []
            for w in range(GW):
                ab = AB[w // 4]
                if w % 4 == 0:
                    need("pe", free[ab])
                if w % 2 == 0:
                    hk = HB[hb % 5]
                    hb += 1
                    need("pe", free[hk])
                ao = bank[ab][:, (w % 4) * WCOL:(w % 4 + 1) * WCOL]
                ho = bank[hk][:, (w % 2) * HC:(w % 2 + 1) * HC]
                for j in range(SLOTS):
                    u = j * GW + w
                    for half in range(2):
                        rhs = oh_c[q][:, :, u].rearrange("p (d h s) -> p d h s", h=2, s=NT)[:, :, half, :]
                        t_a = pe.matmul(ao, oh_s[q][:, :, u], rhs, start=(j == 0 and half == 0),
                                        stop=(j == SLOTS - 1 and half == 1))
                    t_h = pe.matmul(ho, oh_w[q][:, :, u], oh_c[q][:, :, u], start=(j == 0), stop=(j == SLOTS - 1))
                if w % 4 == 3:
                    t_pa = T(t_a)
                if w % 2 == 1:
                    t_ph = T(t_h)
                    need("act", t_ph)
                    d0 = (g % STRIP) * GW * WN + (w - 1) * WN
                    o = strip[st][:, :, d0:d0 + 2 * WN].bitcast(U16).rearrange("p s (x h) -> p x h s", h=2)
                    free[hk] = S(act.activation(o, bank[hk][:, 0:2 * HC].rearrange(
                        "p (x h s) -> p x h s", h=2, s=NT), ACT.Copy))
                if w % 4 == 3:
                    need("act", t_pa)
                    d0 = g * GW * WN + (w - 3) * WN
                    free[ab] = S(act.activation(
                        A[:, :, d0:d0 + 4 * WN].rearrange("p s x -> p x s"),
                        bank[ab][:, 0:4 * WCOL].rearrange("p (x s) -> p x s", s=NT), ACT.Copy, scale=COUNT_SCALE,
                        saturate=False))
            used[q] = (done["pe"], count["pe"])
            t_a_evac = (done["act"], count["act"])
            need("pool", t_a_evac)
            if g % STRIP == 1 and g > STRIP:
                with_strip(g // STRIP - 1, evacuated[g - 2])
            evacuated[g] = t_a_evac
            if g % STRIP == STRIP - 1 or g == NG - 1:
                j = g // STRIP
                need("sp", t_a_evac)
                strip_free[st] = dma("sp", f"strip{st}", pd.rearrange("(i p) n -> p i n", p=P)[:, :, j * SW:(j + 1) * SW],
                                     strip[st][:])
                packed_out = [strip_free[0], strip_free[1]]

        chk = sbuf(c1, "chk", [P, 2], F32)
        chr_ = sbuf(c1, "chr", [1, 4], F32)
        with_strip(NSTR - 1, evacuated[NG - 1])
        need("sp", free[DB])
        t_deg = dma("sp", "deg_out", deg_row.rearrange("(a n) -> a n", a=1), degs[:, 0:N])
        v(vec.tensor_scalar(codes[:], codes[:], 6, 0x01010101, ALU.logical_shift_right, ALU.bitwise_and))
        v(vec.tensor_copy(found[:].bitcast(F32), codes[:]))
        v(vec.tensor_reduce(chk[:, 0:1], found[:].bitcast(F32), axis=AX.XY, op=ALU.max))
        need("pe", (done["dve"], count["dve"]), free[DB], free[6])
        pe.matmul(bank[7][0:1, 0:1], hits[:], ones_f[:, 0:1], start=True, stop=True)
        t = T(pe.transpose(bank[6][0:1, 0:P], chk[:, 0:1], ident[:]))
        need("dve", t)
        v(vec.tensor_reduce(chr_[:, 0:1], bank[6][0:1, 0:P], axis=AX.X, op=ALU.max))
        v(vec.tensor_scalar(chr_[:, 1:2], chr_[:, 0:1], 0.0, None, ALU.is_equal))
        v(vec.tensor_scalar(chr_[:, 2:3], bank[7][0:1, 0:1], float(E), None, ALU.is_equal))
        v(vec.tensor_tensor(flag[:], chr_[:, 1:2], chr_[:, 2:3], ALU.mult))
        need("sp", t_deg, *packed_out)
        barrier()

    def node_rows(ap):
        full = (NT - 1) * P
        return ap[0:full, :].rearrange("(i p) f -> p i f", p=P), ap[full:N, :]

    bank_free = [None] * 8
    sym_written = []
    fast = True

    def feature_pair(ctx, name, width=D):
        if fast:
            return sbuf(ctx, name, [P, 2, NT, width], F16)
        return sbuf(ctx, name, [P, NT, width], F32)[:]

    def count_scale():
        return COUNT_SCALE if fast else 1.0

    def sum_all(nm):
        if not fast:
            scatter_sum(nm, sums, [("src", "to_dst")])

    def now(k):
        return done[k], count[k]

    def v(inst):
        t_ = V(inst)
        need("dve", t_)
        return t_

    def rows_of(i):
        return P if i < NT - 1 else TAIL

    def tiles_of(ch):
        c, cw = ch
        return [(c // P + k, k) for k in range(-(-cw // P))]

    LT = 4

    def layer_norm(ctx, hn, h16=None, residual=False, among=()):
        groups = [slice(i, min(i + LT, NT)) for i in range(0, NT, LT)]
        sq_ = [sbuf(ctx, f"ln_sq{i}", [P, LT, D], F32) for i in range(2)]
        st_ = sbuf(ctx, "ln_st", [P, 3, NT], F32)
        need("dve", *t_x)
        tok, t_hn, t_h = {}, {}, {}

        def wide(g, r):
            return st_[:, r, groups[g], None].to_broadcast([P, groups[g].stop - groups[g].start, D])

        def square(g):
            return sq_[g % 2][:, 0:groups[g].stop - groups[g].start, :]

        def center(g):
            s = groups[g]
            v(vec.tensor_reduce(st_[:, 0, s], xn[:, s, :], axis=AX.X, op=ALU.add))
            v(vec.tensor_scalar(st_[:, 0, s], st_[:, 0, s], 1.0 / D, None, ALU.mult))
            need("act", v(vec.tensor_tensor(hn[:, s, :], xn[:, s, :], wide(g, 0), ALU.subtract)), tok.get(("sum", g - 2)))
            tok[("sq", g)] = S(act.activation(square(g), hn[:, s, :], ACT.Square))

        def variance(g):
            s = groups[g]
            need("dve", tok[("sq", g)])
            tok[("sum", g)] = v(vec.tensor_reduce(st_[:, 1, s], square(g), axis=AX.X, op=ALU.add))
            need("act", v(vec.tensor_scalar(st_[:, 1, s], st_[:, 1, s], 1.0 / D, EPS, ALU.mult, ALU.add)))
            tok[("sd", g)] = S(act.activation(st_[:, 2, s], st_[:, 1, s], ACT.Sqrt))

        def scale(g):
            s = groups[g]
            need("dve", tok[("sd", g)])
            v(vec.reciprocal(st_[:, 2, s], st_[:, 2, s]))
            t_hn[g] = v(vec.scalar_tensor_tensor(hn[:, s, :], hn[:, s, :], 0.0, wide(g, 2), ALU.max, ALU.mult))
            if h16 is not None and fast:
                need("act", t_hn[g])
                tok[("hi", g)] = S(act.activation(h16[:, 0, s, :], hn[:, s, :], ACT.Copy, scale=FIXED))

        def low(g):
            s = groups[g]
            if h16 is not None:
                if fast:
                    need("dve", tok[("hi", g)])
                    t0 = v(vec.scalar_tensor_tensor(h16[:, 1, s, :], hn[:, s, :], FIXED, h16[:, 0, s, :], ALU.mult, ALU.subtract))
                    t0 = [tok[("hi", g)], t0]
                else:
                    t0 = [v(vec.tensor_scalar(h16[:, s, :], hn[:, s, :], FIXED, None, ALU.mult))]
                t_h.update({i: t0 for i in range(s.start, s.stop)})
            if residual:
                v(vec.tensor_tensor(xn[:, s, :], xn[:, s, :], hn[:, s, :], ALU.add))

        stages = [center, variance, scale, low]
        for x_ in range(len(groups) + len(stages) - 1):
            if x_ in among:
                among[x_]()
            for y_, stage in enumerate(stages):
                if 0 <= x_ - y_ < len(groups):
                    stage(x_ - y_)
        return t_hn, t_h

    def to_feature_rows(ht, hn, t_hn):
        toks = []
        for i0 in range(0, NT, LT):
            k = 6 + (i0 // LT) % 2
            need("pe", bank_free[k], t_hn[i0 // LT])
            w_ = 0
            for i in range(i0, min(i0 + LT, NT)):
                r_ = rows_of(i)
                tt = pe.transpose(bank[k][:, w_:w_ + r_], hn[0:r_, i, :], ident[0:r_, 0:r_])
                w_ += r_
            need("act", T(tt))
            bank_free[k] = S(act.activation(ht[:, i0 * P:i0 * P + w_], bank[k][:, 0:w_], ACT.Copy))
            toks.append(bank_free[k])
        return toks[-1]

    def sum_edges(bk, h16, ch, tok, before=None, aside=None, gate=None):
        if not fast:
            need("pe", *tok.values())
            return load_sums(bk, sums, 0, ch)
        c, cw = ch
        need("pe", bank_free[bk])
        for i in range(NT):
            if before and i in before:
                before[i]()
            need("pe", tok[i])
            if gate is not None and i in (3, 7, 11, 15, 19):
                step(gate)
            if aside is not None and i % 3 == 2:
                step(aside)
            for part in range(2):
                m = pe.matmul(bank[bk][:, 0:cw], h16[:, part, i, :], A[:, i, c:c + cw],
                              start=(i == 0 and part == 0), stop=(i == NT - 1 and part == 1))
        return T(m)

    def node_tiles_to_bank(bk, src_, ch):
        need("pe", bank_free[bk])
        for i, k in tiles_of(ch):
            r_ = rows_of(i)
            m = pe.transpose(bank[bk][0:r_, k * P:k * P + P], src_[:, k * P:k * P + r_], ident[:])
        return T(m)

    def chunk_rows(ch):
        ts = tiles_of(ch)
        return rows_of(ts[-1][0]), ts[0][0], len(ts)

    def add_to_x(bk, ch, tok):
        r_, i0, n_ = chunk_rows(ch)
        need("dve", tok)
        o = xn[0:r_, i0:i0 + n_, :]
        bank_free[bk] = V(vec.tensor_tensor(o, o, bank[bk][0:r_, 0:n_ * P].rearrange("p (i f) -> p i f", f=D), ALU.add))
        return bank_free[bk]

    def split_from_bank(bk, h16, ch, tok, scale):
        r_, i0, n_ = chunk_rows(ch)
        s3 = bank[bk][0:r_, 0:n_ * P].rearrange("p (i f) -> p i f", f=D)
        if not fast:
            need("dve", tok)
            bank_free[bk] = v(vec.tensor_scalar(h16[0:r_, i0:i0 + n_, :], s3, scale, None, ALU.mult))
            return [bank_free[bk]]
        hi, lo = (h16[0:r_, part, i0:i0 + n_, :] for part in range(2))
        need("act", tok)
        t1_ = S(act.activation(hi, s3, ACT.Copy, scale=scale))
        need("dve", tok, t1_)
        bank_free[bk] = V(vec.scalar_tensor_tensor(lo, s3, scale, hi, ALU.mult, ALU.subtract))
        return [t1_, bank_free[bk]]

    def power_scale(m, sc_, inv_, work):
        v(vec.tensor_scalar(work, m, 1e-15, None, ALU.max))
        v(vec.tensor_scalar(work.bitcast(I32), work.bitcast(I32), 0x7F800000, None, ALU.bitwise_and))
        v(vec.tensor_scalar(sc_.bitcast(I32), work.bitcast(I32), -1.0, float((127 + 14 + 127) << 23), ALU.mult, ALU.add))
        v(vec.tensor_scalar(inv_.bitcast(I32), work.bitcast(I32), float(14 << 23), None, ALU.subtract))

    weight_max = {}

    def weight_maxima(ctx):
        NLAY, PIECE = m_w1.shape[0], 2048
        part = weight_max["part"]
        stage = sbuf(ctx, "w_stage", [P, PIECE], F32)
        t0 = v(vec.memset(part[:], 0.0))
        for l in range(NLAY):
            for t, a in enumerate((m_w1[l].rearrange("e h f -> (e h f)"), m_w2[l].rearrange("e h f -> (e h f)"),
                                   m_ww[l].rearrange("e h f -> (e h f)"), m_b1[l].rearrange("e f -> (e f)"))):
                rows = a.rearrange("(p c) -> p c", p=P)
                for i, c_ in enumerate(range(0, rows.shape[1], PIECE)):
                    w_ = min(PIECE, rows.shape[1] - c_)
                    need("sp", t0)
                    t0 = dma("sp", "w_stage", stage[:, 0:w_], rows[:, c_:c_ + w_])
                    yield
                    need("dve", t0)
                    t0 = v(vec.tensor_reduce(part[:, t, l, i:i + 1], stage[:, 0:w_], axis=AX.X, op=ALU.max,
                                             apply_absolute_value=True))
                    yield

    def make_lists(ctx):
        e_ = {k: sbuf(ctx, "l_" + k, [EP, EC], I32) for k in ("src", "dst", "et", "rd", "rs")}
        padc = sbuf(ctx, "l_pad", [1, 2, ET * P - E], I32)
        v(vec.memset(padc[:, 0, :], 0))
        v(vec.memset(padc[:, 1, :], NREL * NP))
        need("dve", *[dma("sp", "l_in_" + k, e_[k][:], a.rearrange("(p c) -> p c", p=EP))
                      for k, a in (("src", src), ("dst", dst), ("et", et))])
        for o, k in (("rd", "dst"), ("rs", "src")):
            v(vec.scalar_tensor_tensor(e_[o][:], e_["et"][:], float(NP), e_[k][:], ALU.mult, ALU.add))
        need("sp", now("dve"))
        out_ = []
        for name, k, pd_ in (("src", "src", 0), ("dst", "dst", 0), ("to_dst", "dst", 1),
                             ("to_type_dst", "rd", 1), ("to_type_src", "rs", 1)):
            out_.append(dma("sp", "lo_" + name, lists[name][0:E].rearrange("(p c) -> p c", p=EP), e_[k][:]))
            out_.append(dma("sp", "lp_" + name, lists[name][E:ET * P].rearrange("(a n) -> a n", a=1), padc[:, pd_, :]))
        need("sp", *out_)
        barrier()

    loop_sems = []

    def scatter_sum(nm, target, passes):
        if not loop_sems:
            loop_sems.extend(top.enter_context(nc.semaphore("loop_" + k)) for k in ("dve", "pe", "feat", "sum", "put"))
        s_dve, s_pe, s_feat, s_sum, s_put = loop_sems
        with scope() as c:
            at = [4 * D]

            def take(width, dtype=F32):
                at[0] += width
                r = room[:, at[0] - width:at[0]]
                return r if dtype is F32 else r.bitcast(dtype)

            zero = take(NT * D)
            frm, to = take(ET, I32), take(ET, I32)
            low = take(P)
            spare = take(1)
            gi, si, wi = (take(1, I32) for _ in range(3))
            sf, rep = take(1), take(1)
            wide_, eq, before, msg, cur, new = (take(P) for _ in range(6))
            if nm is None:
                v(vec.memset(zero[:], 1.0))
                need("sp", now("dve"))
                t0 = dma("sp", "z_feat", feat.rearrange("(i p) f -> p i f", p=P), zero[:].rearrange("p (i f) -> p i f", f=D))
            else:
                need("sp", now("dve"), now("act"))
                t0 = dma("sp", "z_feat", feat.rearrange("(i p) f -> p i f", p=P), nm)
            need("dve", t0)
            need("sp", t0)
            v(vec.memset(zero[:], 0.0))
            need("sp", now("dve"))
            for r0 in range(0, NREL * NP, NP):
                need("sp", dma("sp", "z_zero", target[r0:r0 + NP, :].rearrange("(i p) f -> p i f", p=P),
                               zero[:].rearrange("p (i f) -> p i f", f=D)))
            need("sp", dma("sp", "z_zero", target[NREL * NP:SUMS, :], zero[:, 0:D]))
            need("pool", G(pool.affine_select(out=low[:], in_=ones_f[:], compare_op=ALU.is_gt, fill=0.0, base=0,
                                              pattern=[[-1, P]], channel_multiplier=1)))
            need("pool", G(pool.iota(spare[:], pattern=[[0, 1]], base=NREL * NP, channel_multiplier=1,
                                     allow_small_or_imprecise_dtypes=True)))
            for from_, to_ in passes:
                barrier()
                t0 = [dma("sp", "z_from", frm[:], lists[from_].rearrange("(p t) -> p t", p=P)),
                      dma("sp", "z_to", to[:], lists[to_].rearrange("(p t) -> p t", p=P))]
                need("sp", *t0)
                barrier()
                with nc.Fori(0, ET) as t_:
                    vec.tensor_copy(gi[:], frm[:, bass.ds(t_, 1)]).then_inc(s_dve, 1)
                    vec.tensor_copy(si[:], to[:, bass.ds(t_, 1)]).then_inc(s_dve, 1)
                    vec.wait_ge(s_dve, 2)
                    vec.tensor_copy(sf[:], si[:]).then_inc(s_dve, 1)
                    vec.wait_ge(s_dve, 3)
                    vec.tensor_copy(wide_[:], sf[:, 0:1].to_broadcast([P, P])).then_inc(s_dve, 1)
                    pool.wait_ge(s_dve, 2)
                    pool.indirect_dma_start(out=msg[:], out_offset=None, in_=feat,
                                            in_offset=bass.IndirectOffsetOnAxis(ap=gi[:], axis=0)).then_inc(s_feat, 16)
                    pool.indirect_dma_start(out=cur[:], out_offset=None, in_=target,
                                            in_offset=bass.IndirectOffsetOnAxis(ap=si[:], axis=0)).then_inc(s_sum, 16)
                    pe.wait_ge(s_dve, 4)
                    pe.matmul(bank[0][:, 0:P], wide_[:], ident[:], start=True, stop=True).then_inc(s_pe, 1)
                    vec.wait_ge(s_pe, 1)
                    vec.tensor_scalar(eq[:], bank[0][:, 0:P], sf[:, 0:1], None, ALU.is_equal).then_inc(s_dve, 1)
                    vec.wait_ge(s_dve, 5)
                    vec.tensor_tensor(before[:], eq[:], low[:], ALU.mult).then_inc(s_dve, 1)
                    vec.wait_ge(s_dve, 6)
                    vec.tensor_reduce(rep[:], before[:], axis=AX.X, op=ALU.max).then_inc(s_dve, 1)
                    vec.wait_ge(s_dve, 7)
                    vec.scalar_tensor_tensor(before[:, 0:1], spare[:], sf[:, 0:1], rep[:], ALU.subtract, ALU.mult).then_inc(s_dve, 1)
                    vec.wait_ge(s_dve, 8)
                    vec.tensor_tensor(wi[:], before[:, 0:1], sf[:], ALU.add).then_inc(s_dve, 1)
                    pe.wait_ge(s_dve, 9)
                    pe.wait_ge(s_feat, 16)
                    pe.matmul(bank[1][:, 0:P], eq[:], msg[:], start=True, stop=True).then_inc(s_pe, 1)
                    vec.wait_ge(s_pe, 2)
                    vec.wait_ge(s_sum, 16)
                    vec.tensor_tensor(new[:], bank[1][:, 0:P], cur[:], ALU.add).then_inc(s_dve, 1)
                    pool.wait_ge(s_dve, 10)
                    pool.indirect_dma_start(out=target, out_offset=bass.IndirectOffsetOnAxis(ap=wi[:], axis=0),
                                            in_=new[:], in_offset=None).then_inc(s_put, 16)
                    pool.wait_ge(s_put, 16)
                    pool.wait_ge(s_feat, 16)
                    pool.wait_ge(s_sum, 16)
                    barrier()
                    pool.dma_reset(range(s_feat.num, s_put.num + 1))
                    for s in loop_sems:
                        pool.sem_clear(s)
                    barrier()
            barrier()

    chunk_buf = {}

    def load_sums(bk, table, r0, ch, at_col=0):
        buf_ = chunk_buf["buf"]
        need("sp", chunk_buf.get("free"))
        R_, i0, n_ = chunk_rows(ch)
        a = r0 + i0 * P
        if n_ > 1:
            t0 = dma("sp", "z_chunk", buf_[:, 0:n_, :], table[a:a + n_ * P, :].rearrange("(i p) f -> p i f", p=P))
        else:
            t0 = dma("sp", "z_chunk", buf_[0:R_, 0, :], table[a:a + R_, :])
        need("pe", t0, bank_free[bk])
        for i, k in tiles_of(ch):
            r_ = rows_of(i)
            m = pe.transpose(bank[bk][:, at_col + k * P:at_col + k * P + r_], buf_[0:r_, k, :], ident[0:r_, 0:r_])
        chunk_buf["free"] = T(m)
        return chunk_buf["free"]

    def degrees():
        with scope() as c1:
            nd = sbuf(c1, "nd", [EP, 3, N // EP], F32)
            t = None
            if not fast:
                scatter_sum(None, sums, [("src", "to_dst")])
                t = dma("sp", "deg_out", deg_row.rearrange("(p c) -> p c", p=EP),
                        bass.AP(sums.tensor, 0, [[N // EP * D, EP], [D, N // EP]]), allow_slow_non_contiguous=True)
            need("sp", t)
            t = dma("sp", "deg_in", nd[:, 0, :], deg_row.rearrange("(p c) -> p c", p=EP))
            need("dve", t)
            v(vec.tensor_scalar(nd[:, 1, :], nd[:, 0, :], 1.0, None, ALU.add))
            need("act", now("dve"))
            need("dve", S(act.activation(nd[:, 1, :], nd[:, 1, :], ACT.Sqrt)))
            v(vec.tensor_scalar(nd[:, 2, :], nd[:, 0, :], 1.0, None, ALU.max))
            v(vec.reciprocal(nd[:, 1:3, :], nd[:, 1:3, :]))
            need("sp", now("dve"))
            need("sp", dma("sp", "dinv_out", dinv_row.rearrange("(p c) -> p c", p=EP), nd[:, 1, :]),
                 dma("sp", "invd_out", invd_row.rearrange("(p c) -> p c", p=EP), nd[:, 2, :]))
            barrier()

    def symmetric_steps(ctx):
        cuts = [(0, 7), (7, 6), (13, 6), (19, 6)]
        pieces = [(j, i0, n_) for j in range(NT) for i0, n_ in cuts]
        R = 3
        rs = [sbuf(ctx, f"sym_rows{r}", [P, 7 * P], I32) for r in range(R)]
        cs = [sbuf(ctx, f"sym_cols{r}", [P, 7, P], I32) for r in range(R)]
        pdv = pd.rearrange("(i p) n -> p i n", p=P)
        sdv = sd.rearrange("(i p) n -> p i n", p=P)
        rows_free, cols_free, loaded = [None] * R, [None] * R, {}

        def load(n):
            if n >= len(pieces):
                return
            j, i0, n_ = pieces[n]
            r = n % R
            need("sp", rows_free[r])
            t_r = dma("sp", f"sym_r{r}", rs[r][:, 0:n_ * P], pd[j * P:(j + 1) * P, i0 * P:(i0 + n_) * P])
            need("sp", cols_free[r])
            loaded[n] = t_r, dma("sp", f"sym_c{r}", cs[r][:, 0:n_, :], pdv[:, i0:i0 + n_, j * P:(j + 1) * P])

        load(0)
        load(1)
        for n, (j, i0, n_) in enumerate(pieces):
            r = n % R
            load(n + 2)
            yield
            t_r, t_c = loaded.pop(n)
            need("pe", t_r)
            need("dve", t_c)
            for g0 in range(0, n_, 4):
                k = 6 + (g0 // 4) % 2
                g = min(4, n_ - g0)
                need("pe", bank_free[k])
                for i in range(g):
                    m = pe.transpose(bank[k][:, i * P:(i + 1) * P], rs[r][:, (g0 + i) * P:(g0 + i + 1) * P].bitcast(F32), ident[:])
                t_t = rows_free[r] = T(m)
                need("dve", t_t)
                o = cs[r][:, g0:g0 + g, :].rearrange("p i n -> p (i n)").bitcast(U16)
                bank_free[k] = V(vec.tensor_tensor(o, o, bank[k][:, 0:g * P].bitcast(U16), ALU.add))
                if g0 + 4 < n_:
                    yield
            need("sp", bank_free[k], bank_free[6 + (k + 1) % 2])
            cols_free[r] = dma("sp", f"sym_o{r}", sdv[:, i0:i0 + n_, j * P:(j + 1) * P], cs[r][:, 0:n_, :])
        sym_written.extend(cols_free)
        yield

    aside = {}

    def step(bg):
        next(bg, None)

    def block_gru():
        with scope() as c:
            hn = sbuf(c, "g_hn", [P, NT, D], F32)
            NL = g_w.shape[0]
            h16 = [feature_pair(c, f"g_h16{i}") for i in range(2)]
            ht = sbuf(c, "g_ht", [P, N], F32)
            wl = sbuf(c, "g_wl", [P, NL, D], F32)
            wt = {}
            raw = sbuf(c, "g_raw", [P, 3, D], F32)
            bb = sbuf(c, "g_b", [P, 3, 3], F32)
            t_wl = dma("act", "g_wl", wl[:], g_w.rearrange("l i o -> i l o"))
            t_b = [dma("act", "g_bi", bb[:, 0, :], g_bih.rearrange("(b o) -> o b", o=P), allow_slow_non_contiguous=True),
                   dma("act", "g_bh", bb[:, 1, :], g_bhh.rearrange("(b o) -> o b", o=P), allow_slow_non_contiguous=True)]
            t_tr = None
            for n_, a in (("ih", g_ih), ("hh", g_hh)):
                wt[n_] = sbuf(c, "g_w" + n_, [P, 3, D], F32)
                need("act", t_tr)
                t_raw = dma("act", "g_raw", raw[:], a.rearrange("(b o) i -> o b i", o=P))
                need("pe", t_raw, bank_free[7])
                for b in range(3):
                    m = pe.transpose(bank[7][:, b * P:(b + 1) * P], raw[:, b, :], ident[:])
                t_tr = T(m)
                need("act", t_tr)
                bank_free[7] = t_w = S(act.activation(wt[n_][:], bank[7][:, 0:3 * P].rearrange("p (b o) -> p b o", b=3), ACT.Copy))
            t_hn, tok = layer_norm(c, hn, h16[0], residual=True)
            need("dve", *t_b)
            t_bb = v(vec.tensor_tensor(bb[:, 2, :], bb[:, 0, :], bb[:, 1, :], ALU.add))
            v(vec.memset(h16[1][:, :, NT - 1, :] if fast else h16[1][:, NT - 1, :], 0.0))
            buf = {n_: [sbuf(c, f"g_{n_}{i}", [P, BANK], F32) for i in range(2)] for n_ in ("ag", "m", "r", "z", "t", "n")}
            bg = aside["steps"]
            BR, BZ, BI, BH, BM, BT = 2, 3, 4, 5, 6, 7
            last_use = {}

            def gate(ci, l, t_agg, new):
                c_, cw = CH[ci]
                q = ci % 2
                ag, m_, r_, z_, t_, n_ = (buf[b][q][:, 0:cw] for b in ("ag", "m", "r", "z", "t", "n"))
                h_ = ht[:, c_:c_ + cw]
                need("act", t_agg, last_use.get(("pe", q)))
                bank_free[q] = t0 = S(act.activation(ag, bank[q][:, 0:cw], ACT.Copy, scale=1.0 / FIXED / count_scale()))
                yield
                need("pe", t0, bank_free[BM])
                t0 = T(pe.matmul(bank[BM][:, 0:cw], wl[:, l, :], ag, start=True, stop=True))
                need("act", t0)
                bank_free[BM] = t_m = S(act.activation(m_, bank[BM][:, 0:cw], ACT.Copy))
                need("pe", bank_free[BR], bank_free[BZ], bank_free[BI], bank_free[BH])
                pe.matmul(bank[BR][:, 0:cw], wt["hh"][:, 0, :], h_, start=True, stop=False)
                pe.matmul(bank[BZ][:, 0:cw], wt["hh"][:, 1, :], h_, start=True, stop=False)
                t_hh = T(pe.matmul(bank[BH][:, 0:cw], wt["hh"][:, 2, :], h_, start=True, stop=True))
                yield
                need("pe", t_m)
                t_r = T(pe.matmul(bank[BR][:, 0:cw], wt["ih"][:, 0, :], m_, start=False, stop=True))
                t_z = T(pe.matmul(bank[BZ][:, 0:cw], wt["ih"][:, 1, :], m_, start=False, stop=True))
                t_i = T(pe.matmul(bank[BI][:, 0:cw], wt["ih"][:, 2, :], m_, start=True, stop=True))
                last_use[("pe", q)] = t_i
                need("act", t_r, last_use.get(("dve", q)))
                bank_free[BR] = t0 = S(act.activation(r_, bank[BR][:, 0:cw], ACT.Sigmoid, bias=bb[:, 2, 0:1]))
                need("act", t_z)
                bank_free[BZ] = t_zz = S(act.activation(z_, bank[BZ][:, 0:cw], ACT.Sigmoid, bias=bb[:, 2, 1:2]))
                need("dve", t0, t_hh)
                bank_free[BH] = v(vec.scalar_tensor_tensor(t_, bank[BH][:, 0:cw], bb[:, 1, 2:3], r_, ALU.add, ALU.mult))
                need("dve", t_i)
                bank_free[BI] = t0 = v(vec.tensor_tensor(t_, t_, bank[BI][:, 0:cw], ALU.add))
                need("act", t0)
                t0 = S(act.activation(n_, t_, ACT.Tanh, bias=bb[:, 0, 2:3]))
                need("dve", t0)
                v(vec.tensor_tensor(t_, h_, n_, ALU.subtract))
                need("dve", t_zz)
                v(vec.tensor_tensor(t_, t_, z_, ALU.mult))
                last_use[("dve", q)] = t0 = v(vec.tensor_tensor(h_, t_, n_, ALU.add))
                new[ci] = t0

            def finish(ci, l, t_new, toks):
                need("pe", t_new)
                c_, cw = CH[ci]
                t0 = node_tiles_to_bank(BT, ht[:, c_:c_ + cw], CH[ci])
                if l == NL - 1:
                    add_to_x(BT, CH[ci], t0)
                else:
                    t0 = split_from_bank(BT, h16[(l + 1) % 2], CH[ci], t0, FIXED)
                    toks.update({i: t0 for i, _ in tiles_of(CH[ci])})

            LC = len(CH) - 1
            for l in range(NL):
                toks = {}
                new = {}
                cur, nxt = h16[l % 2], h16[(l + 1) % 2]
                if l == 0 or not fast:
                    sum_all(cur)
                    t_agg = {0: sum_edges(0, cur, CH[0], tok)}
                if l == 0:
                    t_ht = to_feature_rows(ht, hn, t_hn)
                    need("pe", t_wl, t_w, t_ht)
                    need("act", t_bb)
                    need("dve", t_ht)
                for ci in range(len(CH)):
                    cell = gate(ci, l, t_agg[ci], new)
                    if ci < LC:
                        t_agg[ci + 1] = sum_edges((ci + 1) % 2, cur, CH[ci + 1], tok, aside=bg, gate=cell)
                    for _ in cell:
                        pass
                    if 0 < ci < LC:
                        finish(ci - 1, l, new[ci - 1], toks)
                last_two = [lambda c=c: finish(c, l, new[c], toks) for c in (LC - 1, LC)]
                if fast and l < NL - 1:
                    t_agg = {0: sum_edges(0, nxt, CH[0], toks, aside=bg, before={
                        tiles_of(CH[LC - 1])[0][0]: last_two[0], tiles_of(CH[LC])[0][0]: last_two[1]})}
                else:
                    last_two[0]()
                    last_two[1]()
                tok = toks
            barrier()

    def block_gcn():
        with scope() as c:
            hn = sbuf(c, "c_hn", [P, NT, D], F32)
            h16 = feature_pair(c, "c_h16")
            yt = sbuf(c, "c_yt", [P, N], F32)
            dinv = sbuf(c, "c_dinv", [P, N], F32)
            w01 = [sbuf(c, f"c_w{i}", [P, D], F32) for i in range(2)]
            b01 = sbuf(c, "c_b", [P, 2], F32)
            mx = sbuf(c, "c_mx", [P, len(CH)], F32)
            sc = sbuf(c, "c_sc", [P, 4], F32)
            buf = {n_: [sbuf(c, f"c_{n_}{i}", [P, BANK], F32) for i in range(2)] for n_ in ("ag", "t", "o")}
            ld = [dma("sp", "c_w0", w01[0][:], c_w0), dma("sp", "c_w1", w01[1][:], c_w1),
                  dma("act", "c_b0", b01[:, 0:1], c_b0.rearrange("(p a) -> p a", a=1)),
                  dma("act", "c_b1", b01[:, 1:2], c_b1.rearrange("(p a) -> p a", a=1)),
                  dma("sp", "c_dinv", dinv[:], bass.AP(dinv_row.tensor, 0, [[0, P], [1, N]]))]
            _, tok = layer_norm(c, hn, h16)
            for k in ("pe", "act", "dve"):
                need(k, *ld)
            use = {}
            sum_all(h16)
            t_agg = {0: sum_edges(0, h16, CH[0], tok)}
            for ci, (c_, cw) in enumerate(CH):
                if ci + 1 < len(CH):
                    t_agg[ci + 1] = sum_edges((ci + 1) % 2, h16, CH[ci + 1], tok, aside=aside["steps"])
                q = ci % 2
                ag, t_ = buf["ag"][q][:, 0:cw], buf["t"][q][:, 0:cw]
                y_ = yt[:, c_:c_ + cw]
                need("act", t_agg[ci], use.get(("ag", q)), use.get(("t", q)))
                bank_free[q] = t0 = S(act.activation(ag, bank[q][:, 0:cw], ACT.Copy, scale=1.0 / FIXED / count_scale()))
                need("pe", t0, bank_free[2 + q])
                use[("ag", q)] = t0 = T(pe.matmul(bank[2 + q][:, 0:cw], w01[0][:], ag, start=True, stop=True))
                need("act", t0)
                bank_free[2 + q] = t0 = S(act.activation(t_, bank[2 + q][:, 0:cw], ACT.Identity, bias=b01[:, 0:1]))
                need("dve", t0)
                use[("t", q)] = v(vec.tensor_tensor(y_, t_, dinv[:, c_:c_ + cw], ALU.mult))
                v(vec.tensor_reduce(mx[:, ci:ci + 1], y_, axis=AX.X, op=ALU.max, apply_absolute_value=True))
            v(vec.tensor_reduce(sc[:, 0:1], mx[:], axis=AX.X, op=ALU.max))
            power_scale(sc[:, 0:1], sc[:, 1:2], sc[:, 2:3], sc[:, 3:4])
            v(vec.tensor_scalar(sc[:, 3:4], sc[:, 2:3], 1.0 / count_scale(), None, ALU.mult))
            t_h = [(done["pe"], count["pe"])]
            toks = {}

            def scaled_again(ci):
                c_, cw = CH[ci]
                q = ci % 2
                t_ = buf["t"][q][:, 0:cw]
                need("dve", use.get(("tr", q)))
                t0 = v(vec.tensor_scalar(t_, yt[:, c_:c_ + cw], sc[:, 1:2], None, ALU.mult))
                need("pe", t0)
                t0 = use[("tr", q)] = node_tiles_to_bank(6 + q, t_, CH[ci])
                need("act", t_h)
                t0 = split_from_bank(6 + q, h16, CH[ci], t0, 1.0)
                toks.update({i: t0 for i, _ in tiles_of(CH[ci])})

            ahead = 2 if fast else len(CH)
            for ci in range(ahead):
                scaled_again(ci)
            sum_all(h16)
            t_agg = {0: sum_edges(0, h16, CH[0], toks, before={
                tiles_of(CH[ci - 1])[0][0]: lambda ci=ci: scaled_again(ci) for ci in range(ahead, len(CH))})}
            for ci, (c_, cw) in enumerate(CH):
                if ci + 1 < len(CH):
                    t_agg[ci + 1] = sum_edges((ci + 1) % 2, h16, CH[ci + 1], toks, aside=aside["steps"])
                q = ci % 2
                ag, o_ = buf["ag"][q][:, 0:cw], buf["o"][q][:, 0:cw]
                need("dve", t_agg[ci], use.get(("ag", q)))
                bank_free[q] = v(vec.scalar_tensor_tensor(ag, bank[q][:, 0:cw], sc[:, 3:4], yt[:, c_:c_ + cw],
                                                          ALU.mult, ALU.add))
                t0 = v(vec.tensor_tensor(ag, ag, dinv[:, c_:c_ + cw], ALU.mult))
                need("pe", t0, bank_free[2 + q])
                use[("ag", q)] = t0 = T(pe.matmul(bank[2 + q][:, 0:cw], w01[1][:], ag, start=True, stop=True))
                need("act", t0, use.get(("o", q)))
                bank_free[2 + q] = t0 = S(act.activation(o_, bank[2 + q][:, 0:cw], ACT.Identity, bias=b01[:, 1:2]))
                need("pe", t0)
                use[("o", q)] = t0 = node_tiles_to_bank(6 + q, o_, CH[ci])
                add_to_x(6 + q, CH[ci], t0)
            barrier()

    def block_relations():
        PT = 5
        RW = BANK // 2
        WRING, RING = 4, 3
        ACT_PIECES = (3 * PT,)
        CR = [(c, min(RW, N - c)) for c in range(0, N, RW)]
        with scope() as c:
            hn = sbuf(c, "r_hn", [P, NT, D], F32)
            h16 = feature_pair(c, "r_h16")
            ht = sbuf(c, "r_ht", [P, N], F32)
            wr = sbuf(c, "r_w", [P, NREL, D], F32)
            ws = sbuf(c, "r_ws", [P, D], F32)
            wd = [sbuf(c, f"r_wd{i}", [P, PT, RW], I32) for i in range(WRING)]
            f8 = [sbuf(c, f"r_f8{i}", [P, PT, 4 * RW], F8) for i in range(RING)]
            acc = [sbuf(c, f"r_acc{i}", [P, 2, RW], I32) for i in range(2)]
            accb = sbuf(c, "r_accb", [P, 2, 4 * RW], BF16)
            dg = sbuf(c, "r_dg", [P, 2, 4], F32)
            ags = sbuf(c, "r_ags", [P, 4, RW], F32)
            ld = [dma("sp", "r_wr", wr[:], r_w.rearrange("r i o -> i r o")), dma("sp", "r_ws", ws[:], r_self)]
            need("pe", t_onesb, *ld)
            if not fast:
                t_hn, t_h = layer_norm(c, hn, h16)
                need("pe", to_feature_rows(ht, hn, t_hn))
                both = [("src", "to_type_dst"), ("dst", "to_type_src")]
                scatter_sum(None, degs8, both)
                scatter_sum(h16, sums, both)
            sdv = sd.rearrange("(i p) n -> p i n", p=P)
            BD, BW, BS = 4, (5, 6), 7
            use = {}
            need("sp", *sym_written)

            def finish_unit(ch, h, t_mm, t_acc, pair, q):
                c_, cw = ch
                ts = tiles_of(ch)
                if fast:
                    need("act", t_mm, use.get("ags"))
                    for b in range(2):
                        bank_free[pair[b]] = t_ags = S(act.activation(
                            ags[:, 2 * b:2 * b + 2, 0:cw],
                            bank[pair[b]][:, 0:2 * cw].rearrange("p (k n) -> p k n", k=2), ACT.Copy, scale=1.0 / FIXED))
                    need("dve", t_acc, use.get("accb"))
                    use[("acc", q)] = t0 = v(vec.tensor_copy(accb[:, :, 0:4 * cw], acc[q][:, :, 0:cw].bitcast(U8)))
                    yield
                    need("pe", t0, bank_free[BD])
                    for i, t in ts:
                        r_ = rows_of(i)
                        for k in range(4):
                            for g_ in range(2):
                                m = pe.matmul(bank[BD][0:r_, 4 * t + k:4 * t + k + 1],
                                              accb[:, g_, 0:4 * cw].rearrange("p (n k) -> p n k", k=4)[:, t * P:t * P + r_, k],
                                              ones_bf[:, 0:1], start=(g_ == 0), stop=(g_ == 1))
                    use["accb"] = t0 = T(m)
                    need("dve", t0, use.get("dg"))
                    r_, _, n_ = chunk_rows(ch)
                    bank_free[BD] = v(vec.tensor_scalar(dg[0:r_, 0:n_, :], bank[BD][0:r_, 0:4 * n_].rearrange(
                        "p (t k) -> p t k", k=4), 1.0, None, ALU.max))
                else:
                    need("act", use.get("ags"))
                    for k in range(4):
                        t0 = load_sums(pair[k // 2], sums, (2 * k + h) * NP, ch, at_col=(k % 2) * cw)
                        need("act", t0)
                        bank_free[pair[k // 2]] = t_ags = S(act.activation(
                            ags[:, k, 0:cw], bank[pair[k // 2]][:, (k % 2) * cw:(k % 2 + 1) * cw], ACT.Copy, scale=1.0 / FIXED))
                    need("sp", use.get("dg"))
                    for i, t in ts:
                        r_ = rows_of(i)
                        for k in range(4):
                            row_ = (2 * k + h) * NP + i * P
                            need("dve", dma("sp", "r_dg", dg[0:r_, t, k:k + 1], degs8[row_:row_ + r_, 0:1],
                                            allow_slow_non_contiguous=True))
                            need("sp", (slots["r_dg"][0], slots["r_dg"][1]))
                    r_, _, n_ = chunk_rows(ch)
                    v(vec.tensor_scalar(dg[0:r_, 0:n_, :], dg[0:r_, 0:n_, :], 1.0, None, ALU.max))
                v(vec.reciprocal(dg[0:r_, 0:n_, :], dg[0:r_, 0:n_, :]))
                yield
                need("pe", t_ags)
                for i, t in ts:
                    r_ = rows_of(i)
                    b_ = BW[t]
                    need("pe", bank_free[b_])
                    for k in range(4):
                        m = pe.matmul(bank[b_][0:r_, k * D:(k + 1) * D], ags[:, k, t * P:t * P + r_], wr[:, 2 * k + h, :],
                                      start=True, stop=True)
                    use["ags"] = t0 = T(m)
                    need("dve", t0)
                    for k in range(4):
                        use["dg"] = bank_free[b_] = v(vec.scalar_tensor_tensor(
                            xn[0:r_, i, :], bank[b_][0:r_, k * D:(k + 1) * D], dg[0:r_, t, k:k + 1], xn[0:r_, i, :],
                            ALU.mult, ALU.add))
                    yield
                if h == 0:
                    need("pe", bank_free[BS])
                    for i, t in ts:
                        r_ = rows_of(i)
                        m = pe.matmul(bank[BS][0:r_, t * D:(t + 1) * D], ht[:, c_ + t * P:c_ + t * P + r_], ws[:],
                                      start=True, stop=True)
                    t0 = T(m)
                    need("dve", t0)
                    for i, t in ts:
                        r_ = rows_of(i)
                        bank_free[BS] = v(vec.tensor_tensor(xn[0:r_, i, :], xn[0:r_, i, :], bank[BS][0:r_, t * D:(t + 1) * D], ALU.add))
                yield

            tail = iter(())
            maxima = weight_maxima(c)
            units = [(ch, h) for ch in CR for h in range(2)]
            pieces = [(u, p0) for u in range(len(units) if fast else 0) for p0 in range(0, NT, PT)]
            ready, t_acc = {}, {}

            def fetch(n):
                if n < len(pieces):
                    u, p0 = pieces[n]
                    c_, cw = units[u][0]
                    q = n % WRING
                    need("sp", *use.get(("wd", q), ()))
                    ready[("wd", n)] = dma("sp", f"r_wd{q}", wd[q][:, :, 0:cw], sdv[:, p0:p0 + PT, c_:c_ + cw])

            def spread(n):
                if n >= len(pieces):
                    return
                u, p0 = pieces[n]
                (c_, cw), h = units[u]
                q, r, qa = n % WRING, n % RING, u % 2
                if p0 == 0:
                    need("pool", use.get(("acc", qa)))
                    need("pool", G(pool.memset(acc[qa][:], 0)))
                need("dve", ready.pop(("wd", n)))
                t0 = v(vec.tensor_scalar(wd[q][:, :, 0:cw], wd[q][:, :, 0:cw], 4 * h, 0x0F0F0F0F,
                                         ALU.logical_shift_right, ALU.bitwise_and))
                bytes_ = wd[q][:, :, 0:cw].bitcast(U8)
                if p0 in ACT_PIECES or n < 2:
                    need("act", t0, use.get(("f8", r)))
                    t1_ = S(act.activation(f8[r][:, :, 0:4 * cw], bytes_, ACT.Copy, saturate=False))
                else:
                    need("dve", use.get(("f8", r)))
                    t1_ = V(vec.tensor_copy(f8[r][:, :, 0:4 * cw], bytes_, saturate=False))
                need("pool", t0)
                for i in range(PT):
                    g_ = 0 if p0 + i < 13 else 1
                    t_acc[u] = G(pool.tensor_tensor(acc[qa][:, g_, 0:cw], acc[qa][:, g_, 0:cw], wd[q][:, i, 0:cw], ALU.add))
                    need("pool", t_acc[u])
                use[("wd", q)] = [t_acc[u], t1_]
                ready[("f8", n)] = t1_

            if not fast:
                for ch, h in units:
                    for _ in finish_unit(ch, h, None, None, (0, 1), 0):
                        pass
            else:
                for n in range(3):
                    fetch(n)
                t_hn, t_h = layer_norm(c, hn, h16, among={3: lambda: spread(0), 4: lambda: spread(1)})
            for n, (u, p0) in enumerate(pieces):
                (c_, cw), h = units[u]
                pair = (0, 1) if u % 2 == 0 else (2, 3)
                r = n % RING
                fetch(n + 3)
                need("pe", bank_free[pair[0]], bank_free[pair[1]], ready.pop(("f8", n)))
                if n == 2:
                    need("pe", to_feature_rows(ht, hn, t_hn))
                for i in range(PT):
                    need("pe", t_h[p0 + i])
                    f_ = f8[r][:, i, 0:4 * cw].rearrange("p (n k) -> p k n", k=4)
                    for part in range(2):
                        for b in range(2):
                            m = pe.matmul(bank[pair[b]][:, 0:2 * cw], h16[:, part, p0 + i, :], f_[:, 2 * b:2 * b + 2, :],
                                          start=(p0 + i == 0 and part == 0),
                                          stop=(p0 + i == NT - 1 and part == 1))
                use[("f8", r)] = t_mm = T(m)
                spread(n + 2)
                next(tail, None)
                if p0 in (0, 2 * PT):
                    step(maxima)
                if p0 + PT == NT:
                    for _ in tail:
                        pass
                    tail = finish_unit(units[u][0], h, t_mm, t_acc[u], pair, u % 2)
            for _ in tail:
                pass
            for _ in maxima:
                pass
            barrier()

    def block_experts():
        NLAY, H = m_rw.shape[0], m_win.shape[1]
        KB = H // P
        NWK, NSG = m_ww.shape[1], m_w1.shape[1]
        NE = NWK + NSG
        FB = m_w1.shape[3] // P
        with scope() as c:
            h2 = sbuf(c, "m_h", [P, NT, H], F32)
            bcast = sbuf(c, "m_bias", [P, NE * H], F32)
            agg = sbuf(c, "m_agg", [P, KB, BANK], F32)
            agg16 = sbuf(c, "m_agg16", [P, 2, KB, BANK], F16)
            hT = sbuf(c, "m_hT", [P, KB, BANK], F32)
            rw = sbuf(c, "m_rw", [P, 2 * KB, NE + 1], F32)
            rb = sbuf(c, "m_rb", [P, NE + 1], F32)
            sc = sbuf(c, "m_sc", [P, 4], F32)
            hmax = sbuf(c, "m_hmax", [P, len(CH)], F32)
            wout = sbuf(c, "m_wo", [P, KB, D], F32)
            bout = sbuf(c, "m_bo", [P, D], F32)
            prio = sbuf(c, "m_prio", [P, NE], F32)
            t_prio = G(pool.iota(prio[:], pattern=[[-1, NE]], base=NE, channel_multiplier=0,
                                 allow_small_or_imprecise_dtypes=True))
            t_wo = [dma("act", "m_wo", wout[:], m_wout.rearrange("(k p) o -> p k o", p=P)),
                    dma("act", "m_bo", bout[:], bass.AP(m_bout.tensor, m_bout.offset, [[0, P], [1, D]]))]
            NM = 4 * NLAY
            wmax, wsc, winv, wwork = (sbuf(c, f"m_wmax{i}", [P, NM], F32) for i in range(4))
            with scope() as c0:
                hn = sbuf(c0, "m_hn", [P, NT, D], F32)
                t_park = dma("sp", "park", xpark, xn[:].rearrange("p i f -> p (i f)"))
                win = sbuf(c0, "m_win", [P, H], F32)
                bin_ = sbuf(c0, "m_bin", [P, H], F32)
                xT = [sbuf(c0, f"m_xT{i}", [P, BANK], F32) for i in range(2)]
                ld = [dma("act", "m_win", win[:], m_win),
                      dma("act", "m_bin", bin_[:], bass.AP(m_bin.tensor, m_bin.offset, [[0, P], [1, H]]))]
                t_hn, _ = layer_norm(c0, hn)
                need("pe", *ld)
                need("dve", *ld)
                xt_free = [None, None]
                for i0 in range(0, NT, LT):
                    q = (i0 // LT) % 2
                    n_ = min(LT, NT - i0)
                    need("pe", bank_free[6 + q], t_hn[i0 // LT])
                    for k in range(n_):
                        m = pe.transpose(bank[6 + q][:, k * P:(k + 1) * P], hn[:, i0 + k, :], ident[:])
                    need("act", T(m), xt_free[q])
                    bank_free[6 + q] = t0 = S(act.activation(xT[q][:, 0:n_ * P], bank[6 + q][:, 0:n_ * P], ACT.Copy))
                    need("pe", t0)
                    for k in range(n_):
                        b_ = (i0 + k) % 6
                        need("pe", bank_free[b_])
                        xt_free[q] = t0 = T(pe.matmul(bank[b_][:, 0:H], xT[q][:, k * P:(k + 1) * P], win[:], start=True, stop=True))
                        need("dve", t0)
                        bank_free[b_] = V(vec.tensor_tensor(h2[:, i0 + k, :], bank[b_][:, 0:H], bin_[:], ALU.add))
                v(vec.tensor_reduce(wmax[:], weight_max["part"][:].rearrange("p t l i -> p (t l) i"), axis=AX.X, op=ALU.max))
                need("pe", now("dve"), bank_free[6], bank_free[7])
                t0 = T(pe.transpose(bank[6][0:NM, 0:P], wmax[:], ident[:]))
                need("dve", t0)
                v(vec.tensor_reduce(wwork[0:NM, 0:1], bank[6][0:NM, 0:P], axis=AX.X, op=ALU.max))
                v(vec.tensor_scalar(wsc[0:NM, :], ident[0:NM, 0:NM], wwork[0:NM, 0:1], None, ALU.mult))
                need("pe", now("dve"))
                t0 = T(pe.matmul(bank[7][:, 0:NM], ones_f[0:NM, :], wsc[0:NM, :], start=True, stop=True))
                need("dve", t0)
                v(vec.tensor_copy(wmax[:], bank[7][:, 0:NM]))
                power_scale(wmax[:], wsc[:], winv[:], wwork[:])
                bank_free[6] = bank_free[7] = now("dve")
                need("sp", t_park)
                barrier()
            with scope() as c0:
                h16 = feature_pair(c0, "m_h16", H)
                SL = 2 * BANK
                NPC = 2 * NSG + NWK // 2
                wroom = sbuf(c0, "m_weights", [P, NPC, SL], F32)
                b1 = sbuf(c0, "m_b1", [P, NSG * FB], F32)
                NSH = 6
                xroom = xn[:].rearrange("p i f -> p (i f)")
                sh = [xroom[:, i * BANK:(i + 1) * BANK].bitcast(F16) for i in range(NSH)]
                spare = xroom[:, (NSH - 2) * BANK:NSH * BANK]

                def loaded_piece(k):
                    return spare if k + 1 == NPC else wroom[:, k + 1, :]

                def pair_of(k, blocks):
                    return wroom[:, k, :].bitcast(F16).rearrange("p (x k f) -> p x k f", x=2, k=blocks)

                order = [("w1", 0), ("w1", 1), ("w2", 0), ("w2", 1), ("w1", 2), ("ww", 0), ("ww", 1), ("w2", 2), ("w1", 3), ("w2", 3)]
                piece_no = {p_: k for k, p_ in enumerate(order)}
                assert len(order) == NPC
                wtmp = sbuf(c0, "m_wtmp", [P, 2 * H], F32)
                tmp = [wtmp[:, i * H:(i + 1) * H] for i in range(2)]
                invd = sbuf(c0, "m_invd", [P, BANK], F32)
                rt = [sbuf(c0, f"m_rt{i}", [P, 4, NE], F32) for i in range(4)]
                small = xroom[:, NSH * BANK:]
                lg = small[:, 0:4 * (NE + 1)].rearrange("p (t e) -> p t e", e=NE + 1)
                sm = small[:, 36:76].rearrange("p (s t) -> p s t", t=4)
                b1s, ks = small[:, 76:76 + NSG * FB], small[:, 92:100]
                gates = [sbuf(c0, f"m_g{i}", [P, 4, NE], F32) for i in range(2)]
                v(vec.memset(rw[:, KB:2 * KB, NE:NE + 1], 0.0))
                for l in range(NLAY):
                    ld_r = [dma("act", "m_rw", rw[:, :, 0:NE], m_rw[l].rearrange("(k p) e -> p k e", p=P)),
                            dma("act", "m_cw", rw[:, 0:KB, NE:NE + 1], m_cw[l].rearrange("(k p) e -> p k e", p=P), allow_slow_non_contiguous=True),
                            dma("act", "m_rb", rb[:, 0:NE], bass.AP(m_rb.tensor, m_rb.offset + l * NE, [[0, P], [1, NE]])),
                            dma("act", "m_cb", rb[:, NE:NE + 1], bass.AP(m_cb.tensor, m_cb.offset + l, [[0, P], [1, 1]]))]
                    ld_b1 = dma("act", "m_b1", b1[:], m_b1[l].rearrange("e (k p) -> p (e k)", p=P), allow_slow_non_contiguous=True)
                    ld_w = []
                    for k, (n_, e) in enumerate(order):
                        room_ = loaded_piece(k)
                        if n_ == "ww":
                            r3 = room_.rearrange("p (k f) -> p k f", k=KB)
                            ld_w.append([dma("sp", f"m_ww{2 * e + x_}", r3[:, :, x_ * H:(x_ + 1) * H],
                                             m_ww[l, 2 * e + x_].rearrange("(k p) h -> p k h", p=P)) for x_ in range(2)])
                        else:
                            w_, nb = (m_w1, KB) if n_ == "w1" else (m_w2, FB)
                            ld_w.append(dma("sp", f"m_{n_}{e}", room_.rearrange("p (k f) -> p k f", k=nb),
                                            w_[l, e].rearrange("(k p) f -> p k f", p=P)))
                    w_scale = {n_: wsc[:, t * NLAY + l:t * NLAY + l + 1] for t, n_ in enumerate(("w1", "w2", "ww"))}
                    w_inv = {n_: winv[:, t * NLAY + l:t * NLAY + l + 1] for t, n_ in enumerate(("w1", "w2", "ww"))}
                    t_pair = {}

                    def split_piece(k):
                        n_, e = order[k]
                        flat = wroom[:, k, :].bitcast(F16).rearrange("p (x f) -> p x f", x=2)
                        need("act", ld_w[k], t_pair.get(order[k - 1]) if k else None)
                        t0 = S(act.activation(flat[:, 0, :], loaded_piece(k), ACT.Copy, scale=w_scale[n_]))
                        need("dve", ld_w[k], t0)
                        t_pair[(n_, e)] = V(vec.scalar_tensor_tensor(flat[:, 1, :], loaded_piece(k), w_scale[n_], flat[:, 0, :],
                                                                     ALU.mult, ALU.subtract))

                    ld_bb = [dma("act", "m_wb", bcast[:, 0:NWK * H], bass.AP(m_wb.tensor, m_wb.offset + l * NWK * H, [[0, P], [1, NWK * H]])),
                             dma("act", "m_b2", bcast[:, NWK * H:NE * H], bass.AP(m_b2.tensor, m_b2.offset + l * NSG * H, [[0, P], [1, NSG * H]]))]
                    if l == 0:
                        v(vec.tensor_reduce(sc[:, 0:1], h2[:], axis=AX.XY, op=ALU.max, apply_absolute_value=True))
                    else:
                        v(vec.tensor_reduce(sc[:, 0:1], hmax[:], axis=AX.X, op=ALU.max))
                    need("pe", now("dve"), bank_free[6], bank_free[7])
                    t0 = T(pe.transpose(bank[6][0:1, 0:P], sc[:, 0:1], ident[:]))
                    need("dve", t0)
                    t0 = v(vec.tensor_reduce(sc[0:1, 1:2], bank[6][0:1, 0:P], axis=AX.X, op=ALU.max))
                    need("pe", t0)
                    t0 = T(pe.matmul(bank[7][:, 0:1], ones_f[0:1, :], sc[0:1, 1:2], start=True, stop=True))
                    need("dve", t0)
                    v(vec.tensor_copy(sc[:, 0:1], bank[7][:, 0:1]))
                    power_scale(sc[:, 0:1], sc[:, 1:2], sc[:, 2:3], sc[:, 3:4])
                    v(vec.tensor_scalar(sc[:, 3:4], sc[:, 2:3], 1.0 / count_scale(), None, ALU.mult))
                    bank_free[6] = bank_free[7] = now("dve")
                    need("act", now("dve"))
                    t_h = []
                    if not fast:
                        t_h = [v(vec.tensor_scalar(h16, h2[:], sc[:, 1:2], None, ALU.mult))]
                    for i0 in range(0, NT, 5) if fast else ():
                        hs = h2[:, i0:i0 + 5, :]
                        t0 = S(act.activation(h16[:, 0, i0:i0 + 5, :], hs, ACT.Copy, scale=sc[:, 1:2]))
                        need("dve", t0)
                        t_h.append(V(vec.scalar_tensor_tensor(h16[:, 1, i0:i0 + 5, :], hs, sc[:, 1:2],
                                                              h16[:, 0, i0:i0 + 5, :], ALU.mult, ALU.subtract)))
                    need("dve", ld_b1)
                    v(vec.tensor_scalar(ks[:, 0:1], sc[:, 0:1], float(H), wmax[:, l:l + 1], ALU.mult, ALU.mult))
                    v(vec.tensor_tensor(ks[:, 0:1], ks[:, 0:1], wmax[:, 3 * NLAY + l:3 * NLAY + l + 1], ALU.add))
                    power_scale(ks[:, 0:1], ks[:, 1:2], ks[:, 2:3], ks[:, 3:4])
                    k_hidden, k_strong, k_weak = (ks[:, i:i + 1] for i in (4, 5, 6))
                    v(vec.tensor_scalar(k_hidden, ks[:, 1:2], sc[:, 2:3], w_inv["w1"], ALU.mult, ALU.mult))
                    v(vec.tensor_tensor(k_strong, ks[:, 2:3], w_inv["w2"], ALU.mult))
                    v(vec.tensor_tensor(k_weak, sc[:, 2:3], w_inv["ww"], ALU.mult))
                    t_ks = v(vec.tensor_scalar(b1s[:], b1[:], ks[:, 1:2], None, ALU.mult))
                    use = {}
                    t_route = {}
                    t_agg = {}

                    def edges(ci, blocks=range(KB), tiles=range(NT)):
                        c_, cw = CH[ci]
                        for kb in blocks:
                            if not fast:
                                if tiles[-1] == NT - 1:
                                    t_agg[(ci, kb)] = load_sums(kb, block_sums[kb], 0, CH[ci])
                                continue
                            need("pe", bank_free[kb])
                            for i in tiles:
                                need("pe", t_h[i // 5])
                                for part in range(2):
                                    m = pe.matmul(bank[kb][:, 0:cw], h16[:, part, i, kb * P:(kb + 1) * P],
                                                  A[:, i, c_:c_ + cw], start=(i == 0 and part == 0),
                                                  stop=(i == NT - 1 and part == 1))
                            t_agg[(ci, kb)] = T(m)

                    def turn(ci):
                        c_, cw = CH[ci]
                        ts = tiles_of(CH[ci])
                        for kb in range(KB):
                            b_ = 2 + kb
                            need("pe", bank_free[b_])
                            for i, k in ts:
                                m = pe.transpose(bank[b_][:, k * P:(k + 1) * P], h2[:, i, kb * P:(kb + 1) * P], ident[:])
                            need("act", T(m), use.get("hT"))
                            wd_ = len(ts) * P
                            bank_free[b_] = use["t_hT"] = S(act.activation(hT[:, kb, 0:wd_], bank[b_][:, 0:wd_], ACT.Copy))
                        need("sp", use.get("invd"))
                        use["t_invd"] = dma("sp", "invd", invd[:, 0:cw], bass.AP(invd_row.tensor, c_, [[0, P], [1, cw]]))

                    def mean(ci):
                        c_, cw = CH[ci]
                        need("dve", use["t_invd"], use.get("agg"), use.get("agg16"))
                        for kb in range(KB):
                            need("dve", t_agg[(ci, kb)])
                            bank_free[kb] = use["invd"] = v(vec.scalar_tensor_tensor(
                                agg[:, kb, 0:cw], bank[kb][:, 0:cw], sc[:, 3:4], invd[:, 0:cw], ALU.mult, ALU.mult))
                        need("act", now("dve"), use.get("agg16"))
                        t0 = S(act.activation(agg16[:, 0, :, 0:cw], agg[:, :, 0:cw], ACT.Copy, scale=sc[:, 1:2]))
                        need("dve", t0)
                        use["t_agg16"] = v(vec.scalar_tensor_tensor(agg16[:, 1, :, 0:cw], agg[:, :, 0:cw], sc[:, 1:2],
                                                                    agg16[:, 0, :, 0:cw], ALU.mult, ALU.subtract))

                    def route(ci):
                        ts = tiles_of(CH[ci])
                        need("pe", use["invd"], use["t_hT"], bank_free[2], *ld_r)
                        for i, k in ts:
                            r_ = rows_of(i)
                            for kk in range(2 * KB):
                                lhs = (hT if kk < KB else agg)[:, kk % KB, k * P:k * P + r_]
                                m = pe.matmul(bank[2][0:r_, k * (NE + 1):(k + 1) * (NE + 1)], lhs, rw[:, kk, :],
                                              start=(kk == 0), stop=(kk == 2 * KB - 1))
                        use["agg"] = use["hT"] = t0 = T(m)
                        R_, _, n_ = chunk_rows(CH[ci])
                        need("dve", t0, *ld_r)
                        need("dve", t_prio)
                        lg_ = lg[0:R_, 0:n_, :]
                        l_ = lg[0:R_, 0:n_, 0:NE]
                        v(vec.tensor_tensor(lg_, bank[2][0:R_, 0:n_ * (NE + 1)].rearrange("p (t e) -> p t e", e=NE + 1),
                                            rb[0:R_, None, :].to_broadcast([R_, n_, NE + 1]), ALU.add))
                        bank_free[2] = now("dve")
                        o1, o2, l2, e_ = (r[0:R_, 0:n_, :] for r in rt[0:4])
                        S1 = [sm[0:R_, i_, 0:n_] for i_ in range(10)]

                        def wide(a):
                            return a[:, :, None].to_broadcast([R_, n_, NE])

                        def pick(logits, top_, first, o):
                            v(vec.tensor_reduce(top_, logits, axis=AX.X, op=ALU.max))
                            v(vec.tensor_tensor(e_, logits, wide(top_), ALU.is_equal))
                            v(vec.tensor_tensor(e_, e_, prio[0:R_, None, :].to_broadcast([R_, n_, NE]), ALU.mult))
                            v(vec.tensor_reduce(first, e_, axis=AX.X, op=ALU.max))
                            v(vec.tensor_tensor(o, e_, wide(first), ALU.is_equal))

                        pick(l_, S1[0], S1[1], o1)
                        v(vec.scalar_tensor_tensor(l2, o1, -3e38, l_, ALU.mult, ALU.add))
                        pick(l2, S1[2], S1[3], o2)
                        v(vec.tensor_tensor(S1[4], S1[2], S1[0], ALU.subtract))
                        v(vec.tensor_scalar(S1[5], lg[0:R_, 0:n_, NE], -1.0, 80.0, ALU.mult, ALU.min))
                        need("act", now("dve"))
                        t0 = S(act.activation(sm[0:R_, 6:8, 0:n_], sm[0:R_, 4:6, 0:n_], ACT.Exp))
                        need("dve", t0)
                        v(vec.tensor_scalar(sm[0:R_, 8:10, 0:n_], sm[0:R_, 6:8, 0:n_], 1.0, None, ALU.add))
                        v(vec.reciprocal(sm[0:R_, 8:10, 0:n_], sm[0:R_, 8:10, 0:n_]))
                        v(vec.tensor_tensor(S1[8], S1[8], S1[9], ALU.mult))
                        v(vec.tensor_tensor(S1[6], S1[6], S1[8], ALU.mult))
                        g_ = gates[ci % 2][0:R_, 0:n_, :]
                        need("dve", use.get(("g", ci % 2)))
                        v(vec.tensor_tensor(o1, o1, wide(S1[8]), ALU.mult))
                        v(vec.tensor_tensor(o2, o2, wide(S1[6]), ALU.mult))
                        t_route[ci] = v(vec.tensor_tensor(g_, o1, o2, ALU.add))

                    n_sh = [0]
                    blk = {}

                    PARTS = ((0, 0), (0, 1), (1, 0))

                    def hidden(ci, e, blocks):
                        c_, cw = CH[ci]
                        w_ = pair_of(piece_no[("w1", e)], KB)
                        need("pe", t_pair[("w1", e)], use["t_agg16"])
                        need("act", t_ks, use["agg"])
                        for f in blocks:
                            b_ = 4 + n_sh[0] % 2
                            s_i = n_sh[0] % NSH
                            wide32 = agg[:, n_sh[0] % 2, 0:cw]
                            n_sh[0] += 1
                            need("pe", bank_free[b_])
                            todo = [(kb, pa) for kb in range(KB) for pa in PARTS]
                            for x_, (kb, (i, j)) in enumerate(todo):
                                m = pe.matmul(bank[b_][:, 0:cw], w_[:, i, kb, f * P:(f + 1) * P], agg16[:, j, kb, 0:cw],
                                              start=(x_ == 0), stop=(x_ == len(todo) - 1))
                            t0 = use["agg16"] = T(m)
                            need("act", t0, use.get(("wide32", n_sh[0] % 2)))
                            bank_free[b_] = t0 = S(act.activation(wide32, bank[b_][:, 0:cw], ACT.Relu,
                                                                  bias=b1s[:, e * FB + f:e * FB + f + 1], scale=k_hidden))
                            need("dve", t0, use.get(("sh", s_i)))
                            v(vec.tensor_copy(sh[s_i][:, 0:cw], wide32))
                            use[("wide32", n_sh[0] % 2)] = t0 = v(vec.tensor_tensor(sh[s_i][:, BANK:BANK + cw], wide32,
                                                                                    sh[s_i][:, 0:cw], ALU.subtract))
                            blk[(e, f)] = (s_i, t0)

                    def strong(ci, e):
                        w_ = pair_of(piece_no[("w2", e)], FB)
                        need("pe", t_pair[("w2", e)])
                        need("dve", *ld_bb)
                        need("dve", t_route[ci])
                        for i, k in tiles_of(CH[ci]):
                            r_ = rows_of(i)
                            b_ = 6 + k % 2
                            need("pe", bank_free[b_])
                            for f in range(FB):
                                s_i, t0 = blk[(e, f)]
                                need("pe", t0)
                                for pa in PARTS:
                                    m = pe.matmul(bank[b_][0:r_, 0:H], sh[s_i][:, pa[0] * BANK + k * P:pa[0] * BANK + k * P + r_],
                                                  w_[:, pa[1], f, :], start=(f == 0 and pa == PARTS[0]),
                                                  stop=(f == FB - 1 and pa == PARTS[-1]))
                            t0 = T(m)
                            for f in range(FB):
                                use[("sh", blk[(e, f)][0])] = t0
                            q = k % 2
                            ge = NWK + e
                            need("dve", t0)
                            bank_free[b_] = v(vec.scalar_tensor_tensor(tmp[q][0:r_, :], bank[b_][0:r_, 0:H], k_strong[0:r_],
                                                                       bcast[0:r_, ge * H:(ge + 1) * H], ALU.mult, ALU.add))
                            use[("g", ci % 2)] = v(vec.scalar_tensor_tensor(
                                h2[0:r_, i, :], tmp[q][0:r_, :], gates[ci % 2][0:r_, k, ge:ge + 1], h2[0:r_, i, :],
                                ALU.mult, ALU.add))

                    def weak(ci, tiles):
                        need("dve", *ld_bb)
                        need("dve", t_route[ci])
                        for i, k in tiles:
                            r_ = rows_of(i)
                            for pr in range(NWK * H // BANK):
                                w_ = pair_of(piece_no[("ww", pr)], KB)
                                need("pe", t_pair[("ww", pr)])
                                b_ = 2 + pr % 2
                                need("pe", bank_free[b_])
                                todo = [(kb, pa) for kb in range(KB) for pa in PARTS]
                                for y_, (kb, pa) in enumerate(todo):
                                    m = pe.matmul(bank[b_][0:r_, :], agg16[:, pa[0], kb, k * P:k * P + r_], w_[:, pa[1], kb, :],
                                                  start=(y_ == 0), stop=(y_ == len(todo) - 1))
                                use["agg16"] = t0 = T(m)
                                need("dve", t0, use["hT"])
                                room_ = hT[0:r_, pr, :]
                                bank_free[b_] = t0 = v(vec.scalar_tensor_tensor(
                                    room_, bank[b_][0:r_, :], k_weak[0:r_], bcast[0:r_, pr * BANK:(pr + 1) * BANK],
                                    ALU.mult, ALU.add))
                                need("act", t0)
                                for x_ in range(BANK // H):
                                    o_ = room_[:, x_ * H:(x_ + 1) * H]
                                    e = pr * (BANK // H) + x_
                                    t_gated = S(act.activation(o_, o_, ACT.Relu, scale=gates[ci % 2][0:r_, k, e:e + 1]))
                            need("dve", t_gated)
                            for e in range(NWK):
                                o_ = hT[0:r_, e * H // BANK, e * H % BANK:e * H % BANK + H]
                                use["hT"] = use[("g", ci % 2)] = v(vec.tensor_tensor(h2[0:r_, i, :], h2[0:r_, i, :], o_, ALU.add))

                    block_sums = [sums, degs8]
                    if not fast:
                        for kb in range(KB):
                            scatter_sum(h16[:, :, kb * P:(kb + 1) * P], block_sums[kb], [("src", "to_dst")])
                    for k in range(4):
                        split_piece(k)
                    edges(0)
                    turn(0)
                    mean(0)
                    half = FB // 2
                    cuts = [range(0, 5), range(5, 10), range(10, 15), range(15, NT)]
                    for ci in range(len(CH)):
                        more = ci + 1 < len(CH)
                        ts = tiles_of(CH[ci])
                        route(ci)
                        hidden(ci, 0, range(FB))
                        if ci == 0:
                            for k in range(4, NPC):
                                split_piece(k)
                            use[("sh", NSH - 2)] = use[("sh", NSH - 1)] = t_pair[order[-1]]
                        if more:
                            edges(ci + 1, range(KB - 1))
                        weak(ci, ts[0:1])
                        for e in range(1, NSG):
                            hidden(ci, e, range(half))
                            if more:
                                edges(ci + 1, [KB - 1], cuts[e - 1])
                            strong(ci, e - 1)
                            weak(ci, ts[e:e + 1])
                            hidden(ci, e, range(half, FB))
                        if more:
                            edges(ci + 1, [KB - 1], cuts[-1])
                            turn(ci + 1)
                            mean(ci + 1)
                        strong(ci, NSG - 1)
                        i0, n_ = tiles_of(CH[ci])[0][0], len(tiles_of(CH[ci]))
                        v(vec.tensor_reduce(hmax[:, ci:ci + 1], h2[:, i0:i0 + n_, :], axis=AX.XY, op=ALU.max,
                                            apply_absolute_value=True))
                    barrier()
                barrier()
            with scope() as c0:
                xr = xn
                t_x = dma("sp", "unpark", xr[:].rearrange("p i f -> p (i f)"), xpark)
                need("dve", t_x, *t_wo)
                need("pe", *t_wo)
                out_full, out_tail = node_rows(out)
                t_o = []
                hf = {}
                for ci in range(len(CH)):
                    ts = tiles_of(CH[ci])
                    for kb in range(KB):
                        b_ = 2 + kb
                        need("pe", bank_free[b_])
                        for i, k in ts:
                            m = pe.transpose(bank[b_][:, k * P:(k + 1) * P], h2[:, i, kb * P:(kb + 1) * P], ident[:])
                        wd_ = len(ts) * P
                        need("act", T(m), hf.get("hT"))
                        bank_free[b_] = t0 = S(act.activation(hT[:, kb, 0:wd_], bank[b_][:, 0:wd_], ACT.Copy))
                    need("pe", t0)
                    for i, k in ts:
                        r_ = rows_of(i)
                        b_ = (0, 1, 4, 5, 6, 7)[i % 6]
                        need("pe", bank_free[b_])
                        for kb in range(KB):
                            m = pe.matmul(bank[b_][0:r_, 0:D], hT[:, kb, k * P:k * P + r_], wout[:, kb, :],
                                          start=(kb == 0), stop=(kb == KB - 1))
                        hf["hT"] = t0 = T(m)
                        need("dve", t0)
                        bank_free[b_] = v(vec.tensor_tensor(xr[0:r_, i, :], xr[0:r_, i, :], bank[b_][0:r_, 0:D], ALU.add))
                        t0 = v(vec.tensor_tensor(xr[0:r_, i, :], xr[0:r_, i, :], bout[0:r_, :], ALU.add))
                    need("sp", t0)
                    i0, n_ = ts[0][0], len(ts)
                    if i0 == NT - 1:
                        t_o.append(dma("sp", f"out{ci}", out_tail, xr[0:TAIL, i0, :]))
                    else:
                        t_o.append(dma("sp", f"out{ci}", out_full[:, i0:i0 + n_, :], xr[:, i0:i0 + n_, :]))
                need("sp", *t_o)
                barrier()

    def network():
        with scope() as c:
            if not fast:
                with scope() as c0:
                    make_lists(c0)
                chunk_buf["buf"] = room[:, 0:4 * D].rearrange("p (i f) -> p i f", f=D)
            degrees()
            with scope() as c0:
                aside["steps"] = symmetric_steps(c0) if fast else iter(())
                step(aside["steps"])
                block_gru()
                block_gcn()
                for _ in aside["steps"]:
                    pass
                barrier()
            weight_max["part"] = sbuf(c, "w_part", [P, 4, m_w1.shape[0], 2], F32)
            block_relations()
            block_experts()

    room = A[:].rearrange("p i c -> p (i c)").bitcast(F32)
    for k in engines:
        seen[k] = {}
    ok = nc.values_load(flag[0:1, 0:1], min_val=0, max_val=1)
    at_branch = dict(count)
    slots_at_branch = {n_: s[1] for n_, s in slots.items()}
    with nc.If(ok == 1):
        network()
    with nc.Else():
        count.update(at_branch)
        for n_, s in slots.items():
            s[1] = slots_at_branch.get(n_, 0)
        for k in engines:
            seen[k] = {}
        bank_free[:] = [None] * 8
        sym_written.clear()
        fast = False
        network()
    top.close()


_INS = ["x", "src", "dst", "edge_type_8", "L0_gnn_weight", "L0_gnn_w_ih", "L0_gnn_w_hh", "L0_gnn_b_ih",
        "L0_gnn_b_hh", "L1_gnn_W0", "L1_gnn_b0", "L1_gnn_W1", "L1_gnn_b1", "L2_gnn_weight", "L2_gnn_self_weight",
        "L3_gnn_W_in", "L3_gnn_b_in", "L3_gnn_router_W", "L3_gnn_router_b", "L3_gnn_weak_W", "L3_gnn_weak_b",
        "L3_gnn_strong_W1", "L3_gnn_strong_b1", "L3_gnn_strong_W2", "L3_gnn_strong_b2", "L3_gnn_conf_W",
        "L3_gnn_conf_b", "L3_gnn_W_out", "L3_gnn_b_out"]


def kernel(**inputs):
    import concourse.bacc as bacc
    from concourse.bass_utils import run_bass_kernel_spmd

    nc = bacc.Bacc("TRN2", target_bir_lowering=False, num_devices=1)
    arrays, args = {}, []
    for name in _INS:
        a = np.ascontiguousarray(inputs[name])
        arrays["in_" + name] = a
        args.append(nc.dram_tensor("in_" + name, a.shape, dt.from_np(a.dtype), kind="ExternalInput").ap())
    out = nc.dram_tensor("out", arrays["in_x"].shape, F32, kind="ExternalOutput").ap()
    build_program(nc, *args, out)
    r = run_bass_kernel_spmd(nc, [arrays], core_ids=[0])
    return r.results[0]["out"]
```
